# Optimizing a Trainium2 kernel written in Bass

```python
import numpy as np
import jax
import jax.numpy as jnp

def _softmax(x, axis=-1):
    return jax.nn.softmax(x, axis=axis)

def _gelu(x):
    return jax.nn.gelu(x, approximate=True)

def _silu(x):
    return jax.nn.silu(x)

def _sigmoid(x):
    return jax.nn.sigmoid(x)

def _layernorm(x, axis=-1, eps=1e-05):
    m = jnp.mean(x, axis=axis, keepdims=True)
    v = jnp.var(x, axis=axis, keepdims=True)
    return (x - m) / jnp.sqrt(v + eps)

def _scatter_add(tgt, idx, src, axis=0):
    return tgt.at[idx].add(src)

def _segment_sum(src, seg, n):
    return jax.ops.segment_sum(src, seg, n)
kernel_name = 'mk_adj_ffn_d2_adj_r2_130863'

def setup_inputs(seed: int=0):
    np.random.seed(seed)
    _w = jnp.asarray

    def _rec_inputs():
        import jax
        import jax.numpy as jnp
        _gk = jax.random.key(seed)
        x = -0.0005207 + 1.001 * jax.random.normal(jax.random.fold_in(_gk, 1), (128, 128, 128), jnp.float32)
        _a = jax.random.bernoulli(jax.random.fold_in(_gk, 2), 0.125, (128, 128, 128))
        _a = jnp.logical_or(_a, jnp.swapaxes(_a, -1, -2))
        _a = jnp.logical_or(_a, jnp.eye(128, dtype=bool))
        _af = _a.astype(jnp.float32)
        _af = _af * jax.random.uniform(jax.random.fold_in(_gk, 3), (128, 128, 128), jnp.float32, 0.05, 1)
        adj = _af
        return (x, adj)
    x, adj = _rec_inputs()

    def _L0_gnn_setup():
        import jax, jax.numpy as jnp
        import numpy as np
        B, N, D = (2, 2048, 128)
        key = jax.random.key(seed)
        ks = jax.random.split(key, 6)
        return {'hidden': jax.random.normal(ks[0], (B, N, D), dtype=jnp.float32), 'mask': jax.random.uniform(ks[1], (B, N, N), dtype=jnp.float32), 'W_w': jax.random.normal(ks[2], (D, D), dtype=jnp.float32) * 0.05, 'W_b': jax.random.normal(ks[3], (D,), dtype=jnp.float32) * 0.05, 'a_w': jax.random.normal(ks[4], (2 * D,), dtype=jnp.float32) * 0.05, 'a_b': jax.random.normal(ks[5], (1,), dtype=jnp.float32) * 0.05}
    _L0_gnn_all = _L0_gnn_setup()
    _L0_gnn_in = {k: v for k, v in _L0_gnn_all.items() if k in ('W_w', 'W_b', 'a_w', 'a_b')}
    del _L0_gnn_all

    def _L0_ffn_setup():
        import jax, jax.numpy as jnp
        import numpy as np
        C = 128
        EPS = 1e-05
        N_ITERS = 30

        def _layernorm(x, w, bias):
            mu = jnp.mean(x, axis=-1, keepdims=True)
            var = jnp.mean(jnp.square(x - mu), axis=-1, keepdims=True)
            return (x - mu) * jax.lax.rsqrt(var + EPS) * w + bias
        key = jax.random.key(seed)
        kx, kw, kb, klw, klb = jax.random.split(key, 5)
        x = jax.random.normal(kx, (8, 1024, C), dtype=jnp.float32)
        bound = 1.0 / np.sqrt(C)
        W = jax.random.uniform(kw, (C, C), minval=-bound, maxval=bound, dtype=jnp.float32)
        b = jax.random.uniform(kb, (C,), minval=-bound, maxval=bound, dtype=jnp.float32)
        ln_w = jnp.ones((C,), dtype=jnp.float32)
        ln_b = jnp.zeros((C,), dtype=jnp.float32)
        return {'x': x, 'ln_w': ln_w, 'ln_b': ln_b, 'W': W, 'b': b}
    _L0_ffn_all = _L0_ffn_setup()
    _L0_ffn_in = {k: v for k, v in _L0_ffn_all.items() if k in ('ln_w', 'ln_b', 'W', 'b')}
    del _L0_ffn_all

    def _L1_gnn_setup():
        import jax, jax.numpy as jnp
        import numpy as np
        key = jax.random.key(seed)
        k1, k2, k3 = jax.random.split(key, 3)
        b, n, d, f = (16, 1024, 128, 128)
        features = jax.random.normal(k1, (b, n, d), dtype=jnp.float32)
        A = jax.random.uniform(k2, (b, n, n), dtype=jnp.float32)
        A = A / jnp.sum(A, axis=-1, keepdims=True)
        weight = jax.random.normal(k3, (2 * d, f), dtype=jnp.float32) * (1.0 / np.sqrt(2 * d))
        bias = jnp.zeros((f,), dtype=jnp.float32)
        return {'features': features, 'A': A, 'weight': weight, 'bias': bias}
    _L1_gnn_all = _L1_gnn_setup()
    _L1_gnn_in = {k: v for k, v in _L1_gnn_all.items() if k in ('weight', 'bias')}
    del _L1_gnn_all

    def _L1_ffn_setup():
        import jax, jax.numpy as jnp
        import numpy as np
        TOP_K = 2
        LN_EPS = 1e-05
        key = jax.random.key(seed)
        ks = jax.random.split(key, 8)
        B, S, D, E, H = (16, 512, 128, 8, 512)
        x = jax.random.normal(ks[0], (B, S, D), dtype=jnp.float32)
        Wr = jax.random.normal(ks[1], (D, E), dtype=jnp.float32) * 0.1
        br = jnp.zeros((E,), dtype=jnp.float32)
        ln_g = jnp.ones((E, D), dtype=jnp.float32)
        ln_b = jnp.zeros((E, D), dtype=jnp.float32)
        W1 = jax.random.normal(ks[2], (E, D, H), dtype=jnp.float32) * (1.0 / np.sqrt(D))
        b1 = jnp.zeros((E, H), dtype=jnp.float32)
        W2 = jax.random.normal(ks[3], (E, H, D), dtype=jnp.float32) * (1.0 / np.sqrt(H))
        b2 = jnp.zeros((E, D), dtype=jnp.float32)
        return {'x': x, 'Wr': Wr, 'br': br, 'ln_g': ln_g, 'ln_b': ln_b, 'W1': W1, 'b1': b1, 'W2': W2, 'b2': b2}
    _L1_ffn_all = _L1_ffn_setup()
    _L1_ffn_in = {k: v for k, v in _L1_ffn_all.items() if k in ('Wr', 'br', 'ln_g', 'ln_b', 'W1', 'b1', 'W2', 'b2')}
    del _L1_ffn_all
    return {'x': x, 'adj': adj, 'L0_gnn_W_w': _L0_gnn_in['W_w'], 'L0_gnn_W_b': _L0_gnn_in['W_b'], 'L0_gnn_a_w': _L0_gnn_in['a_w'], 'L0_gnn_a_b': _L0_gnn_in['a_b'], 'L0_ffn_ln_w': _L0_ffn_in['ln_w'], 'L0_ffn_ln_b': _L0_ffn_in['ln_b'], 'L0_ffn_W': _L0_ffn_in['W'], 'L0_ffn_b': _L0_ffn_in['b'], 'L1_gnn_weight': _L1_gnn_in['weight'], 'L1_gnn_bias': _L1_gnn_in['bias'], 'L1_ffn_Wr': _L1_ffn_in['Wr'], 'L1_ffn_br': _L1_ffn_in['br'], 'L1_ffn_ln_g': _L1_ffn_in['ln_g'], 'L1_ffn_ln_b': _L1_ffn_in['ln_b'], 'L1_ffn_W1': _L1_ffn_in['W1'], 'L1_ffn_b1': _L1_ffn_in['b1'], 'L1_ffn_W2': _L1_ffn_in['W2'], 'L1_ffn_b2': _L1_ffn_in['b2']}

def reference(x, adj, L0_gnn_W_w, L0_gnn_W_b, L0_gnn_a_w, L0_gnn_a_b, L0_ffn_ln_w, L0_ffn_ln_b, L0_ffn_W, L0_ffn_b, L1_gnn_weight, L1_gnn_bias, L1_ffn_Wr, L1_ffn_br, L1_ffn_ln_g, L1_ffn_ln_b, L1_ffn_W1, L1_ffn_b1, L1_ffn_W2, L1_ffn_b2):
    import jax
    import jax.numpy as jnp

    def _L0_gnn_ref(hidden, mask, W_w, W_b, a_w, a_b):
        import jax, jax.numpy as jnp
        import numpy as np
        B, N, D = (2, 2048, 128)
        h = jnp.einsum('bnd,ed->bne', hidden, W_w) + W_b
        Dh = h.shape[-1]
        a1, a2 = (a_w[:Dh], a_w[Dh:])
        e = h @ a1
        f = h @ a2
        logits = e[:, :, None] + f[:, None, :] + a_b[0]
        u = mask * jnp.exp(logits)
        a = u / jnp.sum(u, axis=2, keepdims=True)
        h_prime = jnp.einsum('bnm,bmd->bnd', a, h)
        return h_prime

    def _L0_ffn_ref(x, ln_w, ln_b, W, b):
        import jax, jax.numpy as jnp
        import numpy as np
        C = 128
        EPS = 1e-05
        N_ITERS = 30

        def _layernorm(x, w, bias):
            mu = jnp.mean(x, axis=-1, keepdims=True)
            var = jnp.mean(jnp.square(x - mu), axis=-1, keepdims=True)
            return (x - mu) * jax.lax.rsqrt(var + EPS) * w + bias

        def step(h, _):
            h = h + 0.01 * jnp.tanh(h)
            h = h * jax.nn.sigmoid(h)
            h = _layernorm(h, ln_w, ln_b)
            h = jnp.einsum('bsc,dc->bsd', h, W) + b
            return (h, None)
        x, _ = jax.lax.scan(step, x, None, length=N_ITERS)
        return x

    def _L1_gnn_ref(features, A, weight, bias):
        import jax, jax.numpy as jnp
        import numpy as np
        agg = jnp.einsum('bnm,bmd->bnd', A, features)
        d = features.shape[-1]
        out = jnp.einsum('bnd,df->bnf', features, weight[:d]) + jnp.einsum('bnd,df->bnf', agg, weight[d:]) + bias
        return jax.nn.relu(out)

    def _L1_ffn_ref(x, Wr, br, ln_g, ln_b, W1, b1, W2, b2):
        import jax, jax.numpy as jnp
        import numpy as np
        TOP_K = 2
        LN_EPS = 1e-05
        B, S, D = x.shape
        N = B * S
        xt = x.reshape(N, D)
        logits = xt @ Wr + br
        probs = jax.nn.softmax(logits, axis=-1)
        top_p, top_idx = jax.lax.top_k(probs, TOP_K)
        weights = top_p / top_p.sum(axis=-1, keepdims=True)
        mu = xt.mean(axis=-1, keepdims=True)
        var = ((xt - mu) ** 2).mean(axis=-1, keepdims=True)
        xn = (xt - mu) * jax.lax.rsqrt(var + LN_EPS)
        xe = xn[None, :, :] * ln_g[:, None, :] + ln_b[:, None, :]
        h = jax.nn.gelu(jnp.einsum('end,edh->enh', xe, W1) + b1[:, None, :], approximate=False)
        y = jnp.einsum('enh,ehd->end', h, W2) + b2[:, None, :]
        y_tok = jnp.transpose(y, (1, 0, 2))
        sel = jnp.take_along_axis(y_tok, top_idx[:, :, None], axis=1)
        out = (weights[:, :, None] * sel).sum(axis=1)
        return out.reshape(B, S, D)
    x = x + _L0_gnn_ref(_layernorm(x, axis=-1), adj, L0_gnn_W_w, L0_gnn_W_b, L0_gnn_a_w, L0_gnn_a_b)
    x = x + _L0_ffn_ref(_layernorm(x, axis=-1), L0_ffn_ln_w, L0_ffn_ln_b, L0_ffn_W, L0_ffn_b)
    x = x + _L1_gnn_ref(_layernorm(x, axis=-1), adj, L1_gnn_weight, L1_gnn_bias)
    x = x + _L1_ffn_ref(_layernorm(x, axis=-1), L1_ffn_Wr, L1_ffn_br, L1_ffn_ln_g, L1_ffn_ln_b, L1_ffn_W1, L1_ffn_b1, L1_ffn_W2, L1_ffn_b2)
    return x

_drawn_inputs = setup_inputs


def setup_inputs(seed=0):
    import zlib

    import numpy as np

    out = dict(_drawn_inputs(seed))
    spreads = {'L0_ffn_ln_w': (1.0, 0.2),
     'L0_ffn_ln_b': (0.0, 0.1),
     'L1_gnn_bias': (0.0, 0.318),
     'L1_ffn_br': (0.0, 0.283),
     'L1_ffn_ln_g': (1.0, 0.2),
     'L1_ffn_ln_b': (0.0, 0.493),
     'L1_ffn_b1': (0.0, 0.488),
     'L1_ffn_b2': (0.0, 0.334)}
    factors = {}
    for name, (base, spread) in spreads.items():
        noise = np.random.default_rng([zlib.crc32(name.encode()), seed]).standard_normal(out[name].shape)
        drawn = base * np.exp(spread * noise) if base else spread * noise
        out[name] = jnp.asarray(drawn.astype(out[name].dtype))
    for name, factor in factors.items():
        out[name] = (out[name] * factor).astype(out[name].dtype)
    return out
```

```python
from contextlib import ExitStack

import concourse.bass as bass
from concourse import mybir

F32 = mybir.dt.float32
BF16 = mybir.dt.bfloat16
I32 = mybir.dt.int32
U32 = mybir.dt.uint32
ALU = mybir.AluOpType
ACT = mybir.ActivationFunctionType
AX = mybir.AxisListType

P = 128
EPS = 1e-5


def network(nc, x, adj, W_w, W_b, a_w, a_b, ln_w, ln_b, F_W, F_b, G_w, G_b,
            R_w, R_b, E_g, E_b, E_W1, E_b1, E_W2, E_b2, out):
    B, N, D = x.shape
    assert N == P and D == P
    TILES = 8
    STREAMS = 8
    BANKS = 4
    ITERS = 30
    COLS = TILES * D
    GROUPS = B // (TILES * STREAMS)
    STEPS = STREAMS * ITERS
    NE = R_w.shape[1]
    H = E_W1.shape[2]
    HC = H // P
    TOKENS = B * N
    SLAB = 512
    SUBS = SLAB // P
    ROW = D + 4
    REGION = TOKENS + SLAB
    SLABS = (2 * TOKENS + NE * (SLAB - 1)) // SLAB
    SLABS += -SLABS % 4
    FAR = 1 << 20
    BATCHES = TILES * STREAMS

    with ExitStack() as ctx:
        def sb(name, shape, dt=F32):
            return ctx.enter_context(nc.sbuf_tensor(name, shape, dt))

        def sem(name):
            return ctx.enter_context(nc.semaphore(name))

        ps = [ctx.enter_context(nc.psum_tensor(f"ps{j}", [P, TILES, D], F32)) for j in range(BANKS)]

        resid = [sb(f"resid{s}", [P, TILES, D]) for s in range(STREAMS)]
        rows_b = [sb(f"adjT{s}", [P, TILES, ROW]) for s in range(STREAMS)]
        rows_a = [sb(f"start_h{s}", [P, TILES, ROW]) for s in range(STREAMS)]
        adjT = [t[:, :, 0:N] for t in rows_b]
        start_h = [t[:, :, 0:D] for t in rows_a]
        raw = [sb(f"raw{j}", [P, TILES, D]) for j in range(2)]
        work = [sb(f"work{j}", [P, TILES, D]) for j in range(4)]
        act_z = [sb(f"act_z{j}", [P, TILES, D]) for j in range(4)]
        scaled = [sb(f"scaled{j}", [P, TILES, D]) for j in range(4)]
        turned = [sb(f"turned{j}", [P, TILES, D]) for j in range(4)]
        stats = [sb(f"stats{j}", [P, TILES, 6]) for j in range(8)]
        small = [sb(f"small{j}", [P, 5, TILES]) for j in range(8)]
        var = [sb(f"var{j}", [P, TILES]) for j in range(8)]
        rstd = [sb(f"rstd{j}", [P, TILES]) for j in range(8)]
        neg_mean = [sb(f"neg_mean{j}", [P, TILES]) for j in range(4)]
        shift = [sb(f"shift{j}", [P, TILES]) for j in range(4)]
        soft_f = [sb(f"soft_f{j}", [P, TILES]) for j in range(4)]
        soft_e = [sb(f"soft_e{j}", [P, TILES]) for j in range(4)]
        soft = [sb(f"soft{j}", [P, 3, TILES]) for j in range(4)]
        eps_minus = sb("eps_minus", [P, TILES])
        eps_plus = sb("eps_plus", [P, TILES])
        minus_half = sb("minus_half", [P, TILES])
        tick = sb("tick", [P, 1])
        pool_buf = sb("pool_buf", [P, 1])
        act_tick = sb("act_tick", [P, 1])
        ident = sb("ident", [P, P])
        mean_mat = sb("mean_mat", [P, P])
        ones_bf = sb("ones_bf", [P, P], BF16)
        ones_f = sb("ones_f", [P, P])

        wr = sb("wr", [P, NE])
        br_b = sb("br_b", [P, NE])
        tri = sb("tri", [P, P], BF16)
        descend = sb("descend", [P, NE])
        region_0 = sb("region_0", [P, NE])
        ids = sb("ids", [P, 2, B], I32)
        extra = [sb(f"extra{j}", [P, 5, TILES]) for j in range(4)]
        logits = [sb(f"logits{j}", [P, TILES, NE]) for j in range(4)]
        probs = [sb(f"probs{j}", [P, TILES, NE]) for j in range(4)]
        edge = [sb(f"edge{j}", [P, 8, TILES]) for j in range(4)]
        cand = [sb(f"cand{j}", [P, TILES, NE]) for j in range(2)]
        hot = [sb(f"hot{j}", [P, 2, TILES, NE]) for j in range(4)]
        chosen = [sb(f"chosen{j}", [P, TILES, NE], BF16) for j in range(4)]
        rank = [sb(f"rank{j}", [P, 2, TILES]) for j in range(4)]
        slot = sb("slot", [P, STREAMS, 2, TILES], I32)
        taken = sb("taken", [P, NE])
        taken_new = sb("taken_new", [P, NE])
        taken_bf = sb("taken_bf", [P, NE], BF16)
        share = sb("share", [P, 2, B])
        slab_j = sb("slab_j", [P, SLABS])
        slab_rows = sb("slab_rows", [P, TOKENS // SLAB])
        count_f = sb("count_f", [P, NE])
        slabs_f = sb("slabs_f", [P, NE])
        slab_end = sb("slab_end", [P, NE])
        pad_f = sb("pad_f", [P, NE])
        slab_e = sb("slab_e", [P, SLABS])
        slab_0 = sb("slab_0", [P, SLABS])
        slab_row = sb("slab_row", [P, SLABS], I32)
        slab_exp = sb("slab_exp", [P, SLABS], I32)
        pad_row = sb("pad_row", [P, NE], I32)
        pad = sb("pad", [P, SUBS, ROW], I32)
        params_rows = sb("params_rows", [(2 + HC) * NE, P])
        params = sb("params", [P, NE, 2 + HC])
        params_in = [sb(f"params_in{j}", [P, 2 + HC]) for j in range(4)]

        def part(t, first, n):
            return t[:, :, :].rearrange("p t d -> p (t d)")[:, first:first + n]

        def by_tile(v, n):
            return v.rearrange("p (t d) -> p t d", t=n)

        below = [part(turned[j], 0, TOKENS // SLAB * NE) for j in range(1)][0].rearrange("p (e j) -> p e j", e=NE)
        past = part(turned[1], 0, SLABS * NE).rearrange("p (j e) -> p j e", e=NE)
        before = part(turned[2], 0, SLABS * NE).rearrange("p (j e) -> p j e", e=NE)
        rows_in = [by_tile(part(rows_a[q], 0, SUBS * ROW), SUBS) for q in range(4)]
        w1_in = [part(rows_a[q], SUBS * ROW, H) for q in range(4)]
        w2_in = [by_tile(part(rows_b[q], 0, HC * D), HC) for q in range(4)]
        b2_in = [part(rows_b[q], HC * D, D) for q in range(4)]
        y_out = [by_tile(part(rows_a[4 + q], 0, SLAB), SUBS) for q in range(4)]
        rows_T = [part(resid[4], SLAB * j, SLAB) for j in range(2)]
        hidden = [[part(resid[2 * j + c // 2], SLAB * (c % 2), SLAB) for c in range(HC)] for j in range(2)]
        psX = [part(ps[0], SLAB * j, SLAB) for j in range(2)]
        psH = [part(ps[1 + c // 2], SLAB * (c % 2), SLAB) for c in range(HC)]
        psY = [by_tile(part(ps[3], SLAB * j, SLAB), SUBS) for j in range(2)]

        x3_dram = nc.dram_tensor("x3_dram", (B, N, D), F32, kind="Internal").ap()
        sorted_rows = nc.dram_tensor("sorted_rows", (NE * REGION + SLAB, ROW), F32, kind="Internal").ap()
        params_dram = nc.dram_tensor("params_dram", (P, NE, 2 + HC), F32, kind="Internal").ap()
        y_dram = nc.dram_tensor("y_dram", (2 * TOKENS, D), F32, kind="Internal").ap()

        wl = sb("wl", [P, 4, P])
        lnw_b = sb("lnw_b", [P, P])
        cols_in = sb("cols_in", [P, 4])
        ab_b = sb("ab_b", [P, 1])
        bias_rows = sb("bias_rows", [P, 3, P])
        lnb_wide = sb("lnb_wide", [P, P])
        wb_wide = sb("wb_wide", [P, P])
        centred = sb("centred", [P, 2, P])
        sums = sb("sums", [P, 4])
        w_gnn0 = sb("w_gnn0", [P, P])
        w_ef = sb("w_ef", [P, 2])
        c_ef = sb("c_ef", [P, 2])
        w_ffn = sb("w_ffn", [P, P])
        w_ffn_plain = sb("w_ffn_plain", [P, P])
        w_mix = sb("w_mix", [P, 2, P])
        crow = sb("crow", [P, 3, P])
        cpart = sb("cpart", [P, 3, 3, P], BF16)
        bias_mv = [sb(f"bias_mv{j}", [P, 4, P], BF16) for j in range(3)]

        weights_in = sem("weights_in")
        consts_ready = sem("consts_ready")
        prep_v = sem("prep_v")
        prep_t = sem("prep_t")
        group_open = sem("group_open")
        x_in = [sem(f"x_in{s}") for s in range(STREAMS)]
        adj_in = [sem(f"adj_in{s}") for s in range(2)]
        out_done = [sem(f"out_done{s}") for s in range(STREAMS)]
        adj_psum = sem("adj_psum")
        adjT_ready = sem("adjT_ready")
        stat_step = [sem(f"stat_step{j}") for j in range(3)]
        stat_var = [sem(f"stat_var{j}") for j in range(3)]
        stat_pow = [sem(f"stat_pow{j}") for j in range(3)]
        mean_step = sem("mean_step")
        shift_ready = sem("shift_ready")
        pool_step = sem("pool_step")
        x_scaled = sem("x_scaled")
        x2_scaled = sem("x2_scaled")
        x_flip = sem("x_flip")
        x2_flip = sem("x2_flip")
        x_turned = sem("x_turned")
        x2_turned = sem("x2_turned")
        h_psum = sem("h_psum")
        ef_psum = sem("ef_psum")
        soft_e_ready = sem("soft_e_ready")
        den_psum = sem("den_psum")
        src_ready = sem("src_ready")
        soft_step = sem("soft_step")
        ratio_ready = sem("ratio_ready")
        num_psum = sem("num_psum")
        gnn0_rows = sem("gnn0_rows")
        x1_ready = sem("x1_ready")
        h0_ready = sem("h0_ready")
        x2_ready = sem("x2_ready")
        q_psum = sem("q_psum")
        q_copied = sem("q_copied")
        mix_psum = sem("mix_psum")
        x3_ready = sem("x3_ready")
        a_step = sem("a_step")
        b_step = sem("b_step")
        c_step = sem("c_step")
        r_stat = sem("r_stat")
        r_mean = sem("r_mean")
        r_var = sem("r_var")
        r_pow = sem("r_pow")
        r_small = sem("r_small")
        r_scales = sem("r_scales")
        rows_ready = sem("rows_ready")
        rows_copied = sem("rows_copied")
        ids_ready = sem("ids_ready")
        r_flip = sem("r_flip")
        r_turned = sem("r_turned")
        logit_psum = sem("logit_psum")
        centred_logits = sem("centred_logits")
        exps = sem("exps")
        chosen_ready = sem("chosen_ready")
        rank_psum = sem("rank_psum")
        slots_ready = sem("slots_ready")
        scattered = sem("scattered")
        total_psum = sem("total_psum")
        tables_ready = sem("tables_ready")
        pads_in = sem("pads_in")
        table_step = sem("table_step")
        params_ready = sem("params_ready")
        pool_tick = sem("pool_tick")
        params_stored = sem("params_stored")
        slab_in = [sem(f"slab_in{q}") for q in range(4)]
        slab_flip = sem("slab_flip")
        slab_turned = sem("slab_turned")
        hidden_psum = sem("hidden_psum")
        hidden_ready = sem("hidden_ready")
        y_psum = sem("y_psum")
        y_ready = sem("y_ready")
        y_stored = [sem(f"y_stored{q}") for q in range(4)]
        fin_in = [sem(f"fin_in{j}") for j in range(2)]
        fin_mid = sem("fin_mid")
        fin_ready = sem("fin_ready")
        fin_out = [sem(f"fin_out{j}") for j in range(2)]
        tanh_done = sem("tanh_done")
        state_read = sem("state_read")
        silu_done = sem("silu_done")
        it_step = sem("it_step")
        it_var = sem("it_var")
        it_pow = sem("it_pow")
        it_scaled = sem("it_scaled")
        it_scaled_v = sem("it_scaled_v")
        it_scaled_a = sem("it_scaled_a")
        it_flip = sem("it_flip")
        it_turned = sem("it_turned")
        product = sem("product")

        xv = x.rearrange("(g s t) n d -> g s n t d", g=GROUPS, s=STREAMS)
        av = adj.rearrange("(g s t) n d -> g s n t d", g=GROUPS, s=STREAMS)
        ov = out.rearrange("(g s t) n d -> g s n t d", g=GROUPS, s=STREAMS)
        x3v = x3_dram.rearrange("(g s t) n d -> g s n t d", g=GROUPS, s=STREAMS)
        yv = y_dram.rearrange("(i t n k) d -> i n t k d", i=GROUPS * STREAMS, t=TILES, k=2)
        A_STEPS, B_STEPS, C_STEPS, SMALL_STEPS = 3, 15, 3, 6
        SLAB_LOADS = 5

        prep_ready = [0]

        block = ctx.enter_context(nc.Block())

        def wide(v):
            return v.unsqueeze(2).to_broadcast([P, v.shape[1], D])

        loads = ((wl[:, 0, :], W_w), (wl[:, 1, :], F_W), (wl[:, 2, :], G_w[0:D, :]),
                 (wl[:, 3, :], G_w[D:2 * D, :]),
                 (lnw_b[:, :], ln_w.partition_broadcast(P)),
                 (cols_in[:, 0:1], a_w[0:D].rearrange("(p o) -> p o", o=1)),
                 (cols_in[:, 1:2], a_w[D:2 * D].rearrange("(p o) -> p o", o=1)),
                 (cols_in[:, 2:3], ln_b.rearrange("(p o) -> p o", o=1)),
                 (cols_in[:, 3:4], W_b.rearrange("(p o) -> p o", o=1)),
                 (ab_b[:, :], a_b.partition_broadcast(P)),
                 (bias_rows[:, 0, :], W_b.partition_broadcast(P)),
                 (bias_rows[:, 1, :], F_b.partition_broadcast(P)),
                 (bias_rows[:, 2, :], G_b.partition_broadcast(P)),
                 (params_rows[0:NE, :], E_g), (params_rows[NE:2 * NE, :], E_b),
                 (params_rows[2 * NE:(2 + HC) * NE, :], E_b1.rearrange("e (c p) -> (e c) p", p=P)),
                 (wr[:, :], R_w), (br_b[:, :], R_b.partition_broadcast(P)))

        SILU_LAG, STATS_LAG, SCALE_LAG, FLIP_LAG, EVAC_LAG = 1, 2, 4, 5, 6
        POOL_TILES, VECTOR_TILES = 6, 1

        ADJ_LAG, H_LAG, NUM_LAG, X1_LAG, X1_STATS_LAG, H0_LAG = 1, 2, 3, 4, 5, 6
        Q_LAG, MIX_LAG = 1, 2

        def in_flight(k, *lags):
            return [k - lag if 0 <= k - lag < STREAMS else None for lag in lags]

        def stages(lags, k, base, peeled, tail):
            for lag in lags:
                j = k - lag
                if tail and j >= 0 or peeled and j < 0:
                    yield None, None
                else:
                    yield base + j, j % STREAMS

        @block.sync
        def _(sp):
            for dst, src in loads:
                sp.dma_start(dst, src).then_inc(weights_in, 16)
            def load_x(g, s):
                sp.dma_start(resid[s][:, :, :], xv[g, s]).then_inc(x_in[s], 16)

            for g in range(GROUPS):
                for s in range(STREAMS):
                    if g or s >= 2:
                        sp.wait_ge(adj_psum, g * STREAMS + s - 1)
                    sp.dma_start(raw[s % 2][:, :, :], av[g, s]).then_inc(adj_in[s % 2], 16)
                    if g == 0:
                        load_x(g, s)
                if g == 0:
                    sp.wait_ge(params_ready, 1)
                    sp.dma_start(params_dram, params[:, :, :]).then_inc(params_stored, 16)
                for s in range(STREAMS + 1):
                    if s < STREAMS:
                        sp.wait_ge(x3_ready, g * STREAMS + s + 1)
                        sp.dma_start(x3v[g, s], resid[s][:, :, :]).then_inc(out_done[s], 16)
                    if s >= 1:
                        sp.wait_ge(out_done[s - 1], g * 16 + 16)
                        if g + 1 < GROUPS:
                            sp.wait_ge(rows_ready, g * STREAMS + s)
                            load_x(g + 1, s - 1)

            sp.wait_ge(tables_ready, 1)
            for e in range(NE + 1):
                if e < NE:
                    at = sp.value_load(pad_row[0:1, e:e + 1], min_val=e * REGION, max_val=e * REGION + TOKENS)
                    dst = sorted_rows[bass.ds(at, SLAB), :]
                else:
                    dst = sorted_rows[NE * REGION:NE * REGION + SLAB, :]
                sp.dma_start(dst.rearrange("(t p) d -> p t d", t=SUBS),
                             pad[:, :, :].bitcast(F32)).then_inc(pads_in, 16)
            sp.wait_ge(pads_in, 16 * (NE + 1))
            sp.wait_ge(scattered, 16 * 2 * B)
            sp.wait_ge(params_stored, 16)

            def load_slab(j, q, wait):
                at = sp.value_load(slab_row[0:1, bass.ds(j, 1)], min_val=0, max_val=NE * REGION)
                e = sp.value_load(slab_exp[0:1, bass.ds(j, 1)], min_val=0, max_val=NE - 1)
                wait()
                sp.dma_start(rows_in[q], sorted_rows[bass.ds(at, SLAB), :].rearrange("(t p) d -> p t d", p=P)
                             ).then_inc(slab_in[q], 16)
                sp.dma_start(w1_in[q], E_W1[bass.ds(e, 1)].rearrange("o p n -> p (o n)")).then_inc(slab_in[q], 16)
                sp.dma_start(w2_in[q], E_W2[bass.ds(e, 1)].rearrange("o (c p) d -> p (o c) d", p=P)
                             ).then_inc(slab_in[q], 16)
                sp.dma_start(b2_in[q], E_b2[bass.ds(e, 1)].rearrange("o d -> (o d)").partition_broadcast(P)
                             ).then_inc(slab_in[q], 16)
                sp.dma_start(params_in[q][:, :], params_dram[:, bass.ds(e, 1), :].rearrange("p o c -> p (o c)")
                             ).then_inc(slab_in[q], 16)

            for q in range(4):
                load_slab(q, q, lambda: None)
            for j in range(4, SLABS):
                def wait():
                    sp.wait_ge(y_stored[j % 4], 16 * SUBS * (j // 4))
                load_slab(j, j % 4, wait)

            for i in range(GROUPS * STREAMS + 1):
                if i < GROUPS * STREAMS:
                    b = i % 2
                    if i == 0:
                        for q in range(4):
                            sp.wait_ge(y_stored[q], 16 * SUBS * SLABS // 4)
                    if i >= 2:
                        sp.wait_ge(fin_out[b], 16 * (i // 2))
                    for k in range(2):
                        sp.dma_start(act_z[2 * b + k][:, :, :], yv[i][:, :, k, :]).then_inc(fin_in[b], 16)
                    sp.dma_start(scaled[b][:, :, :], x3v[i // STREAMS, i % STREAMS]).then_inc(fin_in[b], 16)
                if i >= 1:
                    sp.wait_ge(fin_ready, i)
                    sp.dma_start(ov[(i - 1) // STREAMS, (i - 1) % STREAMS],
                                 scaled[(i - 1) % 2][:, :, :]).then_inc(fin_out[(i - 1) % 2], 16)
            for q in range(2):
                sp.wait_ge(fin_out[q], 16 * GROUPS * STREAMS // 2)

        @block.gpsimd
        def _(pool):
            nc.gpsimd.memset(ident[:, :], 0.0).then_inc(pool_step, 1)
            nc.gpsimd.memset(minus_half[:, :], -0.5)
            for rows_to in (*rows_a, *rows_b):
                nc.gpsimd.memset(rows_to[:, :, D + 1:ROW], 0.0)
            nc.gpsimd.memset(pool_buf[:, :], 0.0).then_inc(pool_tick, 1)
            nc.gpsimd.memset(eps_minus[:, :], -EPS)
            nc.gpsimd.memset(eps_plus[:, :], 1.0 + EPS)
            nc.gpsimd.memset(mean_mat[:, :], 1.0 / D)
            nc.gpsimd.memset(ones_bf[:, :], 1.0)
            nc.gpsimd.memset(ones_f[:, :], 1.0)
            for dst, step, first in ((descend, -1, NE), (region_0, REGION, 0), (slab_j, 1, 0), (slab_rows, SLAB, 0)):
                nc.gpsimd.iota(dst[:, :], pattern=[[step, dst.shape[1]]], base=first, channel_multiplier=0,
                               allow_small_or_imprecise_dtypes=True)
            nc.gpsimd.iota(ids[:, :, :], pattern=[[1, 2], [2 * N, B]], base=0, channel_multiplier=2)
            nc.gpsimd.memset(pad[:, :, :], 0)
            nc.gpsimd.memset(tri[:, :], 0.0).then_inc(pool_step, 1)
            pool.wait_ge(pool_step, 2)
            nc.gpsimd.memset(pad[:, :, D:D + 1], FAR)
            nc.gpsimd.affine_select(out=tri[:, :], in_=tri[:, :], compare_op=ALU.is_ge, fill=1.0, base=0,
                                    pattern=[[-1, P]], channel_multiplier=1)
            nc.gpsimd.affine_select(out=ident[:, :], in_=ident[:, :], compare_op=ALU.not_equal, fill=1.0, base=0,
                                    pattern=[[-1, P]], channel_multiplier=1).then_inc(consts_ready, 1)

            def rstd_of(c, var_sem, n, pow_sem):
                pool.wait_ge(var_sem, n + 1)
                nc.gpsimd.tensor_tensor(rstd[c][:, :], var[c][:, :], minus_half[:, :], ALU.pow).then_inc(pow_sem, 1)
                pool.wait_ge(pow_sem, n + 1)

            def iteration(base, peeled):
                for k in range(STREAMS):
                    rstd_of(k % 4, it_var, base + k, it_pow)
                    if k >= 4 or not peeled:
                        pool.wait_ge(it_flip, base + (k - 3))
                    nc.gpsimd.tensor_tensor(scaled[k % 4][:, 0:POOL_TILES, :], act_z[k % 4][:, 0:POOL_TILES, :],
                                            wide(rstd[k % 4][:, 0:POOL_TILES]), ALU.mult).then_inc(it_scaled, 1)

            with pool.Fori(0, GROUPS) as g:
                pool.wait_ge(group_open, g + 1)
                for k in range(STREAMS + X1_STATS_LAG):
                    a, b, d = in_flight(k, X1_LAG, X1_STATS_LAG, 0)
                    if a is not None:
                        pool.wait_ge(gnn0_rows, g * STREAMS + a + 1)
                        nc.gpsimd.tensor_tensor(resid[a][:, :, :], resid[a][:, :, :], act_z[a % 4][:, :, :],
                                                ALU.add).then_inc(x1_ready, 1)
                    if d is not None:
                        rstd_of(4 + d % 4, stat_var[0], g * STREAMS + d, stat_pow[0])
                        if d >= 4:
                            pool.wait_ge(x_flip, g * STREAMS + d - 3)
                        nc.gpsimd.tensor_tensor(scaled[d % 4][:, :, :], resid[d][:, :, :], wide(rstd[4 + d % 4][:, :]),
                                                ALU.mult).then_inc(x_scaled, 1)
                    if b is not None:
                        if b >= 4:
                            pool.wait_ge(h0_ready, g * STREAMS + b - 3)
                        rstd_of(b % 4, stat_var[1], g * STREAMS + b, stat_pow[1])
                        nc.gpsimd.tensor_tensor(shift[b % 4][:, :], neg_mean[b % 4][:, :], rstd[b % 4][:, :],
                                                ALU.mult).then_inc(shift_ready, 1)
                pool.wait_ge(h0_ready, g * STREAMS + STREAMS)
                q0 = g * STEPS
                iteration(q0, True)
                with pool.Fori(q0 + STREAMS, q0 + STEPS, STREAMS) as q:
                    iteration(q, False)
                for s in range(STREAMS):
                    rstd_of(4 + s % 4, stat_var[2], g * STREAMS + s, stat_pow[2])
                    if s < 4:
                        pool.wait_ge(it_flip, g * STEPS + (STEPS - 3 + s))
                    else:
                        pool.wait_ge(x2_flip, g * STREAMS + s - 3)
                    nc.gpsimd.tensor_tensor(scaled[s % 4][:, :, :], resid[s][:, :, :], wide(rstd[4 + s % 4][:, :]),
                                            ALU.mult).then_inc(x2_scaled, 1)
                for s in range(STREAMS):
                    c, n = s % 4, g * STREAMS + s
                    ex = extra[c]
                    if s >= 4:
                        pool.wait_ge(a_step, (n - 4) * A_STEPS + 1)
                        pool.wait_ge(rows_ready, n - 3)
                    rstd_of(c, r_var, n, r_pow)

                    def small(i, ins):
                        ins.then_inc(r_small, 1)
                        pool.wait_ge(r_small, n * SMALL_STEPS + i)

                    small(1, nc.gpsimd.tensor_tensor(ex[:, 0, :], rstd[c][:, :], rstd[c][:, :], ALU.mult))
                    small(2, nc.gpsimd.tensor_tensor(ex[:, 0, :], ex[:, 0, :], eps_minus[:, :], ALU.mult))
                    small(3, nc.gpsimd.tensor_tensor(ex[:, 1, :], ex[:, 0, :], eps_plus[:, :], ALU.add))
                    small(4, nc.gpsimd.tensor_tensor(ex[:, 2, :], ex[:, 1, :], minus_half[:, :], ALU.pow))
                    nc.gpsimd.tensor_tensor(ex[:, 3, :], ex[:, 1, :], ex[:, 2, :], ALU.mult)
                    small(5, nc.gpsimd.tensor_tensor(ex[:, 4, :], rstd[c][:, :], ex[:, 2, :], ALU.mult))
                    nc.gpsimd.tensor_tensor(shift[c][:, :], neg_mean[c][:, :], ex[:, 4, :],
                                            ALU.mult).then_inc(r_small, 1)
                    for k, dst in enumerate((rows_a[s], rows_b[s])):
                        last = nc.gpsimd.tensor_copy(
                            dst[:, :, D:D + 1].bitcast(I32),
                            ids[:, k, bass.ds(g * BATCHES + s * TILES, TILES)].unsqueeze(2))
                    last.then_inc(ids_ready, 1)
                for s in range(STREAMS):
                    n = g * STREAMS + s
                    pool.wait_ge(pool_step, 1)
                    pool.wait_ge(slots_ready, n + 1)
                    pool.wait_ge(rows_copied, n + 1)
                    pool.wait_ge(ids_ready, n + 1)
                    for t in range(TILES):
                        for k, src in enumerate((rows_a[s], rows_b[s])):
                            nc.gpsimd.indirect_dma_start(
                                out=sorted_rows, in_=src[:, t, :], in_offset=None,
                                out_offset=bass.IndirectOffsetOnAxis(ap=slot[:, s, k, t:t + 1].bitcast(U32), axis=0),
                            ).then_inc(scattered, 16)

            with pool.Fori(0, SLABS, 4) as j:
                for q in range(4):
                    pool.wait_ge(y_ready, j + (q + 1))
                    pool.wait_ge(pool_tick, j + (q + 1))
                    nc.gpsimd.tensor_tensor(pool_buf[:, :], minus_half[:, 0:1], minus_half[:, 0:1],
                                            ALU.add).then_inc(pool_tick, 1)
                    for t in range(SUBS):
                        nc.gpsimd.indirect_dma_start(
                            out=y_dram, in_=y_out[q][:, t, :], in_offset=None,
                            out_offset=bass.IndirectOffsetOnAxis(ap=rows_in[q][:, t, D:D + 1].bitcast(U32), axis=0),
                            bounds_check=2 * TOKENS - 1, oob_is_err=False).then_inc(y_stored[q], 16)

        @block.vector
        def _(dve):
            chain = [0]

            def link(ins):
                chain[0] += 1
                ins.then_inc(prep_v, 1)
                dve.wait_ge(prep_v, chain[0])

            dve.wait_ge(weights_in, 16 * len(loads))
            dve.wait_ge(consts_ready, 1)
            nc.vector.tensor_scalar(wb_wide[:, :], ones_f[:, :], cols_in[:, 3:4], None, ALU.mult)
            nc.vector.tensor_scalar(lnb_wide[:, :], ones_f[:, :], cols_in[:, 2:3], None, ALU.mult)
            link(nc.vector.tensor_tensor(centred[:, 1, :], wl[:, 1, :], lnw_b[:, :], ALU.mult))
            nc.vector.tensor_reduce(sums[:, 0:1], wl[:, 0, :], AX.X, ALU.add)
            link(nc.vector.tensor_reduce(sums[:, 1:2], centred[:, 1, :], AX.X, ALU.add))
            link(nc.vector.tensor_scalar(sums[:, 2:4], sums[:, 0:2], -1.0 / D, None, ALU.mult))
            nc.vector.tensor_scalar(centred[:, 0, :], wl[:, 0, :], sums[:, 2:3], None, ALU.add)
            link(nc.vector.tensor_scalar(centred[:, 1, :], centred[:, 1, :], sums[:, 3:4], None, ALU.add))
            dve.wait_ge(prep_t, 1)
            nc.vector.tensor_copy(w_gnn0[:, :], ps[0][:, 0, :])
            nc.vector.tensor_copy(w_ffn[:, :], ps[0][:, 1, :])
            nc.vector.tensor_copy(w_ef[:, :], ps[1][:, 0, 0:2])
            nc.vector.tensor_copy(params[:, :, 0], ps[1][:, 4, 0:NE])
            nc.vector.tensor_copy(params[:, :, 1], ps[1][:, 4, NE:2 * NE])
            nc.vector.tensor_copy(params[:, :, 2:2 + HC], ps[1][:, 4, 2 * NE:(2 + HC) * NE].rearrange(
                "p (e c) -> p e c", c=HC)).then_inc(params_ready, 1)
            nc.vector.tensor_copy(c_ef[:, 1:2], ps[1][:, 0, 9:10])
            nc.vector.tensor_tensor(c_ef[:, 0:1], ps[1][:, 0, 8:9], ab_b[:, :], ALU.add)
            nc.vector.tensor_tensor(w_mix[:, :, :], wl[:, 2:4, :], ps[2][:, 0:2, :], ALU.subtract)
            link(nc.vector.tensor_copy(w_ffn_plain[:, :], ps[0][:, 2, :]))
            PLAIN_READY = chain[0]
            dve.wait_ge(prep_t, 2)
            link(nc.vector.tensor_copy(crow[:, :, :], bias_rows[:, :, :]))
            link(nc.vector.tensor_tensor(crow[:, 1, :], ps[3][:, 0, :], bias_rows[:, 1, :], ALU.add))
            for part in range(3):
                link(nc.vector.tensor_copy(cpart[:, part, :, :], crow[:, :, :]))
                if part < 2:
                    link(nc.vector.tensor_tensor(crow[:, :, :], crow[:, :, :], cpart[:, part, :, :], ALU.subtract))
            for j in range(3):
                link(nc.vector.memset(bias_mv[j][:, :, :], 0.0))
                for part in range(3):
                    row = slice(32 * part, 32 * part + 1)
                    last = nc.vector.tensor_copy(bias_mv[j][row, :, :],
                                                 cpart[row, part, j, :].unsqueeze(1).to_broadcast([1, 4, P]))
            link(last)

            nc.vector.memset(taken[:, :], 0.0)
            link(nc.vector.memset(taken_bf[:, :], 0.0))
            prep_ready[0] = chain[0]

            def tile_statistics(src, c, step_sem, n):
                for t in range(TILES):
                    last = nc.vector.bn_stats(stats[c][:, t, :], src[:, t, :])
                last.then_inc(step_sem, 1)

            def half_differences(c, step_sem, n):
                st, sm = stats[c], small[c]
                dve.wait_ge(step_sem, n * 3 + 1)
                nc.vector.tensor_tensor(sm[:, 0, :], st[:, :, 1], st[:, :, 4], ALU.subtract)
                nc.vector.scalar_tensor_tensor(sm[:, 1, :], st[:, :, 2], EPS * D, st[:, :, 5], ALU.add,
                                               ALU.add).then_inc(step_sem, 1)

            def between_halves(c, step_sem, n):
                sm = small[c]
                dve.wait_ge(step_sem, n * 3 + 2)
                nc.vector.scalar_tensor_tensor(sm[:, 2, :], sm[:, 0, :], 0.25, sm[:, 0, :], ALU.mult,
                                               ALU.mult).then_inc(step_sem, 1)

            def variance(c, step_sem, n, var_sem):
                sm = small[c]
                dve.wait_ge(step_sem, n * 3 + 3)
                nc.vector.scalar_tensor_tensor(var[c][:, :], sm[:, 1, :], 1.0 / D, sm[:, 2, :], ALU.mult,
                                               ALU.add).then_inc(var_sem, 1)

            def statistics(src, c, step_sem, n, var_sem, mean_n=None, mean_sem=mean_step):
                tile_statistics(src, c, step_sem, n)
                half_differences(c, step_sem, n)
                if mean_n is not None:
                    nc.vector.tensor_tensor(small[c][:, 3, :], stats[c][:, :, 1], stats[c][:, :, 4],
                                            ALU.add).then_inc(mean_sem, 1)
                between_halves(c, step_sem, n)
                if mean_n is not None:
                    dve.wait_ge(mean_sem, mean_n + 1)
                    nc.vector.tensor_scalar(neg_mean[c][:, :], small[c][:, 3, :], -0.5, None, ALU.mult)
                variance(c, step_sem, n, var_sem)

            def over_e(v):
                return v.unsqueeze(2).to_broadcast([P, TILES, NE])

            def over_t(v):
                return v.unsqueeze(1).to_broadcast([P, TILES, NE])

            def linker(step_sem, first):
                at = [0]

                def linked(ins):
                    at[0] += 1
                    ins.then_inc(step_sem, 1)
                    dve.wait_ge(step_sem, first + at[0])
                return linked, at

            def route_a(s, n):
                c = s % 4
                linked, at = linker(a_step, n * A_STEPS)
                dve.wait_ge(logit_psum, n + 1)
                dve.wait_ge(r_small, n * SMALL_STEPS + SMALL_STEPS)
                linked(nc.vector.tensor_tensor(logits[c][:, :, :], ps[c][:, 0, 0:TILES * NE].rearrange(
                    "p (t e) -> p t e", e=NE), over_e(extra[c][:, 3, :]), ALU.mult))
                linked(nc.vector.tensor_tensor(logits[c][:, :, :], logits[c][:, :, :], over_t(br_b[:, :]), ALU.add))
                linked(nc.vector.tensor_reduce(edge[c][:, 0, :], logits[c][:, :, :], AX.X, ALU.max))
                assert at[0] == A_STEPS
                nc.vector.tensor_tensor(logits[c][:, :, :], logits[c][:, :, :], over_e(edge[c][:, 0, :]),
                                        ALU.subtract).then_inc(centred_logits, 1)
                nc.vector.tensor_copy(rows_b[s][:, :, 0:D], rows_a[s][:, :, 0:D]).then_inc(rows_copied, 1)

            def route_b(s, n, tile0):
                c = s % 4
                pr, ed, cd, ht = probs[c][:, :, :], edge[c], cand[s % 2][:, :, :], hot[c]
                linked, at = linker(b_step, n * B_STEPS)
                dve.wait_ge(exps, n + 1)
                linked(nc.vector.tensor_reduce(ed[:, 1, :], pr, AX.X, ALU.add))
                linked(nc.vector.reciprocal(ed[:, 2, :], ed[:, 1, :]))
                linked(nc.vector.tensor_tensor(pr, pr, over_e(ed[:, 2, :]), ALU.mult))
                for k in range(2):
                    linked(nc.vector.tensor_reduce(ed[:, 3 + k, :], pr, AX.X, ALU.max))
                    linked(nc.vector.tensor_tensor(cd, pr, over_e(ed[:, 3 + k, :]), ALU.is_ge))
                    linked(nc.vector.tensor_tensor(cd, cd, over_t(descend[:, :]), ALU.mult))
                    linked(nc.vector.tensor_reduce(ed[:, 5 + k, :], cd, AX.X, ALU.max))
                    if k == 1:
                        nc.vector.tensor_tensor(ed[:, 7, :], ed[:, 3, :], ed[:, 4, :], ALU.add)
                    linked(nc.vector.tensor_tensor(ht[:, k, :, :], over_t(descend[:, :]), over_e(ed[:, 5 + k, :]),
                                                   ALU.is_equal))
                    if k == 0:
                        linked(nc.vector.scalar_tensor_tensor(pr, ht[:, 0, :, :], -4.0, pr, ALU.mult, ALU.add))
                nc.vector.tensor_tensor(chosen[c][:, :, :], ht[:, 0, :, :], ht[:, 1, :, :], ALU.add)
                linked(nc.vector.reciprocal(ed[:, 1, :], ed[:, 7, :]))
                assert at[0] == B_STEPS
                for k in range(2):
                    nc.vector.tensor_tensor(share[:, k, bass.ds(tile0, TILES)], ed[:, 3 + k, :], ed[:, 1, :],
                                            ALU.mult)
                nc.vector.tensor_reduce(taken_new[:, :], chosen[c][:, :, :].rearrange("p t e -> p e t"), AX.X,
                                        ALU.add).then_inc(chosen_ready, 1)

            def route_c(s, n):
                c = s % 4
                linked, at = linker(c_step, n * C_STEPS)
                dve.wait_ge(rank_psum, n + 1)
                nc.vector.tensor_tensor(taken[:, :], taken[:, :], taken_new[:, :], ALU.add)
                linked(nc.vector.tensor_tensor(logits[c][:, :, :], ps[c][:, 4, 0:TILES * NE].rearrange(
                    "p (t e) -> p t e", e=NE), over_t(region_0[:, :]), ALU.add))
                nc.vector.tensor_copy(taken_bf[:, :], taken[:, :])
                linked(nc.vector.tensor_tensor(hot[c][:, :, :, :], hot[c][:, :, :, :], logits[c][:, :, :].unsqueeze(1)
                                               .to_broadcast([P, 2, TILES, NE]), ALU.mult))
                linked(nc.vector.tensor_reduce(rank[c][:, :, :], hot[c][:, :, :, :], AX.X, ALU.add))
                assert at[0] == C_STEPS
                nc.vector.tensor_copy(slot[:, s, :, :], rank[c][:, :, :]).then_inc(slots_ready, 1)

            with dve.Fori(0, GROUPS) as g:
                nc.vector.memset(tick[:, :], 0.0).then_inc(group_open, 1)
                for k in range(STREAMS + X1_STATS_LAG):
                    a, b, d, e = in_flight(k, NUM_LAG, X1_LAG, 0, X1_STATS_LAG)
                    if a is not None:
                        c, n = a % 4, g * STREAMS + a
                        dve.wait_ge(h_psum, n + 1)
                        nc.vector.tensor_tensor(work[c][:, :, :], ps[c][:, :, :], wide(soft_f[c][:, :]),
                                                ALU.mult).then_inc(src_ready, 1)
                    if b is not None:
                        c, n = b % 4, g * STREAMS + b
                        dve.wait_ge(num_psum, n + 1)
                        nc.vector.tensor_tensor(act_z[c][:, :, :], ps[c][:, :, :], wide(soft[c][:, 2, :]),
                                                ALU.mult).then_inc(gnn0_rows, 1)
                    if a is not None:
                        c, n = a % 4, g * STREAMS + a
                        dve.wait_ge(den_psum, n + 1)
                        nc.vector.tensor_tensor(soft[c][:, 0, :], ps[c][:, 0, 0:TILES], soft_e[c][:, :],
                                                ALU.mult).then_inc(soft_step, 1)
                        dve.wait_ge(soft_step, n * 2 + 1)
                        nc.vector.reciprocal(soft[c][:, 1, :], soft[c][:, 0, :]).then_inc(soft_step, 1)
                        dve.wait_ge(soft_step, n * 2 + 2)
                        nc.vector.tensor_tensor(soft[c][:, 2, :], soft[c][:, 1, :], soft_e[c][:, :],
                                                ALU.mult).then_inc(ratio_ready, 1)
                    if d is not None:
                        dve.wait_ge(x_in[d], g * 16 + 16)
                        statistics(resid[d], 4 + d % 4, stat_step[0], g * STREAMS + d, stat_var[0])
                    if e is not None:
                        dve.wait_ge(x1_ready, g * STREAMS + e + 1)
                        statistics(resid[e], e % 4, stat_step[1], g * STREAMS + e, stat_var[1], g * STREAMS + e)

                def iteration(base, peeled=False, tail=False):
                    for k in range(STREAMS):
                        (n, s), (m, r) = stages([STATS_LAG, SCALE_LAG], k, base, peeled, tail)
                        if n is not None:
                            dve.wait_ge(silu_done, n + 1)
                            tile_statistics(act_z[s % 4], s % 4, it_step, n)
                        if m is not None:
                            dve.wait_ge(it_pow, m + 1)
                            for t in range(POOL_TILES, POOL_TILES + VECTOR_TILES):
                                last = nc.vector.tensor_scalar(scaled[r % 4][:, t, :], act_z[r % 4][:, t, :],
                                                               rstd[r % 4][:, t:t + 1], None, ALU.mult)
                            last.then_inc(it_scaled_v, 1)
                        if n is not None:
                            half_differences(s % 4, it_step, n)
                            between_halves(s % 4, it_step, n)
                        if tail:
                            dve.wait_ge(product, base + (k - STREAMS + 1))
                            nc.vector.tensor_tensor(resid[k][:, :, :], ps[k % 4][:, :, :], resid[k][:, :, :],
                                                    ALU.add).then_inc(x2_ready, 1)
                        else:
                            h = start_h[k] if peeled else ps[k % 4][:, :, :]
                            dve.wait_ge(tanh_done, base + (k + 1))
                            nc.vector.scalar_tensor_tensor(work[k % 4][:, :, :], work[k % 4][:, :, :], 0.01,
                                                           h, ALU.mult, ALU.add).then_inc(state_read, 1)
                        if n is not None:
                            variance(s % 4, it_step, n, it_var)
                        if tail:
                            dve.wait_ge(x2_ready, g * STREAMS + k + 1)
                            if k >= 4:
                                dve.wait_ge(stat_pow[2], g * STREAMS + k - 3)
                            statistics(resid[k], 4 + k % 4, stat_step[2], g * STREAMS + k, stat_var[2])

                q0 = g * STEPS
                iteration(q0, peeled=True)
                with dve.Fori(q0 + STREAMS, q0 + STEPS, STREAMS) as q:
                    iteration(q)
                iteration(g * STEPS + STEPS, tail=True)
                for s in range(STREAMS):
                    dve.wait_ge(mix_psum, g * STREAMS + s + 1)
                    nc.vector.scalar_tensor_tensor(resid[s][:, :, :], ps[s % 4][:, :, :], 0.0, resid[s][:, :, :],
                                                   ALU.max, ALU.add).then_inc(x3_ready, 1)
                    n = g * STREAMS + s
                    dve.wait_ge(x3_ready, n + 1)
                    if s >= 4:
                        dve.wait_ge(r_small, (n - 3) * SMALL_STEPS)
                    statistics(resid[s], s % 4, r_stat, n, r_var, n, r_mean)
                for k in range(STREAMS + 3):
                    a, b, d = in_flight(k, 1, 2, 3)
                    if a is not None:
                        route_a(a, g * STREAMS + a)
                    if d is not None:
                        route_c(d, g * STREAMS + d)
                    if b is not None:
                        route_b(b, g * STREAMS + b, g * BATCHES + b * TILES)

            def table(ins):
                table_at[0] += 1
                ins.then_inc(table_step, 1)
                dve.wait_ge(table_step, table_at[0])

            table_at = [0]
            dve.wait_ge(total_psum, 1)
            table(nc.vector.tensor_copy(count_f[:, :], ps[0][:, 0, 0:NE]))
            shape = [P, NE, TOKENS // SLAB]
            table(nc.vector.tensor_tensor(below, slab_rows[:, :].unsqueeze(1).to_broadcast(shape),
                                          count_f[:, :].unsqueeze(2).to_broadcast(shape), ALU.is_lt))
            nc.vector.tensor_tensor(pad_f[:, :], count_f[:, :], region_0[:, :], ALU.add)
            table(nc.vector.tensor_reduce(slabs_f[:, :], below, AX.X, ALU.add))
            nc.vector.tensor_copy(pad_row[:, :], pad_f[:, :])
            table(nc.vector.tensor_copy(slab_end[:, 0:1], slabs_f[:, 0:1]))
            for e in range(1, NE):
                table(nc.vector.tensor_tensor(slab_end[:, e:e + 1], slab_end[:, e - 1:e], slabs_f[:, e:e + 1], ALU.add))
            shape = [P, SLABS, NE]
            table(nc.vector.tensor_tensor(past, slab_j[:, :].unsqueeze(2).to_broadcast(shape),
                                          slab_end[:, :].unsqueeze(1).to_broadcast(shape), ALU.is_ge))
            nc.vector.tensor_reduce(slab_e[:, :], past, AX.X, ALU.add)
            table(nc.vector.tensor_tensor(before, past, slabs_f[:, :].unsqueeze(1).to_broadcast(shape), ALU.mult))
            table(nc.vector.tensor_reduce(slab_0[:, :], before, AX.X, ALU.add))
            table(nc.vector.tensor_tensor(slab_0[:, :], slab_j[:, :], slab_0[:, :], ALU.subtract))
            table(nc.vector.tensor_scalar(slab_0[:, :], slab_0[:, :], float(SLAB), None, ALU.mult))
            table(nc.vector.scalar_tensor_tensor(slab_0[:, :], slab_e[:, :], float(REGION), slab_0[:, :], ALU.mult,
                                                 ALU.add))
            nc.vector.tensor_scalar(slab_row[:, :], slab_0[:, :], float(NE * REGION), None, ALU.min)
            nc.vector.tensor_scalar(slab_exp[:, :], slab_e[:, :], float(NE - 1), None,
                                    ALU.min).then_inc(tables_ready, 1)

            def turn(j_parts, q, b):
                dve.wait_ge(slab_flip, j_parts + 1)
                nc.vector.tensor_scalar(rows_T[b], psX[b], params_in[q][:, 0:1], params_in[q][:, 1:2], ALU.mult,
                                        ALU.add).then_inc(slab_turned, 1)

            turn(0, 0, 0)

            def expert(j, peeled=False, second=False, end=False):
                for q in range(4):
                    n = j + q
                    if not (end and q == 3):
                        turn(n + 1, (q + 1) % 4, (q + 1) % 2)
                    if q or not peeled:
                        join_bias(j + (q - 1), j if q else j - 4, (q - 1) % 4, peeled or second and q == 0)

            def join_bias(n, j, q, peeled):
                dve.wait_ge(y_psum, n + 1)
                if not peeled:
                    dve.wait_ge(y_stored[q], j * (4 * SUBS))
                nc.vector.tensor_tensor(y_out[q], psY[q % 2], b2_in[q].unsqueeze(1).to_broadcast([P, SUBS, D]),
                                        ALU.add).then_inc(y_ready, 1)

            expert(0, peeled=True)
            expert(4, second=True)
            with dve.Fori(8, SLABS - 4, 4) as j:
                expert(j)
            expert(SLABS - 4, end=True)
            join_bias(SLABS - 1, SLABS - 4, 3, False)

            for i in range(GROUPS * STREAMS):
                b = i % 2
                dve.wait_ge(fin_in[b], 48 * (i // 2 + 1))
                for k in range(2):
                    for t in range(TILES):
                        last = nc.vector.scalar_tensor_tensor(
                            scaled[b][:, t, :], act_z[2 * b + k][:, t, :],
                            share[:, k, i * TILES + t:i * TILES + t + 1], scaled[b][:, t, :], ALU.mult, ALU.add)
                    last.then_inc((fin_mid, fin_ready)[k], 1)
                    if k == 0:
                        dve.wait_ge(fin_mid, i + 1)

        @block.scalar
        def _(act):
            with act.Fori(0, GROUPS) as g:
                for k in range(STREAMS + H0_LAG):
                    a, b, d = in_flight(k, ADJ_LAG, H_LAG, H0_LAG)
                    if a is not None:
                        act.wait_ge(adj_psum, g * STREAMS + a + 1)
                        nc.scalar.copy(adjT[a], ps[a % 4][:, :, :]).then_inc(adjT_ready, 1)
                    if b is not None:
                        c, n = b % 4, g * STREAMS + b
                        act.wait_ge(x_flip, n + 1)
                        nc.scalar.copy(turned[c][:, :, :], ps[c][:, :, :]).then_inc(x_turned, 1)
                        act.wait_ge(ef_psum, n + 1)
                        ef = ps[c][:, 0, 0:2 * TILES].rearrange("p (t k) -> p t k", k=2)
                        nc.scalar.activation(soft_f[c][:, :], ef[:, :, 1], ACT.Exp, bias=c_ef[:, 1:2])
                        nc.scalar.activation(soft_e[c][:, :], ef[:, :, 0], ACT.Exp,
                                             bias=c_ef[:, 0:1]).then_inc(soft_e_ready, 1)
                    if d is not None:
                        act.wait_ge(shift_ready, g * STREAMS + d + 1)
                        for t in range(TILES):
                            last = nc.scalar.activation(start_h[d][:, t, :], resid[d][:, t, :], ACT.Identity,
                                                        bias=shift[d % 4][:, t:t + 1], scale=rstd[d % 4][:, t:t + 1])
                        last.then_inc(h0_ready, 1)

                def iteration(base, peeled=False, tail=False):
                    for k in range(EVAC_LAG if tail else STREAMS):
                        (n, s), (m, r), (l, v) = stages([EVAC_LAG, SCALE_LAG, SILU_LAG], k, base, peeled, tail)
                        if n is not None:
                            act.wait_ge(it_flip, n + 1)
                            nc.scalar.copy(turned[s % 4][:, :, :], ps[s % 4][:, :, :]).then_inc(it_turned, 1)
                        if not tail:
                            if peeled:
                                h = start_h[k]
                            else:
                                h = ps[k % 4][:, :, :]
                                act.wait_ge(product, base + (k - STREAMS + 1))
                            nc.scalar.activation(work[k % 4][:, :, :], h, ACT.Tanh).then_inc(tanh_done, 1)
                        if m is not None:
                            act.wait_ge(it_pow, m + 1)
                            for t in range(POOL_TILES + VECTOR_TILES, TILES):
                                last = nc.scalar.mul(scaled[r % 4][:, t, :], act_z[r % 4][:, t, :],
                                                     rstd[r % 4][:, t:t + 1])
                            last.then_inc(it_scaled_a, 1)
                        if l is not None:
                            act.wait_ge(state_read, l + 1)
                            if not (peeled and v < 4):
                                act.wait_ge(it_scaled, l - 3)
                                act.wait_ge(it_scaled_v, l - 3)
                                act.wait_ge(it_scaled_a, l - 3)
                            nc.scalar.activation(act_z[v % 4][:, :, :], work[v % 4][:, :, :],
                                                 ACT.Silu).then_inc(silu_done, 1)

                nc.scalar.activation(act_tick[:, :], minus_half[:, 0:1], ACT.Silu)
                act.wait_ge(h0_ready, g * STREAMS + STREAMS)
                q0 = g * STEPS
                iteration(q0, peeled=True)
                with act.Fori(q0 + STREAMS, q0 + STEPS, STREAMS) as q:
                    iteration(q)
                iteration(g * STEPS + STEPS, tail=True)
                act.wait_ge(product, g * STEPS + STEPS)
                for k in range(STREAMS + Q_LAG):
                    a, b = in_flight(k, 0, Q_LAG)
                    if a is not None:
                        act.wait_ge(x2_flip, g * STREAMS + a + 1)
                        if a >= 4:
                            act.wait_ge(mix_psum, g * STREAMS + a - 3)
                        nc.scalar.copy(turned[a % 4][:, :, :], ps[a % 4][:, :, :]).then_inc(x2_turned, 1)
                    if b is not None:
                        act.wait_ge(q_psum, g * STREAMS + b + 1)
                        nc.scalar.copy(act_z[b % 4][:, :, :], ps[b % 4][:, :, :]).then_inc(q_copied, 1)
                act.wait_ge(mix_psum, g * STREAMS + STREAMS)
                for k in range(STREAMS + 3):
                    a, b, d = in_flight(k, 0, 1, 3)
                    if a is not None:
                        act.wait_ge(r_small, (g * STREAMS + a) * SMALL_STEPS + SMALL_STEPS)
                        for t in range(TILES):
                            last = nc.scalar.activation(rows_a[a][:, t, 0:D], resid[a][:, t, :], ACT.Identity,
                                                        bias=shift[a % 4][:, t:t + 1],
                                                        scale=extra[a % 4][:, 4, t:t + 1])
                        last.then_inc(rows_ready, 1)
                    if b is not None:
                        act.wait_ge(r_flip, g * STREAMS + b + 1)
                        nc.scalar.copy(turned[b % 4][:, :, :], ps[b % 4][:, :, :]).then_inc(r_turned, 1)
                    if d is not None:
                        act.wait_ge(centred_logits, g * STREAMS + d + 1)
                        nc.scalar.activation(probs[d % 4][:, :, :], logits[d % 4][:, :, :], ACT.Exp).then_inc(exps, 1)
                act.wait_ge(scattered, (g + 1) * (16 * 2 * BATCHES))

            def gelus(n, q, b):
                for c in range(HC):
                    act.wait_ge(hidden_psum, n * HC + (c + 1))
                    nc.scalar.activation(hidden[b][c], psH[c], ACT.Gelu,
                                         bias=params_in[q][:, 2 + c:3 + c]).then_inc(hidden_ready, 1)

            with act.Fori(0, SLABS, 4) as j:
                for q in range(4):
                    gelus(j + q, q, q % 2)

        @block.tensor
        def _(pe):
            pe.wait_ge(consts_ready, 1)
            pe.wait_ge(prep_v, 4)
            nc.tensor.transpose(ps[0][:, 0, :], centred[:, 0, :], ident[:, :])
            nc.tensor.transpose(ps[0][:, 1, :], centred[:, 1, :], ident[:, :])
            nc.tensor.transpose(ps[0][:, 2, :], wl[:, 1, :], ident[:, :])
            nc.tensor.transpose(ps[1][:, 4, 0:(2 + HC) * NE], params_rows[:, :],
                                ident[0:(2 + HC) * NE, 0:(2 + HC) * NE])
            nc.tensor.matmul(ps[1][:, 0, 0:2], centred[:, 0, :], cols_in[:, 0:2], start=True, stop=True)
            nc.tensor.matmul(ps[1][:, 0, 8:10], wb_wide[:, :], cols_in[:, 0:2], start=True, stop=True)
            nc.tensor.matmul(ps[2][:, 0:2, :], mean_mat[:, :], wl[:, 2:4, :], start=True,
                             stop=True).then_inc(prep_t, 1)
            pe.wait_ge(prep_v, 5)
            nc.tensor.matmul(ps[3][:, 0, :], lnb_wide[:, :], w_ffn_plain[:, :], start=True,
                             stop=True).then_inc(prep_t, 1)
            pe.wait_ge(prep_v, prep_ready[0])

            def flip(c, src):
                for t in range(TILES):
                    last = nc.tensor.transpose(ps[c][:, t, :], src[:, t, :], ident[:, :])
                return last

            def rows(c, terms, bias=None):
                for bank in range(2):
                    if bias is not None:
                        nc.tensor.matmul(ps[c][:, 4 * bank:4 * bank + 4, :], ones_bf[:, :], bias_mv[bias][:, :, :],
                                         start=True, stop=False, skip_group_check=True)
                    for t in range(4 * bank, 4 * bank + 4):
                        for m, (stationary, moving) in enumerate(terms):
                            last = nc.tensor.matmul(ps[c][:, t, :], stationary[:, t, :], moving(t),
                                                    start=bias is None and m == 0, stop=m == len(terms) - 1,
                                                    skip_group_check=True)
                return last

            with pe.Fori(0, GROUPS) as g:
                pe.wait_ge(group_open, g + 1)
                for k in range(ADJ_LAG, STREAMS + NUM_LAG):
                    a, b, d = in_flight(k, ADJ_LAG, H_LAG, NUM_LAG)
                    if a is not None:
                        pe.wait_ge(adj_in[a % 2], g * (16 * STREAMS // 2) + 16 * (a // 2 + 1))
                        if a >= 4:
                            pe.wait_ge(gnn0_rows, g * STREAMS + a - 3)
                        flip(a % 4, raw[a % 2]).then_inc(adj_psum, 1)
                    if b is not None:
                        pe.wait_ge(adjT_ready, g * STREAMS + b + 1)
                        pe.wait_ge(x_scaled, g * STREAMS + b + 1)
                        flip(b % 4, scaled[b % 4]).then_inc(x_flip, 1)
                    if d is not None:
                        pe.wait_ge(src_ready, g * STREAMS + d + 1)
                        for t in range(TILES):
                            last = nc.tensor.matmul(ps[d % 4][:, 0, t:t + 1], adjT[d][:, t, :],
                                                    soft_f[d % 4][:, t:t + 1], start=True, stop=True)
                        last.then_inc(den_psum, 1)
                    if b is not None:
                        c = b % 4
                        pe.wait_ge(x_turned, g * STREAMS + b + 1)
                        for t in range(TILES):
                            last = nc.tensor.matmul(ps[c][:, 0, 2 * t:2 * t + 2], turned[c][:, t, :], w_ef[:, :],
                                                    start=True, stop=True)
                        last.then_inc(ef_psum, 1)
                        pe.wait_ge(soft_e_ready, g * STREAMS + b + 1)
                        rows(c, [(turned[c], lambda t: w_gnn0[:, :])], bias=0).then_inc(h_psum, 1)
                    if d is not None:
                        pe.wait_ge(ratio_ready, g * STREAMS + d + 1)
                        rows(d % 4, [(adjT[d], lambda t, c=d % 4: work[c][:, t, :])]).then_inc(num_psum, 1)

                def flip_step(n, s, peeled, last_iteration, first):
                    pe.wait_ge(it_scaled, n + 1)
                    pe.wait_ge(it_scaled_v, n + 1)
                    pe.wait_ge(it_scaled_a, n + 1)
                    if last_iteration and s >= 4:
                        pe.wait_ge(x2_ready, g * STREAMS + s - 3)
                    else:
                        pe.wait_ge(state_read, n + 5)
                    flip(s % 4, scaled[s % 4]).then_inc(it_flip, 1)

                def product_step(n, s):
                    pe.wait_ge(it_turned, n + 1)
                    rows(s % 4, [(turned[s % 4], lambda t: w_ffn[:, :])], bias=1).then_inc(product, 1)

                def iteration(base, peeled=False, tail=False):
                    for k in range(STREAMS):
                        for n, s in stages([FLIP_LAG], k, base, peeled, tail):
                            if n is not None:
                                flip_step(n, s, peeled, tail, False)
                        for n, s in stages([EVAC_LAG], k, base, peeled, tail):
                            if n is not None:
                                product_step(n, s)

                pe.wait_ge(gnn0_rows, g * STREAMS + STREAMS)
                q0 = g * STEPS
                iteration(q0, peeled=True)
                with pe.Fori(q0 + STREAMS, q0 + STEPS, STREAMS) as q:
                    iteration(q)
                iteration(g * STEPS + STEPS, tail=True)
                for k in range(STREAMS + MIX_LAG):
                    a, b, d = in_flight(k, 0, Q_LAG, MIX_LAG)
                    if a is not None:
                        pe.wait_ge(x2_scaled, g * STREAMS + a + 1)
                        if a < 4:
                            pe.wait_ge(x2_ready, g * STREAMS + a + 5)
                        else:
                            pe.wait_ge(x3_ready, g * STREAMS + a - 3)
                        flip(a % 4, scaled[a % 4]).then_inc(x2_flip, 1)
                    if b is not None:
                        pe.wait_ge(x2_turned, g * STREAMS + b + 1)
                        rows(b % 4, [(turned[b % 4], lambda t: w_mix[:, 1, :])]).then_inc(q_psum, 1)
                    if d is not None:
                        pe.wait_ge(q_copied, g * STREAMS + d + 1)
                        rows(d % 4, [(turned[d % 4], lambda t: w_mix[:, 0, :]),
                                     (adjT[d], lambda t, c=d % 4: act_z[c][:, t, :])], bias=2).then_inc(mix_psum, 1)
                for k in range(STREAMS + 3):
                    a, b, d = in_flight(k, 0, 1, 3)
                    if d is not None:
                        c, n = d % 4, g * STREAMS + d
                        pe.wait_ge(chosen_ready, n + 1)
                        ranks = ps[c][:, 4, 0:TILES * NE].rearrange("p (t e) -> p t e", e=NE)
                        nc.tensor.matmul(ranks, tri[:, :], chosen[c][:, :, :], start=True, stop=False,
                                         skip_group_check=True)
                        for t in range(TILES - 1):
                            rest = TILES - 1 - t
                            nc.tensor.matmul(ranks[:, t + 1:TILES, :], ones_bf[:, :],
                                             chosen[c][:, t, :].unsqueeze(1).to_broadcast([P, rest, NE]),
                                             start=False, stop=False, skip_group_check=True)
                        nc.tensor.matmul(ranks, ones_bf[:, :],
                                         taken_bf[:, :].unsqueeze(1).to_broadcast([P, TILES, NE]),
                                         start=False, stop=True, skip_group_check=True).then_inc(rank_psum, 1)
                    if b is not None:
                        c, n = b % 4, g * STREAMS + b
                        pe.wait_ge(r_turned, n + 1)
                        for t in range(TILES):
                            last = nc.tensor.matmul(ps[c][:, 0, t * NE:(t + 1) * NE], turned[c][:, t, :], wr[:, :],
                                                    start=True, stop=True)
                        last.then_inc(logit_psum, 1)
                    if a is not None:
                        c, n = a % 4, g * STREAMS + a
                        pe.wait_ge(rows_ready, n + 1)
                        if a < 4:
                            pe.wait_ge(x3_ready, g * STREAMS + a + 5)
                        else:
                            pe.wait_ge(slots_ready, n - 3)
                        flip(c, start_h[a]).then_inc(r_flip, 1)

            pe.wait_ge(slots_ready, GROUPS * STREAMS)
            nc.tensor.matmul(ps[0][:, 0, 0:NE], ones_bf[:, :], taken_bf[:, :], start=True,
                             stop=True).then_inc(total_psum, 1)
            pe.wait_ge(tables_ready, 1)

            def turn(j, q, b):
                pe.wait_ge(slab_in[q], j * (4 * SLAB_LOADS) + 16 * SLAB_LOADS)
                for t in range(SUBS):
                    last = nc.tensor.transpose(psX[b][:, t * P:(t + 1) * P], rows_in[q][:, t, 0:D], ident[:, :])
                last.then_inc(slab_flip, 1)

            def first_product(n, q, b, peeled):
                pe.wait_ge(slab_turned, n + 1)
                for c in range(HC):
                    if not peeled:
                        pe.wait_ge(hidden_ready, (n - 1) * HC + (c + 1))
                    nc.tensor.matmul(psH[c], w1_in[q][:, c * P:(c + 1) * P], rows_T[b], start=True,
                                     stop=True).then_inc(hidden_psum, 1)

            def second_product(n, q, b, peeled):
                pe.wait_ge(hidden_ready, n * HC + HC)
                if not peeled:
                    pe.wait_ge(y_ready, n - 1)
                for t in range(SUBS):
                    for c in range(HC):
                        last = nc.tensor.matmul(psY[b][:, t, :], hidden[b][c][:, t * P:(t + 1) * P],
                                                w2_in[q][:, c, :], start=c == 0, stop=c == HC - 1,
                                                skip_group_check=True)
                last.then_inc(y_psum, 1)

            def expert(j, first=False, end=False):
                for q in range(4):
                    n = j + q
                    first_product(n, q, q % 2, first and q == 0)
                    if not (end and q == 3):
                        turn(j if q < 3 else j + 4, (q + 1) % 4, (q + 1) % 2)
                    if not (first and q == 0):
                        second_product(j + (q - 1), (q - 1) % 4, (q - 1) % 2, first and q < 3)

            turn(0, 0, 0)
            expert(0, first=True)
            with pe.Fori(4, SLABS - 4, 4) as j:
                expert(j)
            expert(SLABS - 4, end=True)
            second_product(SLABS - 1, 3, 1, False)


_INS = ["x", "adj", "L0_gnn_W_w", "L0_gnn_W_b", "L0_gnn_a_w", "L0_gnn_a_b", "L0_ffn_ln_w", "L0_ffn_ln_b",
        "L0_ffn_W", "L0_ffn_b", "L1_gnn_weight", "L1_gnn_bias", "L1_ffn_Wr", "L1_ffn_br", "L1_ffn_ln_g", "L1_ffn_ln_b", "L1_ffn_W1",
        "L1_ffn_b1", "L1_ffn_W2", "L1_ffn_b2"]
_OUTS = [((128, 128, 128), "float32")]


def kernel(**inputs):
    import numpy as _np
    import concourse.bacc as _bacc
    from concourse import mybir as _mybir
    from concourse.bass_utils import run_bass_kernel_spmd as _run

    nc = _bacc.Bacc("TRN2", target_bir_lowering=False, num_devices=1)
    arrays, args = {}, []
    for name in _INS:
        a = _np.ascontiguousarray(inputs[name])
        arrays[f"in_{name}_dram"] = a
        args.append(nc.dram_tensor(f"in_{name}_dram", a.shape, _mybir.dt.from_np(a.dtype), kind="ExternalInput").ap())
    for i, (shape, dtype) in enumerate(_OUTS):
        dt = _mybir.dt.from_np(_np.dtype(dtype))
        args.append(nc.dram_tensor(f"out_{i}_dram", shape, dt, kind="ExternalOutput").ap())
    network(nc, *args)
    r = _run(nc, [arrays], core_ids=[0])
    got = tuple(r.results[0][f"out_{i}_dram"] for i in range(len(_OUTS)))
    return got[0]
```

```python
from contextlib import ExitStack

import concourse.bass as bass
from concourse import mybir

F32 = mybir.dt.float32
BF16 = mybir.dt.bfloat16
I32 = mybir.dt.int32
U32 = mybir.dt.uint32
ALU = mybir.AluOpType
ACT = mybir.ActivationFunctionType
AX = mybir.AxisListType

P = 128
EPS = 1e-5


def network(nc, x, adj, W_w, W_b, a_w, a_b, ln_w, ln_b, F_W, F_b, G_w, G_b,
            R_w, R_b, E_g, E_b, E_W1, E_b1, E_W2, E_b2, out):
    B, N, D = x.shape
    assert N == P and D == P
    TILES = 8
    STREAMS = 8
    BANKS = 4
    ITERS = 30
    COLS = TILES * D
    GROUPS = B // (TILES * STREAMS)
    STEPS = STREAMS * ITERS
    NE = R_w.shape[1]
    H = E_W1.shape[2]
    HC = H // P
    TOKENS = B * N
    SLAB = 512
    SUBS = SLAB // P
    TOKEN, FIRST, WEIGHT = D, D + 1, D + 2
    ROW = D + 4
    REGION = TOKENS + SLAB
    SLABS = (2 * TOKENS + NE * (SLAB - 1)) // SLAB
    SLABS += -SLABS % 4
    FAR = 1 << 20
    BATCHES = TILES * STREAMS

    with ExitStack() as ctx:
        def sb(name, shape, dt=F32):
            return ctx.enter_context(nc.sbuf_tensor(name, shape, dt))

        def sem(name):
            return ctx.enter_context(nc.semaphore(name))

        ps = [ctx.enter_context(nc.psum_tensor(f"ps{j}", [P, TILES, D], F32)) for j in range(BANKS)]

        resid = [sb(f"resid{s}", [P, TILES, D]) for s in range(STREAMS)]
        adjT = [sb(f"adjT{s}", [P, TILES, N]) for s in range(STREAMS)]
        rows_a = [sb(f"start_h{s}", [P, TILES, ROW]) for s in range(STREAMS)]
        start_h = [t[:, :, 0:D] for t in rows_a]
        raw = [sb(f"raw{j}", [P, TILES, D]) for j in range(2)]
        work = [sb(f"work{j}", [P, TILES, D]) for j in range(4)]
        act_z = [sb(f"act_z{j}", [P, TILES, D]) for j in range(4)]
        scaled = [sb(f"scaled{j}", [P, TILES, D]) for j in range(4)]
        turned = [sb(f"turned{j}", [P, TILES, D]) for j in range(4)]
        stats = [sb(f"stats{j}", [P, TILES, 6]) for j in range(8)]
        small = [sb(f"small{j}", [P, 5, TILES]) for j in range(8)]
        var = [sb(f"var{j}", [P, TILES]) for j in range(8)]
        rstd = [sb(f"rstd{j}", [P, TILES]) for j in range(8)]
        neg_mean = [sb(f"neg_mean{j}", [P, TILES]) for j in range(4)]
        shift = [sb(f"shift{j}", [P, TILES]) for j in range(4)]
        soft_f = [sb(f"soft_f{j}", [P, TILES]) for j in range(4)]
        soft_e = [sb(f"soft_e{j}", [P, TILES]) for j in range(4)]
        soft = [sb(f"soft{j}", [P, 3, TILES]) for j in range(4)]
        minus_half = sb("minus_half", [P, TILES])
        tick = sb("tick", [P, 1])
        tokens_out = [sb(f"tokens_out{j}", [P, SUBS], I32) for j in range(4)]
        slab_w = [sb(f"slab_w{j}", [P, 3, SUBS]) for j in range(4)]
        pool_buf = sb("pool_buf", [P, 1])
        act_tick = sb("act_tick", [P, 1])
        ident = sb("ident", [P, P])
        mean_mat = sb("mean_mat", [P, P])
        ones_bf = sb("ones_bf", [P, P], BF16)
        ones_f = sb("ones_f", [P, P])

        wr = sb("wr", [P, NE])
        br_b = sb("br_b", [P, NE])
        tri = sb("tri", [P, P], BF16)
        descend = sb("descend", [P, NE])
        region_0 = sb("region_0", [P, NE])
        ids = sb("ids", [P, B], I32)
        extra = [sb(f"extra{j}", [P, 4, TILES]) for j in range(4)]
        std_y = [sb(f"std_y{s}", [P, TILES]) for s in range(STREAMS)]
        logits = [sb(f"logits{j}", [P, TILES, NE]) for j in range(4)]
        probs = [sb(f"probs{j}", [P, TILES, NE]) for j in range(4)]
        edge = [sb(f"edge{j}", [P, 8, TILES]) for j in range(4)]
        cand = [sb(f"cand{j}", [P, TILES, NE]) for j in range(2)]
        hot = [sb(f"hot{j}", [P, 2, TILES, NE]) for j in range(4)]
        chosen = [sb(f"chosen{j}", [P, TILES, NE], BF16) for j in range(4)]
        rank = [sb(f"rank{j}", [P, 2, TILES]) for j in range(4)]
        slot = sb("slot", [P, STREAMS, 2, TILES], I32)
        taken = sb("taken", [P, NE])
        taken_new = [sb(f"taken_new{j}", [P, NE]) for j in range(2)]
        taken_bf = sb("taken_bf", [P, NE], BF16)
        slab_j = sb("slab_j", [P, SLABS])
        slab_rows = sb("slab_rows", [P, TOKENS // SLAB])
        count_f = sb("count_f", [P, NE])
        slabs_f = sb("slabs_f", [P, NE])
        slab_end = sb("slab_end", [P, NE])
        pad_f = sb("pad_f", [P, NE])
        slab_e = sb("slab_e", [P, SLABS])
        slab_0 = sb("slab_0", [P, SLABS])
        slab_row = sb("slab_row", [P, SLABS], I32)
        slab_exp = sb("slab_exp", [P, SLABS], I32)
        pad_row = sb("pad_row", [P, NE], I32)
        pad = sb("pad", [P, SUBS, ROW], I32)
        PARAMS = 3 + HC
        params_rows = sb("params_rows", [(2 + HC) * NE, P])
        params = sb("params", [P, NE, PARAMS])
        params_in = [sb(f"params_in{j}", [P, PARAMS]) for j in range(4)]

        def part(t, first, n):
            return t[:, :, :].rearrange("p t d -> p (t d)")[:, first:first + n]

        def by_tile(v, n):
            return v.rearrange("p (t d) -> p t d", t=n)

        below = [part(turned[j], 0, TOKENS // SLAB * NE) for j in range(1)][0].rearrange("p (e j) -> p e j", e=NE)
        past = part(turned[1], 0, SLABS * NE).rearrange("p (j e) -> p j e", e=NE)
        before = part(turned[2], 0, SLABS * NE).rearrange("p (j e) -> p j e", e=NE)
        rows_in = [by_tile(part(rows_a[q], 0, SUBS * ROW), SUBS) for q in range(4)]
        w1_in = [part(rows_a[q], SUBS * ROW, H) for q in range(4)]
        w2_in = [by_tile(part(adjT[q], 0, HC * D), HC) for q in range(4)]
        b2_in = [part(adjT[q], HC * D, D) for q in range(4)]
        y_out = [by_tile(part(rows_a[4 + q], 0, SLAB), SUBS) for q in range(4)]
        rows_T = [part(resid[4], SLAB * j, SLAB) for j in range(2)]
        hidden = [[part(resid[2 * j + c // 2], SLAB * (c % 2), SLAB) for c in range(HC)] for j in range(2)]
        psX = [part(ps[0], SLAB * j, SLAB) for j in range(2)]
        psH = [part(ps[1 + c // 2], SLAB * (c % 2), SLAB) for c in range(HC)]
        psY = [by_tile(part(ps[3], SLAB * j, SLAB), SUBS) for j in range(2)]

        sorted_rows = nc.dram_tensor("sorted_rows", (NE * REGION + SLAB, ROW), F32, kind="Internal").ap()
        params_dram = nc.dram_tensor("params_dram", (P, NE, PARAMS), F32, kind="Internal").ap()

        wl = sb("wl", [P, 4, P])
        lnw_b = sb("lnw_b", [P, P])
        cols_in = sb("cols_in", [P, 4])
        ab_b = sb("ab_b", [P, 1])
        bias_rows = sb("bias_rows", [P, 3, P])
        lnb_wide = sb("lnb_wide", [P, P])
        wb_wide = sb("wb_wide", [P, P])
        centred = sb("centred", [P, 2, P])
        sums = sb("sums", [P, 4])
        w_gnn0 = sb("w_gnn0", [P, P])
        w_ef = sb("w_ef", [P, 2])
        c_ef = sb("c_ef", [P, 2])
        w_ffn = sb("w_ffn", [P, P])
        w_ffn_plain = sb("w_ffn_plain", [P, P])
        w_mix = sb("w_mix", [P, 2, P])
        crow = sb("crow", [P, 3, P])
        cpart = sb("cpart", [P, 3, 3, P], BF16)
        bias_mv = [sb(f"bias_mv{j}", [P, 4, P], BF16) for j in range(3)]

        weights_in = sem("weights_in")
        consts_ready = sem("consts_ready")
        prep_v = sem("prep_v")
        prep_t = sem("prep_t")
        group_open = sem("group_open")
        x_in = [sem(f"x_in{s}") for s in range(STREAMS)]
        adj_in = [sem(f"adj_in{s}") for s in range(2)]
        out_done = [sem(f"out_done{s}") for s in range(STREAMS)]
        adj_psum = sem("adj_psum")
        adjT_ready = sem("adjT_ready")
        stat_step = [sem(f"stat_step{j}") for j in range(3)]
        stat_var = [sem(f"stat_var{j}") for j in range(3)]
        stat_pow = [sem(f"stat_pow{j}") for j in range(3)]
        mean_step = sem("mean_step")
        shift_ready = sem("shift_ready")
        pool_step = sem("pool_step")
        x_scaled = sem("x_scaled")
        x2_scaled = sem("x2_scaled")
        x_flip = sem("x_flip")
        x2_flip = sem("x2_flip")
        x_turned = sem("x_turned")
        x2_turned = sem("x2_turned")
        h_psum = sem("h_psum")
        ef_psum = sem("ef_psum")
        soft_e_ready = sem("soft_e_ready")
        den_psum = sem("den_psum")
        src_ready = sem("src_ready")
        soft_step = sem("soft_step")
        ratio_ready = sem("ratio_ready")
        num_psum = sem("num_psum")
        x1_ready = sem("x1_ready")
        h0_ready = sem("h0_ready")
        x2_ready = sem("x2_ready")
        q_psum = sem("q_psum")
        q_copied = sem("q_copied")
        mix_psum = sem("mix_psum")
        x3_ready = sem("x3_ready")
        a_step = sem("a_step")
        b_step = sem("b_step")
        c_step = sem("c_step")
        r_stat = sem("r_stat")
        r_mean = sem("r_mean")
        r_var = sem("r_var")
        r_var2 = sem("r_var2")
        r_pow = sem("r_pow")
        r_small = sem("r_small")
        r_scales = sem("r_scales")
        rows_ready = sem("rows_ready")
        ids_ready = sem("ids_ready")
        r_flip = sem("r_flip")
        r_turned = sem("r_turned")
        logit_psum = sem("logit_psum")
        centred_logits = sem("centred_logits")
        exps = sem("exps")
        chosen_ready = sem("chosen_ready")
        rank_psum = sem("rank_psum")
        slots_ready = sem("slots_ready")
        scattered = [sem(f"scattered{s}") for s in range(STREAMS)]
        total_psum = sem("total_psum")
        tables_ready = sem("tables_ready")
        pads_in = sem("pads_in")
        table_step = sem("table_step")
        params_ready = sem("params_ready")
        pool_tick = sem("pool_tick")
        params_stored = sem("params_stored")
        slab_in = [sem(f"slab_in{q}") for q in range(4)]
        slab_flip = sem("slab_flip")
        slab_turned = sem("slab_turned")
        hidden_psum = sem("hidden_psum")
        hidden_ready = sem("hidden_ready")
        y_psum = sem("y_psum")
        weight_step = sem("weight_step")
        y_biased = sem("y_biased")
        y_ready = sem("y_ready")
        y_stored = [sem(f"y_stored{q}") for q in range(4)]
        tanh_done = sem("tanh_done")
        state_read = sem("state_read")
        silu_done = sem("silu_done")
        it_step = sem("it_step")
        it_var = sem("it_var")
        it_pow = sem("it_pow")
        it_scaled = sem("it_scaled")
        it_scaled_v = sem("it_scaled_v")
        it_scaled_a = sem("it_scaled_a")
        it_flip = sem("it_flip")
        it_turned = sem("it_turned")
        product = sem("product")

        xv = x.rearrange("(g s t) n d -> g s n t d", g=GROUPS, s=STREAMS)
        av = adj.rearrange("(g s t) n d -> g s n t d", g=GROUPS, s=STREAMS)
        ov = out.rearrange("(g s t) n d -> g s n t d", g=GROUPS, s=STREAMS)
        out_rows = out.rearrange("b n d -> (b n) d")
        A_STEPS, B_STEPS, C_STEPS, SMALL_STEPS = 3, 15, 3, 3
        SLAB_LOADS = 5

        prep_ready = [0]

        block = ctx.enter_context(nc.Block())

        def wide(v):
            return v.unsqueeze(2).to_broadcast([P, v.shape[1], D])

        loads = ((wl[:, 0, :], W_w), (wl[:, 1, :], F_W), (wl[:, 2, :], G_w[0:D, :]),
                 (wl[:, 3, :], G_w[D:2 * D, :]),
                 (lnw_b[:, :], ln_w.partition_broadcast(P)),
                 (cols_in[:, 0:1], a_w[0:D].rearrange("(p o) -> p o", o=1)),
                 (cols_in[:, 1:2], a_w[D:2 * D].rearrange("(p o) -> p o", o=1)),
                 (cols_in[:, 2:3], ln_b.rearrange("(p o) -> p o", o=1)),
                 (cols_in[:, 3:4], W_b.rearrange("(p o) -> p o", o=1)),
                 (ab_b[:, :], a_b.partition_broadcast(P)),
                 (bias_rows[:, 0, :], W_b.partition_broadcast(P)),
                 (bias_rows[:, 1, :], F_b.partition_broadcast(P)),
                 (bias_rows[:, 2, :], G_b.partition_broadcast(P)),
                 (params_rows[0:NE, :], E_g), (params_rows[NE:2 * NE, :], E_b),
                 (params_rows[2 * NE:(2 + HC) * NE, :], E_b1.rearrange("e (c p) -> (e c) p", p=P)),
                 (wr[:, :], R_w), (br_b[:, :], R_b.partition_broadcast(P)))

        SILU_LAG, STATS_LAG, SCALE_LAG, FLIP_LAG, EVAC_LAG = 1, 2, 4, 5, 6
        POOL_TILES, VECTOR_TILES = 6, 1

        X_LAG, ADJ_LAG, TURN_LAG, H_LAG, NUM_LAG, X1_STATS_LAG, H0_LAG = 1, 1, 2, 3, 4, 5, 6
        Q_LAG, MIX_LAG, ROWS_LAG = 1, 2, 4
        FLIP_R, LOGIT_R, CHOICE_R, RANK_R = 7, 8, 9, 10

        def in_flight(k, *lags):
            return [k - lag if 0 <= k - lag < STREAMS else None for lag in lags]

        def stages(lags, k, base, peeled, tail):
            for lag in lags:
                j = k - lag
                if tail and j >= 0 or peeled and j < 0:
                    yield None, None
                else:
                    yield base + j, j % STREAMS

        @block.sync
        def _(sp):
            for dst, src in loads:
                sp.dma_start(dst, src).then_inc(weights_in, 16)
            def load_x(g, s):
                sp.dma_start(resid[s][:, :, :], xv[g, s]).then_inc(x_in[s], 16)

            for g in range(GROUPS):
                for s in range(STREAMS):
                    if g or s >= 2:
                        sp.wait_ge(adj_psum, g * STREAMS + s - 1)
                    sp.dma_start(raw[s % 2][:, :, :], av[g, s]).then_inc(adj_in[s % 2], 16)
                    if g == 0:
                        load_x(g, s)
                if g == 0:
                    sp.wait_ge(params_ready, 1)
                    sp.dma_start(params_dram, params[:, :, :]).then_inc(params_stored, 16)
                for s in range(STREAMS + 1):
                    if s < STREAMS:
                        sp.wait_ge(x3_ready, g * STREAMS + s + 1)
                        sp.dma_start(ov[g, s], resid[s][:, :, :]).then_inc(out_done[s], 16)
                    if s >= 1:
                        sp.wait_ge(out_done[s - 1], g * 16 + 16)
                        if g + 1 < GROUPS:
                            sp.wait_ge(rows_ready, g * STREAMS + s)
                            load_x(g + 1, s - 1)

            sp.wait_ge(tables_ready, 1)
            for e in range(NE + 1):
                if e < NE:
                    at = sp.value_load(pad_row[0:1, e:e + 1], min_val=e * REGION, max_val=e * REGION + TOKENS)
                    dst = sorted_rows[bass.ds(at, SLAB), :]
                else:
                    dst = sorted_rows[NE * REGION:NE * REGION + SLAB, :]
                sp.dma_start(dst.rearrange("(t p) d -> p t d", t=SUBS),
                             pad[:, :, :].bitcast(F32)).then_inc(pads_in, 16)
            sp.wait_ge(pads_in, 16 * (NE + 1))
            for s in range(STREAMS):
                sp.wait_ge(scattered[s], GROUPS * 2 * TILES * 16)
            sp.wait_ge(params_stored, 16)

            def load_slab(j, q, wait):
                at = sp.value_load(slab_row[0:1, bass.ds(j, 1)], min_val=0, max_val=NE * REGION)
                e = sp.value_load(slab_exp[0:1, bass.ds(j, 1)], min_val=0, max_val=NE - 1)
                wait()
                sp.dma_start(rows_in[q], sorted_rows[bass.ds(at, SLAB), :].rearrange("(t p) d -> p t d", p=P)
                             ).then_inc(slab_in[q], 16)
                sp.dma_start(w1_in[q], E_W1[bass.ds(e, 1)].rearrange("o p n -> p (o n)")).then_inc(slab_in[q], 16)
                sp.dma_start(w2_in[q], E_W2[bass.ds(e, 1)].rearrange("o (c p) d -> p (o c) d", p=P)
                             ).then_inc(slab_in[q], 16)
                sp.dma_start(b2_in[q], E_b2[bass.ds(e, 1)].rearrange("o d -> (o d)").partition_broadcast(P)
                             ).then_inc(slab_in[q], 16)
                sp.dma_start(params_in[q][:, :], params_dram[:, bass.ds(e, 1), :].rearrange("p o c -> p (o c)")
                             ).then_inc(slab_in[q], 16)

            for q in range(4):
                load_slab(q, q, lambda: None)
            for j in range(4, SLABS):
                def wait():
                    sp.wait_ge(y_ready, j - 3)
                load_slab(j, j % 4, wait)

            for q in range(4):
                sp.wait_ge(y_stored[q], 16 * SUBS * SLABS // 4)

        @block.gpsimd
        def _(pool):
            nc.gpsimd.memset(ident[:, :], 0.0).then_inc(pool_step, 1)
            nc.gpsimd.memset(minus_half[:, :], -0.5)
            nc.gpsimd.memset(pool_buf[:, :], 0.0).then_inc(pool_tick, 1)
            nc.gpsimd.memset(mean_mat[:, :], 1.0 / D)
            nc.gpsimd.memset(ones_bf[:, :], 1.0)
            nc.gpsimd.memset(ones_f[:, :], 1.0)
            for dst, step, first in ((descend, -1, NE), (region_0, REGION, 0), (slab_j, 1, 0), (slab_rows, SLAB, 0)):
                nc.gpsimd.iota(dst[:, :], pattern=[[step, dst.shape[1]]], base=first, channel_multiplier=0,
                               allow_small_or_imprecise_dtypes=True)
            nc.gpsimd.iota(ids[:, :], pattern=[[N, B]], base=0, channel_multiplier=1)
            nc.gpsimd.memset(pad[:, :, :], 0)
            nc.gpsimd.memset(tri[:, :], 0.0).then_inc(pool_step, 1)
            pool.wait_ge(pool_step, 2)
            nc.gpsimd.iota(pad[:, :, TOKEN], pattern=[[1, SUBS]], base=FAR, channel_multiplier=SUBS)
            nc.gpsimd.affine_select(out=tri[:, :], in_=tri[:, :], compare_op=ALU.is_ge, fill=1.0, base=0,
                                    pattern=[[-1, P]], channel_multiplier=1)
            nc.gpsimd.affine_select(out=ident[:, :], in_=ident[:, :], compare_op=ALU.not_equal, fill=1.0, base=0,
                                    pattern=[[-1, P]], channel_multiplier=1).then_inc(consts_ready, 1)

            def rstd_of(c, var_sem, n, pow_sem):
                pool.wait_ge(var_sem, n + 1)
                nc.gpsimd.tensor_tensor(rstd[c][:, :], var[c][:, :], minus_half[:, :], ALU.pow).then_inc(pow_sem, 1)
                pool.wait_ge(pow_sem, n + 1)

            def iteration(base, peeled):
                for k in range(STREAMS):
                    rstd_of(k % 4, it_var, base + k, it_pow)
                    if k >= 4 or not peeled:
                        pool.wait_ge(it_flip, base + (k - 3))
                    nc.gpsimd.tensor_tensor(scaled[k % 4][:, 0:POOL_TILES, :], act_z[k % 4][:, 0:POOL_TILES, :],
                                            wide(rstd[k % 4][:, 0:POOL_TILES]), ALU.mult).then_inc(it_scaled, 1)

            def scatter(g, moves):
                for s, t, k in moves:
                    if t == k == 0:
                        n = g * STREAMS + s
                        pool.wait_ge(slots_ready, n + 1)
                        pool.wait_ge(rows_ready, n + 1)
                        pool.wait_ge(ids_ready, n + 1)
                    nc.gpsimd.indirect_dma_start(
                        out=sorted_rows, in_=rows_a[s][:, t, :], in_offset=None,
                        out_offset=bass.IndirectOffsetOnAxis(ap=slot[:, s, k, t:t + 1].bitcast(U32), axis=0),
                    ).then_inc(scattered[s], 16)

            def moves_of(streams):
                return [(s, t, k) for s in streams for t in range(TILES) for k in range(2)]

            LATE, PER_SLOT = 4, 7
            late = moves_of(range(LATE, STREAMS))

            for g in range(GROUPS):
                for k in range(STREAMS + X1_STATS_LAG):
                    b, d = in_flight(k, X1_STATS_LAG, 0)
                    if d is not None:
                        rstd_of(4 + d % 4, stat_var[0], g * STREAMS + d, stat_pow[0])
                    if g:
                        scatter(g - 1, late[k * PER_SLOT:(k + 1) * PER_SLOT])
                    if b is not None:
                        if g:
                            pool.wait_ge(scattered[b], g * 2 * TILES * 16)
                        if b >= 4:
                            pool.wait_ge(h0_ready, g * STREAMS + b - 3)
                        rstd_of(b % 4, stat_var[1], g * STREAMS + b, stat_pow[1])
                        nc.gpsimd.tensor_tensor(shift[b % 4][:, :], neg_mean[b % 4][:, :], rstd[b % 4][:, :],
                                                ALU.mult).then_inc(shift_ready, 1)
                pool.wait_ge(h0_ready, g * STREAMS + STREAMS)
                q0 = g * STEPS
                iteration(q0, True)
                with pool.Fori(q0 + STREAMS, q0 + STEPS, STREAMS) as q:
                    iteration(q, False)
                for s in range(STREAMS):
                    rstd_of(4 + s % 4, stat_var[2], g * STREAMS + s, stat_pow[2])
                    if s < 4:
                        pool.wait_ge(it_flip, g * STEPS + (STEPS - 3 + s))
                    else:
                        pool.wait_ge(x2_flip, g * STREAMS + s - 3)
                    nc.gpsimd.tensor_tensor(scaled[s % 4][:, :, :], resid[s][:, :, :], wide(rstd[4 + s % 4][:, :]),
                                            ALU.mult).then_inc(x2_scaled, 1)
                for s in range(STREAMS):
                    c, n = s % 4, g * STREAMS + s
                    ex = extra[s % 4]
                    if s >= 4:
                        pool.wait_ge(rows_ready, n - 3)
                    rstd_of(c, r_var, n, r_pow)

                    def small(i, ins):
                        ins.then_inc(r_small, 1)
                        pool.wait_ge(r_small, n * SMALL_STEPS + i)

                    pool.wait_ge(r_var2, n + 1)
                    small(1, nc.gpsimd.tensor_tensor(ex[:, 1, :], ex[:, 0, :], minus_half[:, :], ALU.pow))
                    nc.gpsimd.tensor_tensor(shift[c][:, :], neg_mean[c][:, :], ex[:, 1, :], ALU.mult)
                    small(2, nc.gpsimd.tensor_tensor(ex[:, 2, :], ex[:, 0, :], ex[:, 1, :], ALU.mult))
                    nc.gpsimd.tensor_tensor(std_y[s][:, :], ex[:, 2, :], rstd[c][:, :], ALU.mult).then_inc(r_small, 1)
                    nc.gpsimd.tensor_copy(
                        rows_a[s][:, :, TOKEN:TOKEN + 1].bitcast(I32),
                        ids[:, g * BATCHES + s * TILES:g * BATCHES + (s + 1) * TILES].unsqueeze(2)).then_inc(ids_ready, 1)
                scatter(g, moves_of(range(STREAMS if g == GROUPS - 1 else LATE)))

            def add_rows(j, q, first):
                pool.wait_ge(y_ready, j + (q + 1))
                if not first:
                    pool.wait_ge(y_stored[(q - 1) % 4], j * (4 * SUBS) + (16 * SUBS if q else 0))
                pool.wait_ge(pool_tick, j + (q + 1))
                nc.gpsimd.tensor_tensor(pool_buf[:, :], minus_half[:, 0:1], minus_half[:, 0:1],
                                        ALU.add).then_inc(pool_tick, 1)
                for t in range(SUBS):
                    nc.gpsimd.indirect_dma_start(
                        out=out_rows, in_=y_out[q][:, t, :], in_offset=None,
                        out_offset=bass.IndirectOffsetOnAxis(ap=tokens_out[q][:, t:t + 1].bitcast(U32), axis=0),
                        bounds_check=TOKENS - 1, oob_is_err=False, compute_op=ALU.add).then_inc(y_stored[q], 16)

            for s in range(STREAMS):
                pool.wait_ge(out_done[s], 16 * GROUPS)
            for q in range(4):
                add_rows(0, q, q == 0)
            with pool.Fori(4, SLABS, 4) as j:
                for q in range(4):
                    add_rows(j, q, False)

        @block.vector
        def _(dve):
            chain = [0]

            def link(ins):
                chain[0] += 1
                ins.then_inc(prep_v, 1)
                dve.wait_ge(prep_v, chain[0])

            dve.wait_ge(weights_in, 16 * len(loads))
            dve.wait_ge(consts_ready, 1)
            nc.vector.tensor_scalar(wb_wide[:, :], ones_f[:, :], cols_in[:, 3:4], None, ALU.mult)
            nc.vector.tensor_scalar(lnb_wide[:, :], ones_f[:, :], cols_in[:, 2:3], None, ALU.mult)
            link(nc.vector.tensor_tensor(centred[:, 1, :], wl[:, 1, :], lnw_b[:, :], ALU.mult))
            nc.vector.tensor_reduce(sums[:, 0:1], wl[:, 0, :], AX.X, ALU.add)
            link(nc.vector.tensor_reduce(sums[:, 1:2], centred[:, 1, :], AX.X, ALU.add))
            link(nc.vector.tensor_scalar(sums[:, 2:4], sums[:, 0:2], -1.0 / D, None, ALU.mult))
            nc.vector.tensor_scalar(centred[:, 0, :], wl[:, 0, :], sums[:, 2:3], None, ALU.add)
            link(nc.vector.tensor_scalar(centred[:, 1, :], centred[:, 1, :], sums[:, 3:4], None, ALU.add))
            dve.wait_ge(prep_t, 1)
            nc.vector.tensor_copy(w_gnn0[:, :], ps[0][:, 0, :])
            nc.vector.tensor_copy(w_ffn[:, :], ps[0][:, 1, :])
            nc.vector.tensor_copy(w_ef[:, :], ps[1][:, 0, 0:2])
            nc.vector.tensor_copy(params[:, :, 2 + HC], descend[:, :])
            nc.vector.tensor_copy(params[:, :, 0], ps[1][:, 4, 0:NE])
            nc.vector.tensor_copy(params[:, :, 1], ps[1][:, 4, NE:2 * NE])
            nc.vector.tensor_copy(params[:, :, 2:2 + HC], ps[1][:, 4, 2 * NE:(2 + HC) * NE].rearrange(
                "p (e c) -> p e c", c=HC)).then_inc(params_ready, 1)
            nc.vector.tensor_copy(c_ef[:, 1:2], ps[1][:, 0, 9:10])
            nc.vector.tensor_tensor(c_ef[:, 0:1], ps[1][:, 0, 8:9], ab_b[:, :], ALU.add)
            nc.vector.tensor_tensor(w_mix[:, :, :], wl[:, 2:4, :], ps[2][:, 0:2, :], ALU.subtract)
            link(nc.vector.tensor_copy(w_ffn_plain[:, :], ps[0][:, 2, :]))
            PLAIN_READY = chain[0]
            dve.wait_ge(prep_t, 2)
            link(nc.vector.tensor_copy(crow[:, :, :], bias_rows[:, :, :]))
            link(nc.vector.tensor_tensor(crow[:, 1, :], ps[3][:, 0, :], bias_rows[:, 1, :], ALU.add))
            for part in range(3):
                link(nc.vector.tensor_copy(cpart[:, part, :, :], crow[:, :, :]))
                if part < 2:
                    link(nc.vector.tensor_tensor(crow[:, :, :], crow[:, :, :], cpart[:, part, :, :], ALU.subtract))
            for j in range(3):
                link(nc.vector.memset(bias_mv[j][:, :, :], 0.0))
                for part in range(3):
                    row = slice(32 * part, 32 * part + 1)
                    last = nc.vector.tensor_copy(bias_mv[j][row, :, :],
                                                 cpart[row, part, j, :].unsqueeze(1).to_broadcast([1, 4, P]))
            link(last)

            nc.vector.memset(taken[:, :], 0.0)
            link(nc.vector.memset(taken_bf[:, :], 0.0))
            prep_ready[0] = chain[0]

            def tile_statistics(src, c, tiles=range(TILES)):
                for t in tiles:
                    last = nc.vector.bn_stats(stats[c][:, t, :], src[:, t, :])
                return last

            def half_differences(c, step_sem, n):
                st, sm = stats[c], small[c]
                dve.wait_ge(step_sem, n * 3 + 1)
                nc.vector.tensor_tensor(sm[:, 0, :], st[:, :, 1], st[:, :, 4], ALU.subtract)
                nc.vector.scalar_tensor_tensor(sm[:, 1, :], st[:, :, 2], EPS * D, st[:, :, 5], ALU.add,
                                               ALU.add).then_inc(step_sem, 1)

            def between_halves(c, step_sem, n):
                sm = small[c]
                dve.wait_ge(step_sem, n * 3 + 2)
                nc.vector.scalar_tensor_tensor(sm[:, 2, :], sm[:, 0, :], 0.25, sm[:, 0, :], ALU.mult,
                                               ALU.mult).then_inc(step_sem, 1)

            def variance(c, step_sem, n, var_sem):
                sm = small[c]
                dve.wait_ge(step_sem, n * 3 + 3)
                nc.vector.scalar_tensor_tensor(var[c][:, :], sm[:, 1, :], 1.0 / D, sm[:, 2, :], ALU.mult,
                                               ALU.add).then_inc(var_sem, 1)

            def statistics(src, c, step_sem, n, var_sem, mean_n=None, mean_sem=mean_step):
                tile_statistics(src, c).then_inc(step_sem, 1)
                half_differences(c, step_sem, n)
                if mean_n is not None:
                    nc.vector.tensor_tensor(small[c][:, 3, :], stats[c][:, :, 1], stats[c][:, :, 4],
                                            ALU.add).then_inc(mean_sem, 1)
                between_halves(c, step_sem, n)
                if mean_n is not None:
                    dve.wait_ge(mean_sem, mean_n + 1)
                    nc.vector.tensor_scalar(neg_mean[c][:, :], small[c][:, 3, :], -0.5, None, ALU.mult)
                variance(c, step_sem, n, var_sem)

            def over_e(v):
                return v.unsqueeze(2).to_broadcast([P, TILES, NE])

            def over_t(v):
                return v.unsqueeze(1).to_broadcast([P, TILES, NE])

            def linker(step_sem, first):
                at = [0]

                def linked(ins):
                    at[0] += 1
                    ins.then_inc(step_sem, 1)
                    dve.wait_ge(step_sem, first + at[0])
                return linked, at

            def route_a(s, n):
                c = s % 4
                linked, at = linker(a_step, n * A_STEPS)
                dve.wait_ge(logit_psum, n + 1)
                dve.wait_ge(r_small, n * SMALL_STEPS + SMALL_STEPS)
                linked(nc.vector.tensor_tensor(logits[c][:, :, :], ps[c][:, 0, 0:TILES * NE].rearrange(
                    "p (t e) -> p t e", e=NE), over_e(std_y[s][:, :]), ALU.mult))
                linked(nc.vector.tensor_tensor(logits[c][:, :, :], logits[c][:, :, :], over_t(br_b[:, :]), ALU.add))
                linked(nc.vector.tensor_reduce(edge[c][:, 0, :], logits[c][:, :, :], AX.X, ALU.max))
                assert at[0] == A_STEPS
                nc.vector.tensor_tensor(logits[c][:, :, :], logits[c][:, :, :], over_e(edge[c][:, 0, :]),
                                        ALU.subtract).then_inc(centred_logits, 1)

            def route_b(s, n):
                c = s % 4
                pr, ed, cd, ht = probs[c][:, :, :], edge[c], cand[s % 2][:, :, :], hot[c]
                linked, at = linker(b_step, n * B_STEPS)
                dve.wait_ge(exps, n + 1)
                linked(nc.vector.tensor_reduce(ed[:, 1, :], pr, AX.X, ALU.add))
                linked(nc.vector.reciprocal(ed[:, 2, :], ed[:, 1, :]))
                linked(nc.vector.tensor_tensor(pr, pr, over_e(ed[:, 2, :]), ALU.mult))
                for k in range(2):
                    linked(nc.vector.tensor_reduce(ed[:, 3 + k, :], pr, AX.X, ALU.max))
                    linked(nc.vector.tensor_tensor(cd, pr, over_e(ed[:, 3 + k, :]), ALU.is_ge))
                    linked(nc.vector.tensor_tensor(cd, cd, over_t(descend[:, :]), ALU.mult))
                    linked(nc.vector.tensor_reduce(ed[:, 5 + k, :], cd, AX.X, ALU.max))
                    if k == 1:
                        nc.vector.tensor_tensor(ed[:, 7, :], ed[:, 3, :], ed[:, 4, :], ALU.add)
                    linked(nc.vector.tensor_tensor(ht[:, k, :, :], over_t(descend[:, :]), over_e(ed[:, 5 + k, :]),
                                                   ALU.is_equal))
                    if k == 0:
                        linked(nc.vector.scalar_tensor_tensor(pr, ht[:, 0, :, :], -4.0, pr, ALU.mult, ALU.add))
                nc.vector.tensor_tensor(chosen[c][:, :, :], ht[:, 0, :, :], ht[:, 1, :, :], ALU.add)
                linked(nc.vector.reciprocal(ed[:, 1, :], ed[:, 7, :]))
                assert at[0] == B_STEPS
                nc.vector.tensor_copy(rows_a[s][:, :, FIRST], ed[:, 5, :])
                for k in range(2):
                    nc.vector.tensor_tensor(rows_a[s][:, :, WEIGHT + k], ed[:, 3 + k, :], ed[:, 1, :], ALU.mult)
                nc.vector.tensor_reduce(taken_new[s % 2][:, :], chosen[c][:, :, :].rearrange("p t e -> p e t"), AX.X,
                                        ALU.add).then_inc(chosen_ready, 1)

            def route_c(s, n):
                c = s % 4
                linked, at = linker(c_step, n * C_STEPS)
                dve.wait_ge(rank_psum, n + 1)
                nc.vector.tensor_tensor(taken[:, :], taken[:, :], taken_new[s % 2][:, :], ALU.add)
                linked(nc.vector.tensor_tensor(logits[c][:, :, :], ps[c][:, 4, 0:TILES * NE].rearrange(
                    "p (t e) -> p t e", e=NE), over_t(region_0[:, :]), ALU.add))
                nc.vector.tensor_copy(taken_bf[:, :], taken[:, :])
                linked(nc.vector.tensor_tensor(hot[c][:, :, :, :], hot[c][:, :, :, :], logits[c][:, :, :].unsqueeze(1)
                                               .to_broadcast([P, 2, TILES, NE]), ALU.mult))
                linked(nc.vector.tensor_reduce(rank[c][:, :, :], hot[c][:, :, :, :], AX.X, ALU.add))
                assert at[0] == C_STEPS
                nc.vector.tensor_copy(slot[:, s, :, :], rank[c][:, :, :]).then_inc(slots_ready, 1)

            with dve.Fori(0, GROUPS) as g:
                nc.vector.memset(tick[:, :], 0.0).then_inc(group_open, 1)
                for k in range(STREAMS + X1_STATS_LAG):
                    a, b, d, e = in_flight(k, H_LAG, NUM_LAG, 0, X1_STATS_LAG)
                    if b is not None:
                        c, n = b % 4, g * STREAMS + b
                        dve.wait_ge(den_psum, n + 1)
                        nc.vector.tensor_tensor(soft[c][:, 0, :], ps[c][:, 0, 0:TILES], soft_e[c][:, :],
                                                ALU.mult).then_inc(soft_step, 1)
                        dve.wait_ge(soft_step, n * 2 + 1)
                        nc.vector.reciprocal(soft[c][:, 1, :], soft[c][:, 0, :]).then_inc(soft_step, 1)
                        dve.wait_ge(soft_step, n * 2 + 2)
                        nc.vector.tensor_tensor(soft[c][:, 2, :], soft[c][:, 1, :], soft_e[c][:, :],
                                                ALU.mult).then_inc(ratio_ready, 1)
                    if d is not None:
                        dve.wait_ge(x_in[d], g * 16 + 16)
                        statistics(resid[d], 4 + d % 4, stat_step[0], g * STREAMS + d, stat_var[0])
                    if a is not None:
                        c, n = a % 4, g * STREAMS + a
                        dve.wait_ge(h_psum, n + 1)
                        nc.vector.tensor_tensor(work[c][:, :, :], ps[c][:, :, :], wide(soft_f[c][:, :]),
                                                ALU.mult).then_inc(src_ready, 1)
                    if e is not None:
                        dve.wait_ge(x1_ready, g * STREAMS + e + 1)
                        statistics(resid[e], e % 4, stat_step[1], g * STREAMS + e, stat_var[1], g * STREAMS + e)
                    if b is not None:
                        c, n = b % 4, g * STREAMS + b
                        dve.wait_ge(num_psum, n + 1)
                        dve.wait_ge(ratio_ready, n + 1)
                        for t in range(TILES):
                            last = nc.vector.scalar_tensor_tensor(resid[b][:, t, :], ps[c][:, t, :],
                                                                  soft[c][:, 2, t:t + 1], resid[b][:, t, :],
                                                                  ALU.mult, ALU.add)
                        last.then_inc(x1_ready, 1)

                def iteration(base, peeled=False, tail=False):
                    for k in range(STREAMS):
                        (n, s), (o, w), (m, r) = stages([STATS_LAG, STATS_LAG + 1, SCALE_LAG], k, base, peeled, tail)
                        if n is not None:
                            dve.wait_ge(silu_done, n + 1)
                            tile_statistics(act_z[s % 4], s % 4, range(TILES // 2))
                        if o is not None:
                            between_halves(w % 4, it_step, o)
                        if n is not None:
                            tile_statistics(act_z[s % 4], s % 4, range(TILES // 2, TILES)).then_inc(it_step, 1)
                        if o is not None:
                            variance(w % 4, it_step, o, it_var)
                        if m is not None and VECTOR_TILES:
                            dve.wait_ge(it_pow, m + 1)
                            for t in range(POOL_TILES, POOL_TILES + VECTOR_TILES):
                                last = nc.vector.tensor_scalar(scaled[r % 4][:, t, :], act_z[r % 4][:, t, :],
                                                               rstd[r % 4][:, t:t + 1], None, ALU.mult)
                            last.then_inc(it_scaled_v, 1)
                        if tail:
                            dve.wait_ge(product, base + (k - STREAMS + 1))
                            nc.vector.tensor_tensor(resid[k][:, :, :], ps[k % 4][:, :, :], resid[k][:, :, :],
                                                    ALU.add).then_inc(x2_ready, 1)
                        else:
                            h = start_h[k] if peeled else ps[k % 4][:, :, :]
                            dve.wait_ge(tanh_done, base + (k + 1))
                            nc.vector.scalar_tensor_tensor(work[k % 4][:, :, :], work[k % 4][:, :, :], 0.01,
                                                           h, ALU.mult, ALU.add).then_inc(state_read, 1)
                        if n is not None:
                            half_differences(s % 4, it_step, n)
                        if tail:
                            dve.wait_ge(x2_ready, g * STREAMS + k + 1)
                            if k >= 4:
                                dve.wait_ge(stat_pow[2], g * STREAMS + k - 3)
                            statistics(resid[k], 4 + k % 4, stat_step[2], g * STREAMS + k, stat_var[2])

                q0 = g * STEPS
                iteration(q0, peeled=True)
                with dve.Fori(q0 + STREAMS, q0 + STEPS, STREAMS) as q:
                    iteration(q)
                iteration(g * STEPS + STEPS, tail=True)
                for k in range(STREAMS + RANK_R):
                    s, a, b, d = in_flight(k, MIX_LAG, LOGIT_R, CHOICE_R, RANK_R)
                    if s is not None:
                        dve.wait_ge(mix_psum, g * STREAMS + s + 1)
                        nc.vector.scalar_tensor_tensor(resid[s][:, :, :], ps[s % 4][:, :, :], 0.0, resid[s][:, :, :],
                                                       ALU.max, ALU.add).then_inc(x3_ready, 1)
                        n = g * STREAMS + s
                        dve.wait_ge(x3_ready, n + 1)
                        if s >= 4:
                            dve.wait_ge(r_small, (n - 3) * SMALL_STEPS)
                        statistics(resid[s], s % 4, r_stat, n, r_var, n, r_mean)
                        dve.wait_ge(r_var, n + 1)
                        nc.vector.tensor_scalar(extra[s % 4][:, 0, :], var[s % 4][:, :], 1.0 + EPS, -EPS, ALU.mult,
                                                ALU.add).then_inc(r_var2, 1)
                    if b is not None:
                        route_b(b, g * STREAMS + b)
                    if a is not None:
                        route_a(a, g * STREAMS + a)
                    if d is not None:
                        route_c(d, g * STREAMS + d)

            def table(ins):
                table_at[0] += 1
                ins.then_inc(table_step, 1)
                dve.wait_ge(table_step, table_at[0])

            table_at = [0]
            dve.wait_ge(total_psum, 1)
            table(nc.vector.tensor_copy(count_f[:, :], ps[0][:, 0, 0:NE]))
            shape = [P, NE, TOKENS // SLAB]
            table(nc.vector.tensor_tensor(below, slab_rows[:, :].unsqueeze(1).to_broadcast(shape),
                                          count_f[:, :].unsqueeze(2).to_broadcast(shape), ALU.is_lt))
            nc.vector.tensor_tensor(pad_f[:, :], count_f[:, :], region_0[:, :], ALU.add)
            table(nc.vector.tensor_reduce(slabs_f[:, :], below, AX.X, ALU.add))
            nc.vector.tensor_copy(pad_row[:, :], pad_f[:, :])
            table(nc.vector.tensor_copy(slab_end[:, 0:1], slabs_f[:, 0:1]))
            for e in range(1, NE):
                table(nc.vector.tensor_tensor(slab_end[:, e:e + 1], slab_end[:, e - 1:e], slabs_f[:, e:e + 1], ALU.add))
            shape = [P, SLABS, NE]
            table(nc.vector.tensor_tensor(past, slab_j[:, :].unsqueeze(2).to_broadcast(shape),
                                          slab_end[:, :].unsqueeze(1).to_broadcast(shape), ALU.is_ge))
            nc.vector.tensor_reduce(slab_e[:, :], past, AX.X, ALU.add)
            table(nc.vector.tensor_tensor(before, past, slabs_f[:, :].unsqueeze(1).to_broadcast(shape), ALU.mult))
            table(nc.vector.tensor_reduce(slab_0[:, :], before, AX.X, ALU.add))
            table(nc.vector.tensor_tensor(slab_0[:, :], slab_j[:, :], slab_0[:, :], ALU.subtract))
            table(nc.vector.tensor_scalar(slab_0[:, :], slab_0[:, :], float(SLAB), None, ALU.mult))
            table(nc.vector.scalar_tensor_tensor(slab_0[:, :], slab_e[:, :], float(REGION), slab_0[:, :], ALU.mult,
                                                 ALU.add))
            nc.vector.tensor_scalar(slab_row[:, :], slab_0[:, :], float(NE * REGION), None, ALU.min)
            nc.vector.tensor_scalar(slab_exp[:, :], slab_e[:, :], float(NE - 1), None,
                                    ALU.min).then_inc(tables_ready, 1)

            def turn(j_parts, q, b):
                dve.wait_ge(slab_flip, j_parts + 1)
                nc.vector.tensor_scalar(rows_T[b], psX[b], params_in[q][:, 0:1], params_in[q][:, 1:2], ALU.mult,
                                        ALU.add).then_inc(slab_turned, 1)
                row_weights(j_parts, q)

            def expert(j, peeled=False, second=False, end=False):
                for q in range(4):
                    n = j + q
                    if not (end and q == 3):
                        turn(n + 1, (q + 1) % 4, (q + 1) % 2)
                    if q or not peeled:
                        join_bias(j + (q - 1), j if q else j - 4, (q - 1) % 4, peeled or second and q == 0)

            def row_weights(n, q):
                first, expert_of = rows_in[q][:, :, FIRST], params_in[q][:, 2 + HC:3 + HC]
                nc.vector.scalar_tensor_tensor(slab_w[q][:, 0, :], first, expert_of, rows_in[q][:, :, WEIGHT],
                                               ALU.is_equal, ALU.mult)
                nc.vector.scalar_tensor_tensor(slab_w[q][:, 1, :], first, expert_of, rows_in[q][:, :, WEIGHT + 1],
                                               ALU.not_equal, ALU.mult).then_inc(weight_step, 1)

            def join_bias(n, j, q, peeled):
                dve.wait_ge(weight_step, n + 1)
                nc.vector.tensor_tensor(slab_w[q][:, 2, :], slab_w[q][:, 0, :], slab_w[q][:, 1, :],
                                        ALU.add)
                dve.wait_ge(y_psum, n + 1)
                if not peeled:
                    dve.wait_ge(y_stored[q], j * (4 * SUBS))
                nc.vector.tensor_copy(tokens_out[q][:, :], rows_in[q][:, :, TOKEN].bitcast(I32))
                nc.vector.tensor_tensor(y_out[q], psY[q % 2], b2_in[q].unsqueeze(1).to_broadcast([P, SUBS, D]),
                                        ALU.add).then_inc(y_biased, 1)
                dve.wait_ge(y_biased, n + 1)
                nc.vector.tensor_tensor(y_out[q], y_out[q], slab_w[q][:, 2, :].unsqueeze(2).to_broadcast(
                    [P, SUBS, D]), ALU.mult).then_inc(y_ready, 1)

            turn(0, 0, 0)
            expert(0, peeled=True)
            expert(4, second=True)
            with dve.Fori(8, SLABS - 4, 4) as j:
                expert(j)
            expert(SLABS - 4, end=True)
            join_bias(SLABS - 1, SLABS - 4, 3, False)

        @block.scalar
        def _(act):
            with act.Fori(0, GROUPS) as g:
                for k in range(STREAMS + H0_LAG):
                    a, b, d, e = in_flight(k, ADJ_LAG, TURN_LAG, H0_LAG, X_LAG)
                    if e is not None:
                        act.wait_ge(stat_pow[0], g * STREAMS + e + 1)
                        if e >= 4:
                            act.wait_ge(x_flip, g * STREAMS + e - 3)
                        for t in range(TILES):
                            last = nc.scalar.mul(scaled[e % 4][:, t, :], resid[e][:, t, :],
                                                 rstd[4 + e % 4][:, t:t + 1])
                        last.then_inc(x_scaled, 1)
                    if b is not None:
                        c, n = b % 4, g * STREAMS + b
                        act.wait_ge(x_flip, n + 1)
                        nc.scalar.copy(turned[c][:, :, :], ps[c][:, :, :]).then_inc(x_turned, 1)
                    if d is not None:
                        act.wait_ge(shift_ready, g * STREAMS + d + 1)
                        for t in range(TILES):
                            last = nc.scalar.activation(start_h[d][:, t, :], resid[d][:, t, :], ACT.Identity,
                                                        bias=shift[d % 4][:, t:t + 1], scale=rstd[d % 4][:, t:t + 1])
                        last.then_inc(h0_ready, 1)
                    if a is not None:
                        act.wait_ge(adj_psum, g * STREAMS + a + 1)
                        nc.scalar.copy(adjT[a][:, :, :], ps[a % 4][:, :, :]).then_inc(adjT_ready, 1)
                    if b is not None:
                        act.wait_ge(ef_psum, n + 1)
                        ef = ps[c][:, 0, 0:2 * TILES].rearrange("p (t k) -> p t k", k=2)
                        nc.scalar.activation(soft_f[c][:, :], ef[:, :, 1], ACT.Exp, bias=c_ef[:, 1:2])
                        nc.scalar.activation(soft_e[c][:, :], ef[:, :, 0], ACT.Exp,
                                             bias=c_ef[:, 0:1]).then_inc(soft_e_ready, 1)

                def iteration(base, peeled=False, tail=False):
                    for k in range(EVAC_LAG if tail else STREAMS):
                        (n, s), (m, r), (l, v) = stages([EVAC_LAG, SCALE_LAG, SILU_LAG], k, base, peeled, tail)
                        if n is not None:
                            act.wait_ge(it_flip, n + 1)
                            nc.scalar.copy(turned[s % 4][:, :, :], ps[s % 4][:, :, :]).then_inc(it_turned, 1)
                        if not tail:
                            if peeled:
                                h = start_h[k]
                            else:
                                h = ps[k % 4][:, :, :]
                                act.wait_ge(product, base + (k - STREAMS + 1))
                            nc.scalar.activation(work[k % 4][:, :, :], h, ACT.Tanh).then_inc(tanh_done, 1)
                        if m is not None:
                            act.wait_ge(it_pow, m + 1)
                            for t in range(POOL_TILES + VECTOR_TILES, TILES):
                                last = nc.scalar.mul(scaled[r % 4][:, t, :], act_z[r % 4][:, t, :],
                                                     rstd[r % 4][:, t:t + 1])
                            last.then_inc(it_scaled_a, 1)
                        if l is not None:
                            act.wait_ge(state_read, l + 1)
                            if not (peeled and v < 4):
                                act.wait_ge(it_scaled, l - 3)
                                if VECTOR_TILES:
                                    act.wait_ge(it_scaled_v, l - 3)
                                act.wait_ge(it_scaled_a, l - 3)
                            nc.scalar.activation(act_z[v % 4][:, :, :], work[v % 4][:, :, :],
                                                 ACT.Silu).then_inc(silu_done, 1)

                nc.scalar.activation(act_tick[:, :], minus_half[:, 0:1], ACT.Silu)
                act.wait_ge(h0_ready, g * STREAMS + STREAMS)
                q0 = g * STEPS
                iteration(q0, peeled=True)
                with act.Fori(q0 + STREAMS, q0 + STEPS, STREAMS) as q:
                    iteration(q)
                iteration(g * STEPS + STEPS, tail=True)
                act.wait_ge(product, g * STEPS + STEPS)
                for k in range(STREAMS + CHOICE_R):
                    b, d = in_flight(k, FLIP_R, CHOICE_R)
                    if d is not None:
                        act.wait_ge(centred_logits, g * STREAMS + d + 1)
                        nc.scalar.activation(probs[d % 4][:, :, :], logits[d % 4][:, :, :], ACT.Exp).then_inc(exps, 1)
                    if b is not None:
                        act.wait_ge(r_flip, g * STREAMS + b + 1)
                        nc.scalar.copy(turned[b % 4][:, :, :], ps[b % 4][:, :, :]).then_inc(r_turned, 1)
                    a, b, d = in_flight(k, 0, Q_LAG, ROWS_LAG)
                    if a is not None:
                        act.wait_ge(x2_flip, g * STREAMS + a + 1)
                        if a >= 4:
                            act.wait_ge(mix_psum, g * STREAMS + a - 3)
                        nc.scalar.copy(turned[a % 4][:, :, :], ps[a % 4][:, :, :]).then_inc(x2_turned, 1)
                    if b is not None:
                        act.wait_ge(q_psum, g * STREAMS + b + 1)
                        nc.scalar.copy(act_z[b % 4][:, :, :], ps[b % 4][:, :, :]).then_inc(q_copied, 1)
                    if d is not None:
                        act.wait_ge(r_small, (g * STREAMS + d) * SMALL_STEPS + SMALL_STEPS)
                        for t in range(TILES):
                            last = nc.scalar.activation(rows_a[d][:, t, 0:D], resid[d][:, t, :], ACT.Identity,
                                                        bias=shift[d % 4][:, t:t + 1],
                                                        scale=extra[d % 4][:, 1, t:t + 1])
                        last.then_inc(rows_ready, 1)

            def gelus(n, q, b):
                for c in range(HC):
                    act.wait_ge(hidden_psum, n * HC + (c + 1))
                    nc.scalar.activation(hidden[b][c], psH[c], ACT.Gelu,
                                         bias=params_in[q][:, 2 + c:3 + c]).then_inc(hidden_ready, 1)

            with act.Fori(0, SLABS, 4) as j:
                for q in range(4):
                    gelus(j + q, q, q % 2)

        @block.tensor
        def _(pe):
            pe.wait_ge(consts_ready, 1)
            pe.wait_ge(prep_v, 4)
            nc.tensor.transpose(ps[0][:, 0, :], centred[:, 0, :], ident[:, :])
            nc.tensor.transpose(ps[0][:, 1, :], centred[:, 1, :], ident[:, :])
            nc.tensor.transpose(ps[0][:, 2, :], wl[:, 1, :], ident[:, :])
            nc.tensor.transpose(ps[1][:, 4, 0:(2 + HC) * NE], params_rows[:, :],
                                ident[0:(2 + HC) * NE, 0:(2 + HC) * NE])
            nc.tensor.matmul(ps[1][:, 0, 0:2], centred[:, 0, :], cols_in[:, 0:2], start=True, stop=True)
            nc.tensor.matmul(ps[1][:, 0, 8:10], wb_wide[:, :], cols_in[:, 0:2], start=True, stop=True)
            nc.tensor.matmul(ps[2][:, 0:2, :], mean_mat[:, :], wl[:, 2:4, :], start=True,
                             stop=True).then_inc(prep_t, 1)
            pe.wait_ge(prep_v, 5)
            nc.tensor.matmul(ps[3][:, 0, :], lnb_wide[:, :], w_ffn_plain[:, :], start=True,
                             stop=True).then_inc(prep_t, 1)
            pe.wait_ge(prep_v, prep_ready[0])

            def flip(c, src):
                for t in range(TILES):
                    last = nc.tensor.transpose(ps[c][:, t, :], src[:, t, :], ident[:, :])
                return last

            def rows(c, terms, bias=None):
                for bank in range(2):
                    if bias is not None:
                        nc.tensor.matmul(ps[c][:, 4 * bank:4 * bank + 4, :], ones_bf[:, :], bias_mv[bias][:, :, :],
                                         start=True, stop=False, skip_group_check=True)
                    for t in range(4 * bank, 4 * bank + 4):
                        for m, (stationary, moving) in enumerate(terms):
                            last = nc.tensor.matmul(ps[c][:, t, :], stationary[:, t, :], moving(t),
                                                    start=bias is None and m == 0, stop=m == len(terms) - 1,
                                                    skip_group_check=True)
                return last

            with pe.Fori(0, GROUPS) as g:
                pe.wait_ge(group_open, g + 1)
                for k in range(ADJ_LAG, STREAMS + NUM_LAG):
                    a, b, d, e = in_flight(k, ADJ_LAG, TURN_LAG, NUM_LAG, H_LAG)
                    if d is not None:
                        pe.wait_ge(src_ready, g * STREAMS + d + 1)
                        for t in range(TILES):
                            last = nc.tensor.matmul(ps[d % 4][:, 0, t:t + 1], adjT[d][:, t, :],
                                                    soft_f[d % 4][:, t:t + 1], start=True, stop=True)
                        last.then_inc(den_psum, 1)
                    if b is not None:
                        pe.wait_ge(adjT_ready, g * STREAMS + b + 1)
                        pe.wait_ge(x_scaled, g * STREAMS + b + 1)
                        flip(b % 4, scaled[b % 4]).then_inc(x_flip, 1)
                    if e is not None:
                        pe.wait_ge(soft_e_ready, g * STREAMS + e + 1)
                        rows(e % 4, [(turned[e % 4], lambda t: w_gnn0[:, :])], bias=0).then_inc(h_psum, 1)
                    if a is not None:
                        pe.wait_ge(adj_in[a % 2], g * (16 * STREAMS // 2) + 16 * (a // 2 + 1))
                        if a >= 4:
                            pe.wait_ge(x1_ready, g * STREAMS + a - 3)
                        flip(a % 4, raw[a % 2]).then_inc(adj_psum, 1)
                    if d is not None:
                        pe.wait_ge(ratio_ready, g * STREAMS + d + 1)
                        rows(d % 4, [(adjT[d], lambda t, c=d % 4: work[c][:, t, :])]).then_inc(num_psum, 1)
                    if b is not None:
                        c = b % 4
                        pe.wait_ge(x_turned, g * STREAMS + b + 1)
                        for t in range(TILES):
                            last = nc.tensor.matmul(ps[c][:, 0, 2 * t:2 * t + 2], turned[c][:, t, :], w_ef[:, :],
                                                    start=True, stop=True)
                        last.then_inc(ef_psum, 1)

                def flip_step(n, s, peeled, last_iteration, first):
                    pe.wait_ge(it_scaled, n + 1)
                    if VECTOR_TILES:
                        pe.wait_ge(it_scaled_v, n + 1)
                    pe.wait_ge(it_scaled_a, n + 1)
                    if last_iteration and s >= 4:
                        pe.wait_ge(x2_ready, g * STREAMS + s - 3)
                    else:
                        pe.wait_ge(state_read, n + 5)
                    flip(s % 4, scaled[s % 4]).then_inc(it_flip, 1)

                def product_step(n, s):
                    pe.wait_ge(it_turned, n + 1)
                    rows(s % 4, [(turned[s % 4], lambda t: w_ffn[:, :])], bias=1).then_inc(product, 1)

                def iteration(base, peeled=False, tail=False):
                    for k in range(STREAMS):
                        for n, s in stages([FLIP_LAG], k, base, peeled, tail):
                            if n is not None:
                                flip_step(n, s, peeled, tail, False)
                        for n, s in stages([EVAC_LAG], k, base, peeled, tail):
                            if n is not None:
                                product_step(n, s)

                pe.wait_ge(x1_ready, g * STREAMS + STREAMS)
                q0 = g * STEPS
                iteration(q0, peeled=True)
                with pe.Fori(q0 + STREAMS, q0 + STEPS, STREAMS) as q:
                    iteration(q)
                iteration(g * STEPS + STEPS, tail=True)
                for k in range(STREAMS + RANK_R):
                    a, b, d = in_flight(k, 0, Q_LAG, MIX_LAG)
                    if a is not None:
                        pe.wait_ge(x2_scaled, g * STREAMS + a + 1)
                        if a < 4:
                            pe.wait_ge(x2_ready, g * STREAMS + a + 5)
                        else:
                            pe.wait_ge(x3_ready, g * STREAMS + a - 3)
                        flip(a % 4, scaled[a % 4]).then_inc(x2_flip, 1)
                    if b is not None:
                        pe.wait_ge(x2_turned, g * STREAMS + b + 1)
                        rows(b % 4, [(turned[b % 4], lambda t: w_mix[:, 1, :])]).then_inc(q_psum, 1)
                    if d is not None:
                        pe.wait_ge(q_copied, g * STREAMS + d + 1)
                        rows(d % 4, [(turned[d % 4], lambda t: w_mix[:, 0, :]),
                                     (adjT[d], lambda t, c=d % 4: act_z[c][:, t, :])], bias=2).then_inc(mix_psum, 1)
                    a, b, d = in_flight(k, FLIP_R, LOGIT_R, RANK_R)
                    if b is not None:
                        c, n = b % 4, g * STREAMS + b
                        pe.wait_ge(r_turned, n + 1)
                        for t in range(TILES):
                            last = nc.tensor.matmul(ps[c][:, 0, t * NE:(t + 1) * NE], turned[c][:, t, :], wr[:, :],
                                                    start=True, stop=True)
                        last.then_inc(logit_psum, 1)
                    if a is not None:
                        c, n = a % 4, g * STREAMS + a
                        pe.wait_ge(rows_ready, n + 1)
                        if a < 4:
                            pe.wait_ge(x3_ready, g * STREAMS + a + 5)
                        else:
                            pe.wait_ge(slots_ready, n - 3)
                        flip(c, start_h[a]).then_inc(r_flip, 1)
                    if d is not None:
                        c, n = d % 4, g * STREAMS + d
                        pe.wait_ge(chosen_ready, n + 1)
                        if d:
                            pe.wait_ge(slots_ready, n)
                        ranks = ps[c][:, 4, 0:TILES * NE].rearrange("p (t e) -> p t e", e=NE)
                        nc.tensor.matmul(ranks, tri[:, :], chosen[c][:, :, :], start=True, stop=False,
                                         skip_group_check=True)
                        for t in range(TILES - 1):
                            rest = TILES - 1 - t
                            nc.tensor.matmul(ranks[:, t + 1:TILES, :], ones_bf[:, :],
                                             chosen[c][:, t, :].unsqueeze(1).to_broadcast([P, rest, NE]),
                                             start=False, stop=False, skip_group_check=True)
                        nc.tensor.matmul(ranks, ones_bf[:, :],
                                         taken_bf[:, :].unsqueeze(1).to_broadcast([P, TILES, NE]),
                                         start=False, stop=True, skip_group_check=True).then_inc(rank_psum, 1)

            pe.wait_ge(slots_ready, GROUPS * STREAMS)
            nc.tensor.matmul(ps[0][:, 0, 0:NE], ones_bf[:, :], taken_bf[:, :], start=True,
                             stop=True).then_inc(total_psum, 1)
            pe.wait_ge(tables_ready, 1)

            def turn(j, q, b):
                pe.wait_ge(slab_in[q], j * (4 * SLAB_LOADS) + 16 * SLAB_LOADS)
                for t in range(SUBS):
                    last = nc.tensor.transpose(psX[b][:, t * P:(t + 1) * P], rows_in[q][:, t, 0:D], ident[:, :])
                last.then_inc(slab_flip, 1)

            def first_product(n, q, b, peeled):
                pe.wait_ge(slab_turned, n + 1)
                for c in range(HC):
                    if not peeled:
                        pe.wait_ge(hidden_ready, (n - 1) * HC + (c + 1))
                    nc.tensor.matmul(psH[c], w1_in[q][:, c * P:(c + 1) * P], rows_T[b], start=True,
                                     stop=True).then_inc(hidden_psum, 1)

            def second_product(n, q, b, peeled):
                pe.wait_ge(hidden_ready, n * HC + HC)
                if not peeled:
                    pe.wait_ge(y_ready, n - 1)
                for t in range(SUBS):
                    for c in range(HC):
                        last = nc.tensor.matmul(psY[b][:, t, :], hidden[b][c][:, t * P:(t + 1) * P],
                                                w2_in[q][:, c, :], start=c == 0, stop=c == HC - 1,
                                                skip_group_check=True)
                last.then_inc(y_psum, 1)

            def expert(j, first=False, end=False):
                for q in range(4):
                    n = j + q
                    first_product(n, q, q % 2, first and q == 0)
                    if not (end and q == 3):
                        turn(j if q < 3 else j + 4, (q + 1) % 4, (q + 1) % 2)
                    if not (first and q == 0):
                        second_product(j + (q - 1), (q - 1) % 4, (q - 1) % 2, first and q < 3)

            turn(0, 0, 0)
            expert(0, first=True)
            with pe.Fori(4, SLABS - 4, 4) as j:
                expert(j)
            expert(SLABS - 4, end=True)
            second_product(SLABS - 1, 3, 1, False)


_INS = ["x", "adj", "L0_gnn_W_w", "L0_gnn_W_b", "L0_gnn_a_w", "L0_gnn_a_b", "L0_ffn_ln_w", "L0_ffn_ln_b",
        "L0_ffn_W", "L0_ffn_b", "L1_gnn_weight", "L1_gnn_bias", "L1_ffn_Wr", "L1_ffn_br", "L1_ffn_ln_g", "L1_ffn_ln_b", "L1_ffn_W1",
        "L1_ffn_b1", "L1_ffn_W2", "L1_ffn_b2"]
_OUTS = [((128, 128, 128), "float32")]


def kernel(**inputs):
    import numpy as _np
    import concourse.bacc as _bacc
    from concourse import mybir as _mybir
    from concourse.bass_utils import run_bass_kernel_spmd as _run

    nc = _bacc.Bacc("TRN2", target_bir_lowering=False, num_devices=1)
    arrays, args = {}, []
    for name in _INS:
        a = _np.ascontiguousarray(inputs[name])
        arrays[f"in_{name}_dram"] = a
        args.append(nc.dram_tensor(f"in_{name}_dram", a.shape, _mybir.dt.from_np(a.dtype), kind="ExternalInput").ap())
    for i, (shape, dtype) in enumerate(_OUTS):
        dt = _mybir.dt.from_np(_np.dtype(dtype))
        args.append(nc.dram_tensor(f"out_{i}_dram", shape, dt, kind="ExternalOutput").ap())
    network(nc, *args)
    r = _run(nc, [arrays], core_ids=[0])
    got = tuple(r.results[0][f"out_{i}_dram"] for i in range(len(_OUTS)))
    return got[0]
```

```python
from contextlib import ExitStack

import concourse.bass as bass
from concourse import mybir

F32 = mybir.dt.float32
BF16 = mybir.dt.bfloat16
I32 = mybir.dt.int32
U32 = mybir.dt.uint32
F32R = mybir.dt.float32r
ALU = mybir.AluOpType
ACT = mybir.ActivationFunctionType
AX = mybir.AxisListType

P = 128
EPS = 1e-5


def network(nc, x, adj, W_w, W_b, a_w, a_b, ln_w, ln_b, F_W, F_b, G_w, G_b,
            R_w, R_b, E_g, E_b, E_W1, E_b1, E_W2, E_b2, out):
    B, N, D = x.shape
    assert N == P and D == P
    TILES = 8
    STREAMS = 8
    BANKS = 4
    ITERS = 30
    GROUPS = B // (TILES * STREAMS)
    STEPS = STREAMS * ITERS
    NE = R_w.shape[1]
    H = E_W1.shape[2]
    HC = H // P
    TOKENS = B * N
    SLAB = 512
    SUBS = SLAB // P
    TOKEN, FIRST, WEIGHT = D, D + 1, D + 2
    ROW = D + 4
    REGION = TOKENS + SLAB
    SLABS = (2 * TOKENS + NE * (SLAB - 1)) // SLAB
    SLABS += -SLABS % 4
    FAR = 1 << 20
    BATCHES = TILES * STREAMS

    with ExitStack() as ctx:
        def sb(name, shape, dt=F32):
            return ctx.enter_context(nc.sbuf_tensor(name, shape, dt))

        def sem(name):
            return ctx.enter_context(nc.semaphore(name))

        ps = [ctx.enter_context(nc.psum_tensor(f"ps{j}", [P, TILES, D], F32)) for j in range(BANKS)]

        resid = [sb(f"resid{s}", [P, TILES, D]) for s in range(STREAMS)]
        adjT = [sb(f"adjT{s}", [P, TILES, N]) for s in range(STREAMS)]
        rows_a = [sb(f"start_h{s}", [P, TILES, ROW]) for s in range(STREAMS)]
        start_h = [t[:, :, 0:D] for t in rows_a]
        work = [sb(f"work{j}", [P, TILES, D]) for j in range(4)]
        act_z = [sb(f"act_z{j}", [P, TILES, D]) for j in range(4)]
        scaled = [sb(f"scaled{j}", [P, TILES, D]) for j in range(4)]
        turned = [sb(f"turned{j}", [P, TILES, D]) for j in range(4)]
        stats = [sb(f"stats{j}", [P, TILES, 6]) for j in range(8)]
        small = [sb(f"small{j}", [P, 5, TILES]) for j in range(8)]
        var = [sb(f"var{j}", [P, TILES]) for j in range(8)]
        rstd = [sb(f"rstd{j}", [P, TILES]) for j in range(8)]
        neg_mean = [sb(f"neg_mean{j}", [P, TILES]) for j in range(4)]
        shift = [sb(f"shift{j}", [P, TILES]) for j in range(4)]
        soft_f = [sb(f"soft_f{j}", [P, TILES]) for j in range(4)]
        soft_e = [sb(f"soft_e{j}", [P, TILES]) for j in range(4)]
        soft = [sb(f"soft{j}", [P, 3, TILES]) for j in range(4)]
        minus_half = sb("minus_half", [P, TILES])
        tick = sb("tick", [P, 1])
        tokens_out = [sb(f"tokens_out{j}", [P, SUBS], I32) for j in range(4)]
        slab_w = [sb(f"slab_w{j}", [P, 3, SUBS]) for j in range(4)]
        pool_buf = sb("pool_buf", [P, 1])
        act_tick = sb("act_tick", [P, 1])
        ident = sb("ident", [P, P])
        mean_mat = sb("mean_mat", [P, P])
        ones_bf = sb("ones_bf", [P, P], BF16)
        ones_f = sb("ones_f", [P, P])

        wr = sb("wr", [P, NE])
        br_b = sb("br_b", [P, NE])
        tri = sb("tri", [P, P], BF16)
        descend = sb("descend", [P, NE])
        region_0 = sb("region_0", [P, NE])
        ids = sb("ids", [P, B], I32)
        extra = [sb(f"extra{j}", [P, 4, TILES]) for j in range(4)]
        std_y = [sb(f"std_y{s}", [P, TILES]) for s in range(STREAMS)]
        logits = [sb(f"logits{j}", [P, TILES, NE]) for j in range(4)]
        probs = [sb(f"probs{j}", [P, TILES, NE]) for j in range(4)]
        edge = [sb(f"edge{j}", [P, 8, TILES]) for j in range(4)]
        cand = [sb(f"cand{j}", [P, TILES, NE]) for j in range(2)]
        hot = [sb(f"hot{j}", [P, 2, TILES, NE]) for j in range(4)]
        chosen = [sb(f"chosen{j}", [P, TILES, NE], BF16) for j in range(4)]
        rank = [sb(f"rank{j}", [P, 2, TILES]) for j in range(4)]
        slot = sb("slot", [P, STREAMS, 2, TILES], I32)
        taken = sb("taken", [P, NE])
        taken_new = [sb(f"taken_new{j}", [P, NE]) for j in range(2)]
        taken_bf = sb("taken_bf", [P, NE], BF16)
        slab_j = sb("slab_j", [P, SLABS])
        slab_rows = sb("slab_rows", [P, TOKENS // SLAB])
        count_f = sb("count_f", [P, NE])
        slabs_f = sb("slabs_f", [P, NE])
        slab_end = sb("slab_end", [P, NE])
        pad_f = sb("pad_f", [P, NE])
        slab_e = sb("slab_e", [P, SLABS])
        slab_0 = sb("slab_0", [P, SLABS])
        slab_row = sb("slab_row", [P, SLABS], I32)
        slab_exp = sb("slab_exp", [P, SLABS], I32)
        pad_row = sb("pad_row", [P, NE], I32)
        pad = sb("pad", [P, SUBS, ROW], I32)
        PARAMS = 3 + HC
        params_rows = sb("params_rows", [(2 + HC) * NE, P])
        params = sb("params", [P, NE, PARAMS])
        params_in = [sb(f"params_in{j}", [P, PARAMS]) for j in range(4)]

        def part(t, first, n):
            return t[:, :, :].rearrange("p t d -> p (t d)")[:, first:first + n]

        def by_tile(v, n):
            return v.rearrange("p (t d) -> p t d", t=n)

        below = part(turned[0], 0, TOKENS // SLAB * NE).rearrange("p (e j) -> p e j", e=NE)
        past = part(turned[1], 0, SLABS * NE).rearrange("p (j e) -> p j e", e=NE)
        before = part(turned[2], 0, SLABS * NE).rearrange("p (j e) -> p j e", e=NE)
        rows_in = [by_tile(part(rows_a[q], 0, SUBS * ROW), SUBS) for q in range(4)]
        b2_in = [part(scaled[q], 0, D) for q in range(4)]
        w1_in = [part(adjT[q], HC * D, H) for q in range(4)]
        w2_in = [by_tile(part(adjT[q], 0, HC * D), HC) for q in range(4)]
        y_out = [by_tile(part(rows_a[4 + q], 0, SLAB), SUBS) for q in range(4)]
        turned_32 = [part(resid[6], SLAB * j, SLAB) for j in range(2)]
        rows_T = [sb(f"rows_T{j}", [P, 2, SLAB], F32R)[:, :, :] for j in range(2)]
        w1_parts = [sb(f"w1_parts{j}", [P, 2, H], F32R)[:, :, :] for j in range(2)]
        hidden = [[part(resid[2 * j + c // 2], SLAB * (c % 2), SLAB) for c in range(HC)] for j in range(2)]
        psX = [part(ps[0], SLAB * j, SLAB) for j in range(2)]
        psH = [part(ps[1 + c // 2], SLAB * (c % 2), SLAB) for c in range(HC)]
        psY = [by_tile(part(ps[3], SLAB * j, SLAB), SUBS) for j in range(2)]

        bias_rows = part(turned[3], 0, 3 * P).rearrange("p (j e) -> p j e", j=3)
        crow = part(turned[3], 3 * P, 3 * P).rearrange("p (j e) -> p j e", j=3)
        centred = part(turned[2], 0, 2 * P).rearrange("p (j e) -> p j e", j=2)
        lnb_wide = part(turned[2], 2 * P, P)
        wb_wide = part(turned[2], 3 * P, P)

        sorted_rows = nc.dram_tensor("sorted_rows", (NE * REGION + SLAB, ROW), F32, kind="Internal").ap()
        params_dram = nc.dram_tensor("params_dram", (P, NE, PARAMS), F32, kind="Internal").ap()

        wl = sb("wl", [P, 4, P])
        lnw_b = sb("lnw_b", [P, P])
        cols_in = sb("cols_in", [P, 4])
        ab_b = sb("ab_b", [P, 1])
        sums = sb("sums", [P, 4])
        w_gnn0 = sb("w_gnn0", [P, P])
        w_ef = sb("w_ef", [P, 2])
        c_ef = sb("c_ef", [P, 2])
        w_ffn = sb("w_ffn", [P, P])
        w_ffn_plain = sb("w_ffn_plain", [P, P])
        w_mix = sb("w_mix", [P, 2, P])
        cpart = sb("cpart", [P, 3, 3, P], BF16)
        bias_mv = [sb(f"bias_mv{j}", [P, 4, P], BF16) for j in range(3)]

        weights_in = sem("weights_in")
        weights_late = sem("weights_late")
        consts_ready = sem("consts_ready")
        prep_v = sem("prep_v")
        prep_t = sem("prep_t")
        group_open = sem("group_open")
        x_in = [sem(f"x_in{s}") for s in range(STREAMS)]
        adj_in = [sem(f"adj_in{s}") for s in range(4)]
        out_done = [sem(f"out_done{s}") for s in range(STREAMS)]
        adj_psum = sem("adj_psum")
        adjT_ready = sem("adjT_ready")
        stat_step = [sem(f"stat_step{j}") for j in range(3)]
        stat_var = [sem(f"stat_var{j}") for j in range(3)]
        stat_pow = [sem(f"stat_pow{j}") for j in range(3)]
        mean_step = sem("mean_step")
        shift_ready = sem("shift_ready")
        pool_step = sem("pool_step")
        x_scaled = sem("x_scaled")
        x2_scaled = sem("x2_scaled")
        x_flip = sem("x_flip")
        x2_flip = sem("x2_flip")
        x_turned = sem("x_turned")
        x2_turned = sem("x2_turned")
        h_psum = sem("h_psum")
        ef_psum = sem("ef_psum")
        soft_e_ready = sem("soft_e_ready")
        den_psum = sem("den_psum")
        src_ready = sem("src_ready")
        soft_step = sem("soft_step")
        ratio_ready = sem("ratio_ready")
        num_psum = sem("num_psum")
        x1_ready = sem("x1_ready")
        h0_ready = sem("h0_ready")
        x2_ready = sem("x2_ready")
        q_psum = sem("q_psum")
        q_copied = sem("q_copied")
        mix_psum = sem("mix_psum")
        x3_ready = sem("x3_ready")
        a_step = sem("a_step")
        b_step = sem("b_step")
        c_step = sem("c_step")
        r_stat = sem("r_stat")
        r_mean = sem("r_mean")
        r_var = sem("r_var")
        r_var2 = sem("r_var2")
        r_pow = sem("r_pow")
        r_small = sem("r_small")
        rows_ready = sem("rows_ready")
        ids_ready = sem("ids_ready")
        r_flip = sem("r_flip")
        r_turned = sem("r_turned")
        logit_psum = sem("logit_psum")
        centred_logits = sem("centred_logits")
        exps = sem("exps")
        chosen_ready = sem("chosen_ready")
        rank_psum = sem("rank_psum")
        slots_ready = sem("slots_ready")
        scattered = [sem(f"scattered{s}") for s in range(STREAMS)]
        total_psum = sem("total_psum")
        tables_ready = sem("tables_ready")
        pads_in = sem("pads_in")
        table_step = sem("table_step")
        params_ready = sem("params_ready")
        pool_tick = sem("pool_tick")
        params_stored = sem("params_stored")
        w1_hi = sem("w1_hi")
        slab_32 = sem("slab_32")
        slab_hi = sem("slab_hi")
        slab_in = [sem(f"slab_in{q}") for q in range(4)]
        slab_flip = sem("slab_flip")
        slab_turned = sem("slab_turned")
        hidden_psum = sem("hidden_psum")
        hidden_ready = sem("hidden_ready")
        y_psum = sem("y_psum")
        weight_step = sem("weight_step")
        y_biased = sem("y_biased")
        y_ready = sem("y_ready")
        y_stored = [sem(f"y_stored{q}") for q in range(4)]
        tanh_done = sem("tanh_done")
        state_read = sem("state_read")
        silu_done = sem("silu_done")
        it_step = sem("it_step")
        it_var = sem("it_var")
        it_pow = sem("it_pow")
        it_scaled = sem("it_scaled")
        it_scaled_v = sem("it_scaled_v")
        it_scaled_a = sem("it_scaled_a")
        it_flip = sem("it_flip")
        it_turned = sem("it_turned")
        product = sem("product")

        xv = x.rearrange("(g s t) n d -> g s n t d", g=GROUPS, s=STREAMS)
        av = adj.rearrange("(g s t) n d -> g s n t d", g=GROUPS, s=STREAMS)
        ov = out.rearrange("(g s t) n d -> g s n t d", g=GROUPS, s=STREAMS)
        out_rows = out.rearrange("b n d -> (b n) d")
        A_STEPS, B_STEPS, C_STEPS, SMALL_STEPS = 3, 15, 3, 3
        SLAB_LOADS = 5

        prep_ready = [0]

        block = ctx.enter_context(nc.Block())

        def wide(v):
            return v.unsqueeze(2).to_broadcast([P, v.shape[1], D])

        loads = ((wl[:, 0, :], W_w), (wl[:, 1, :], F_W), (wl[:, 2, :], G_w[0:D, :]),
                 (wl[:, 3, :], G_w[D:2 * D, :]),
                 (lnw_b[:, :], ln_w.partition_broadcast(P)),
                 (cols_in[:, 0:1], a_w[0:D].rearrange("(p o) -> p o", o=1)),
                 (cols_in[:, 1:2], a_w[D:2 * D].rearrange("(p o) -> p o", o=1)),
                 (cols_in[:, 2:3], ln_b.rearrange("(p o) -> p o", o=1)),
                 (cols_in[:, 3:4], W_b.rearrange("(p o) -> p o", o=1)))
        late_loads = ((ab_b[:, :], a_b.partition_broadcast(P)),
                      (bias_rows[:, 0, :], W_b.partition_broadcast(P)),
                      (bias_rows[:, 1, :], F_b.partition_broadcast(P)),
                      (bias_rows[:, 2, :], G_b.partition_broadcast(P)),
                      (params_rows[0:NE, :], E_g), (params_rows[NE:2 * NE, :], E_b),
                      (params_rows[2 * NE:(2 + HC) * NE, :], E_b1.rearrange("e (c p) -> (e c) p", p=P)),
                      (wr[:, :], R_w), (br_b[:, :], R_b.partition_broadcast(P)))

        SILU_LAG, STATS_LAG, SCALE_LAG, FLIP_LAG, EVAC_LAG = 1, 2, 4, 5, 6
        POOL_TILES = 6

        X_LAG, ADJ_LAG, TURN_LAG, H_LAG, NUM_LAG, X1_STATS_LAG, H0_LAG = 1, 1, 2, 3, 4, 5, 6
        STEP_0 = 9
        GNN0_SLOTS = STREAMS + H0_LAG
        Q_LAG, MIX_LAG, ROWS_LAG = 1, 2, 4
        FLIP_R, CHOICE_R, RANK_R = 7, 8, 9

        def in_flight(k, *lags):
            return [k - lag if 0 <= k - lag < STREAMS else None for lag in lags]

        def stages(lags, k, base, peeled, tail):
            for lag in lags:
                j = k - lag
                if tail and j >= 0 or peeled and j < 0:
                    yield None, None
                else:
                    yield base + j, j % STREAMS

        @block.sync
        def _(sp):
            for dst, src in loads:
                sp.dma_start(dst, src).then_inc(weights_in, 16)

            def load_x(g, s):
                sp.dma_start(resid[s][:, :, :], xv[g, s]).then_inc(x_in[s], 16)

            for g in range(GROUPS):
                for s in range(STREAMS):
                    if s >= 4:
                        sp.wait_ge(adj_psum, g * STREAMS + s - 3)
                    sp.dma_start(act_z[s % 4][:, :, :], av[g, s]).then_inc(adj_in[s % 4], 16)
                    if g == 0:
                        load_x(g, s)
                        if s == 0:
                            for dst, src in late_loads:
                                sp.dma_start(dst, src).then_inc(weights_late, 16)
                if g == 0:
                    sp.wait_ge(params_ready, 1)
                    sp.dma_start(params_dram, params[:, :, :]).then_inc(params_stored, 16)
                for s in range(STREAMS + 1):
                    if s < STREAMS:
                        sp.wait_ge(x3_ready, g * STREAMS + s + 1)
                        sp.dma_start(ov[g, s], resid[s][:, :, :]).then_inc(out_done[s], 16)
                    if s >= 1:
                        sp.wait_ge(out_done[s - 1], g * 16 + 16)
                        if g + 1 < GROUPS:
                            sp.wait_ge(rows_ready, g * STREAMS + s)
                            load_x(g + 1, s - 1)

            sp.wait_ge(tables_ready, 1)
            for e in range(NE + 1):
                if e < NE:
                    at = sp.value_load(pad_row[0:1, e:e + 1], min_val=e * REGION, max_val=e * REGION + TOKENS)
                    dst = sorted_rows[bass.ds(at, SLAB), :]
                else:
                    dst = sorted_rows[NE * REGION:NE * REGION + SLAB, :]
                sp.dma_start(dst.rearrange("(t p) d -> p t d", t=SUBS),
                             pad[:, :, :].bitcast(F32)).then_inc(pads_in, 16)
            sp.wait_ge(pads_in, 16 * (NE + 1))
            sp.wait_ge(params_stored, 16)

            def load_rows(q, at):
                sp.dma_start(rows_in[q], sorted_rows[bass.ds(at, SLAB), :].rearrange("(t p) d -> p t d", p=P)
                             ).then_inc(slab_in[q], 16)

            def load_weights(q, e):
                sp.dma_start(w1_in[q], E_W1[bass.ds(e, 1)].rearrange("o p n -> p (o n)")).then_inc(slab_in[q], 16)
                sp.dma_start(w2_in[q], E_W2[bass.ds(e, 1)].rearrange("o (c p) d -> p (o c) d", p=P)
                             ).then_inc(slab_in[q], 16)
                sp.dma_start(b2_in[q], E_b2[bass.ds(e, 1)].rearrange("o d -> (o d)").partition_broadcast(P)
                             ).then_inc(slab_in[q], 16)
                sp.dma_start(params_in[q][:, :], params_dram[:, bass.ds(e, 1), :].rearrange("p o c -> p (o c)")
                             ).then_inc(slab_in[q], 16)

            def first_row(j):
                return sp.value_load(slab_row[0:1, bass.ds(j, 1)], min_val=0, max_val=NE * REGION)

            def expert_of(j):
                return sp.value_load(slab_exp[0:1, bass.ds(j, 1)], min_val=0, max_val=NE - 1)

            for q in range(4):
                load_weights(q, expert_of(q))
            for s in range(STREAMS):
                sp.wait_ge(scattered[s], GROUPS * 2 * TILES * 16)
            for q in range(4):
                load_rows(q, first_row(q))
            for j in range(4, SLABS):
                at, e = first_row(j), expert_of(j)
                sp.wait_ge(y_ready, j - 3)
                load_rows(j % 4, at)
                load_weights(j % 4, e)

            for q in range(4):
                sp.wait_ge(y_stored[q], 16 * SUBS * SLABS // 4)

        @block.gpsimd
        def _(pool):
            nc.gpsimd.memset(ident[:, :], 0.0).then_inc(pool_step, 1)
            nc.gpsimd.memset(minus_half[:, :], -0.5)
            nc.gpsimd.memset(pool_buf[:, :], 0.0).then_inc(pool_tick, 1)
            for j in range(3):
                nc.gpsimd.memset(bias_mv[j][:, :, :], 0.0)
            nc.gpsimd.memset(mean_mat[:, :], 1.0 / D)
            nc.gpsimd.memset(ones_bf[:, :], 1.0)
            nc.gpsimd.memset(ones_f[:, :], 1.0)
            for dst, step, first in ((descend, -1, NE), (region_0, REGION, 0), (slab_j, 1, 0), (slab_rows, SLAB, 0)):
                nc.gpsimd.iota(dst[:, :], pattern=[[step, dst.shape[1]]], base=first, channel_multiplier=0,
                               allow_small_or_imprecise_dtypes=True)
            nc.gpsimd.iota(ids[:, :], pattern=[[N, B]], base=0, channel_multiplier=1)
            nc.gpsimd.memset(pad[:, :, :], 0)
            nc.gpsimd.memset(tri[:, :], 0.0).then_inc(pool_step, 1)
            pool.wait_ge(pool_step, 2)
            nc.gpsimd.iota(pad[:, :, TOKEN], pattern=[[1, SUBS]], base=FAR, channel_multiplier=SUBS)
            nc.gpsimd.affine_select(out=tri[:, :], in_=tri[:, :], compare_op=ALU.is_ge, fill=1.0, base=0,
                                    pattern=[[-1, P]], channel_multiplier=1)
            nc.gpsimd.affine_select(out=ident[:, :], in_=ident[:, :], compare_op=ALU.not_equal, fill=1.0, base=0,
                                    pattern=[[-1, P]], channel_multiplier=1).then_inc(consts_ready, 1)

            def rstd_of(c, var_sem, n, pow_sem):
                pool.wait_ge(var_sem, n + 1)
                nc.gpsimd.tensor_tensor(rstd[c][:, :], var[c][:, :], minus_half[:, :], ALU.pow).then_inc(pow_sem, 1)
                pool.wait_ge(pow_sem, n + 1)

            def iteration(base, peeled):
                for k in range(STREAMS):
                    if peeled and k < 4:
                        pool.wait_ge(h0_ready, g * STREAMS + k + 5)
                    rstd_of(k % 4, it_var, base + k, it_pow)
                    if k >= 4 or not peeled:
                        pool.wait_ge(it_flip, base + (k - 3))
                    nc.gpsimd.tensor_tensor(scaled[k % 4][:, 0:POOL_TILES, :], act_z[k % 4][:, 0:POOL_TILES, :],
                                            wide(rstd[k % 4][:, 0:POOL_TILES]), ALU.mult).then_inc(it_scaled, 1)

            def scatter(g, moves):
                for s, t, k in moves:
                    if t == k == 0:
                        n = g * STREAMS + s
                        pool.wait_ge(slots_ready, n + 1)
                        pool.wait_ge(rows_ready, n + 1)
                        pool.wait_ge(ids_ready, n + 1)
                    nc.gpsimd.indirect_dma_start(
                        out=sorted_rows, in_=rows_a[s][:, t, :], in_offset=None,
                        out_offset=bass.IndirectOffsetOnAxis(ap=slot[:, s, k, t:t + 1].bitcast(U32), axis=0),
                    ).then_inc(scattered[s], 16)

            def moves_of(streams):
                return [(s, t, k) for s in streams for t in range(TILES) for k in range(2)]

            LATE, PER_SLOT = 3, 7
            late = moves_of(range(LATE, STREAMS))
            assert len(late) <= PER_SLOT * (STREAMS + X1_STATS_LAG)

            for g in range(GROUPS):
                for k in range(STREAMS + X1_STATS_LAG):
                    b, d = in_flight(k, X1_STATS_LAG, 0)
                    if d is not None:
                        rstd_of(4 + d % 4, stat_var[0], g * STREAMS + d, stat_pow[0])
                    if g:
                        scatter(g - 1, late[k * PER_SLOT:(k + 1) * PER_SLOT])
                    if b is not None:
                        if g:
                            pool.wait_ge(scattered[b], g * 2 * TILES * 16)
                        if b >= 4:
                            pool.wait_ge(h0_ready, g * STREAMS + b - 3)
                        rstd_of(b % 4, stat_var[1], g * STREAMS + b, stat_pow[1])
                        nc.gpsimd.tensor_tensor(shift[b % 4][:, :], neg_mean[b % 4][:, :], rstd[b % 4][:, :],
                                                ALU.mult).then_inc(shift_ready, 1)
                q0 = g * STEPS
                iteration(q0, True)
                with pool.Fori(q0 + STREAMS, q0 + STEPS, STREAMS) as q:
                    iteration(q, False)
                for s in range(STREAMS):
                    rstd_of(4 + s % 4, stat_var[2], g * STREAMS + s, stat_pow[2])
                    if s < 4:
                        pool.wait_ge(it_flip, g * STEPS + (STEPS - 3 + s))
                    else:
                        pool.wait_ge(x2_flip, g * STREAMS + s - 3)
                    nc.gpsimd.tensor_tensor(scaled[s % 4][:, :, :], resid[s][:, :, :], wide(rstd[4 + s % 4][:, :]),
                                            ALU.mult).then_inc(x2_scaled, 1)
                for s in range(STREAMS):
                    c, n = s % 4, g * STREAMS + s
                    ex = extra[s % 4]
                    if s >= 4:
                        pool.wait_ge(rows_ready, n - 3)
                    rstd_of(c, r_var, n, r_pow)

                    def small(i, ins):
                        ins.then_inc(r_small, 1)
                        pool.wait_ge(r_small, n * SMALL_STEPS + i)

                    pool.wait_ge(r_var2, n + 1)
                    small(1, nc.gpsimd.tensor_tensor(ex[:, 1, :], ex[:, 0, :], minus_half[:, :], ALU.pow))
                    nc.gpsimd.tensor_tensor(shift[c][:, :], neg_mean[c][:, :], ex[:, 1, :], ALU.mult)
                    small(2, nc.gpsimd.tensor_tensor(ex[:, 2, :], ex[:, 0, :], ex[:, 1, :], ALU.mult))
                    nc.gpsimd.tensor_tensor(std_y[s][:, :], ex[:, 2, :], rstd[c][:, :], ALU.mult).then_inc(r_small, 1)
                    nc.gpsimd.tensor_copy(
                        rows_a[s][:, :, TOKEN:TOKEN + 1].bitcast(I32),
                        ids[:, g * BATCHES + s * TILES:g * BATCHES + (s + 1) * TILES].unsqueeze(2)).then_inc(ids_ready, 1)
                scatter(g, moves_of(range(STREAMS if g == GROUPS - 1 else LATE)))

            def add_rows(j, q, first):
                pool.wait_ge(y_ready, j + (q + 1))
                if not first:
                    pool.wait_ge(y_stored[(q - 1) % 4], j * (4 * SUBS) + (16 * SUBS if q else 0))
                pool.wait_ge(pool_tick, j + (q + 1))
                nc.gpsimd.tensor_tensor(pool_buf[:, :], minus_half[:, 0:1], minus_half[:, 0:1],
                                        ALU.add).then_inc(pool_tick, 1)
                for t in range(SUBS):
                    nc.gpsimd.indirect_dma_start(
                        out=out_rows, in_=y_out[q][:, t, :], in_offset=None,
                        out_offset=bass.IndirectOffsetOnAxis(ap=tokens_out[q][:, t:t + 1].bitcast(U32), axis=0),
                        bounds_check=TOKENS - 1, oob_is_err=False, compute_op=ALU.add).then_inc(y_stored[q], 16)

            for s in range(STREAMS):
                pool.wait_ge(out_done[s], 16 * GROUPS)
            for q in range(4):
                add_rows(0, q, q == 0)
            with pool.Fori(4, SLABS, 4) as j:
                for q in range(4):
                    add_rows(j, q, False)

        @block.vector
        def _(dve):
            chain = [0]

            def link(ins):
                chain[0] += 1
                ins.then_inc(prep_v, 1)
                dve.wait_ge(prep_v, chain[0])

            dve.wait_ge(weights_in, 16 * len(loads))
            dve.wait_ge(consts_ready, 1)
            nc.vector.tensor_scalar(wb_wide[:, :], ones_f[:, :], cols_in[:, 3:4], None, ALU.mult)
            nc.vector.tensor_scalar(lnb_wide[:, :], ones_f[:, :], cols_in[:, 2:3], None, ALU.mult)
            link(nc.vector.tensor_tensor(centred[:, 1, :], wl[:, 1, :], lnw_b[:, :], ALU.mult))
            nc.vector.tensor_reduce(sums[:, 0:1], wl[:, 0, :], AX.X, ALU.add)
            link(nc.vector.tensor_reduce(sums[:, 1:2], centred[:, 1, :], AX.X, ALU.add))
            link(nc.vector.tensor_scalar(sums[:, 2:4], sums[:, 0:2], -1.0 / D, None, ALU.mult))
            nc.vector.tensor_scalar(centred[:, 0, :], wl[:, 0, :], sums[:, 2:3], None, ALU.add)
            link(nc.vector.tensor_scalar(centred[:, 1, :], centred[:, 1, :], sums[:, 3:4], None, ALU.add))
            dve.wait_ge(prep_t, 1)
            nc.vector.tensor_copy(w_gnn0[:, :], ps[0][:, 0, :])
            nc.vector.tensor_copy(w_ffn[:, :], ps[0][:, 1, :])
            nc.vector.tensor_copy(w_ef[:, :], ps[1][:, 0, 0:2])
            dve.wait_ge(weights_late, 16 * len(late_loads))
            nc.vector.tensor_copy(c_ef[:, 1:2], ps[1][:, 0, 9:10])
            nc.vector.tensor_tensor(c_ef[:, 0:1], ps[1][:, 0, 8:9], ab_b[:, :], ALU.add)
            nc.vector.tensor_tensor(w_mix[:, :, :], wl[:, 2:4, :], ps[2][:, 0:2, :], ALU.subtract)
            link(nc.vector.tensor_copy(w_ffn_plain[:, :], ps[0][:, 2, :]))
            dve.wait_ge(prep_t, 2)
            link(nc.vector.tensor_copy(crow[:, :, :], bias_rows[:, :, :]))
            link(nc.vector.tensor_tensor(crow[:, 1, :], ps[3][:, 0, :], bias_rows[:, 1, :], ALU.add))
            for part in range(3):
                link(nc.vector.tensor_copy(cpart[:, part, :, :], crow[:, :, :]))
                if part < 2:
                    link(nc.vector.tensor_tensor(crow[:, :, :], crow[:, :, :], cpart[:, part, :, :], ALU.subtract))
            for j in range(3):
                for part in range(3):
                    row = slice(32 * part, 32 * part + 1)
                    last = nc.vector.tensor_copy(bias_mv[j][row, :, :],
                                                 cpart[row, part, j, :].unsqueeze(1).to_broadcast([1, 4, P]))
            link(last)
            dve.wait_ge(prep_t, 3)
            nc.vector.tensor_copy(params[:, :, 2 + HC], descend[:, :])
            nc.vector.tensor_copy(params[:, :, 0], ps[1][:, 4, 0:NE])
            nc.vector.tensor_copy(params[:, :, 1], ps[1][:, 4, NE:2 * NE])
            nc.vector.tensor_copy(params[:, :, 2:2 + HC], ps[1][:, 4, 2 * NE:(2 + HC) * NE].rearrange(
                "p (e c) -> p e c", c=HC)).then_inc(params_ready, 1)

            nc.vector.memset(taken[:, :], 0.0)
            link(nc.vector.memset(taken_bf[:, :], 0.0))
            prep_ready[0] = chain[0]

            def tile_statistics(src, c, tiles=range(TILES)):
                for t in tiles:
                    last = nc.vector.bn_stats(stats[c][:, t, :], src[:, t, :])
                return last

            def half_differences(c, step_sem, n):
                st, sm = stats[c], small[c]
                dve.wait_ge(step_sem, n * 3 + 1)
                nc.vector.tensor_tensor(sm[:, 0, :], st[:, :, 1], st[:, :, 4], ALU.subtract)
                nc.vector.scalar_tensor_tensor(sm[:, 1, :], st[:, :, 2], EPS * D, st[:, :, 5], ALU.add,
                                               ALU.add).then_inc(step_sem, 1)

            def between_halves(c, step_sem, n):
                sm = small[c]
                dve.wait_ge(step_sem, n * 3 + 2)
                nc.vector.scalar_tensor_tensor(sm[:, 2, :], sm[:, 0, :], 0.25, sm[:, 0, :], ALU.mult,
                                               ALU.mult).then_inc(step_sem, 1)

            def variance(c, step_sem, n, var_sem):
                sm = small[c]
                dve.wait_ge(step_sem, n * 3 + 3)
                nc.vector.scalar_tensor_tensor(var[c][:, :], sm[:, 1, :], 1.0 / D, sm[:, 2, :], ALU.mult,
                                               ALU.add).then_inc(var_sem, 1)

            def statistics(src, c, step_sem, n, var_sem, mean_n=None, mean_sem=mean_step):
                tile_statistics(src, c).then_inc(step_sem, 1)
                half_differences(c, step_sem, n)
                if mean_n is not None:
                    nc.vector.tensor_tensor(small[c][:, 3, :], stats[c][:, :, 1], stats[c][:, :, 4],
                                            ALU.add).then_inc(mean_sem, 1)
                between_halves(c, step_sem, n)
                if mean_n is not None:
                    dve.wait_ge(mean_sem, mean_n + 1)
                    nc.vector.tensor_scalar(neg_mean[c][:, :], small[c][:, 3, :], -0.5, None, ALU.mult)
                variance(c, step_sem, n, var_sem)

            def over_e(v):
                return v.unsqueeze(2).to_broadcast([P, TILES, NE])

            def over_t(v):
                return v.unsqueeze(1).to_broadcast([P, TILES, NE])

            def linker(step_sem, first):
                at = [0]

                def linked(ins):
                    at[0] += 1
                    ins.then_inc(step_sem, 1)
                    dve.wait_ge(step_sem, first + at[0])
                return linked, at

            def route_a(s, n):
                c = s % 4
                linked, at = linker(a_step, n * A_STEPS)
                dve.wait_ge(logit_psum, n + 1)
                dve.wait_ge(r_small, n * SMALL_STEPS + SMALL_STEPS)
                linked(nc.vector.tensor_tensor(logits[c][:, :, :], ps[c][:, 0, 0:TILES * NE].rearrange(
                    "p (t e) -> p t e", e=NE), over_e(std_y[s][:, :]), ALU.mult))
                linked(nc.vector.tensor_tensor(logits[c][:, :, :], logits[c][:, :, :], over_t(br_b[:, :]), ALU.add))
                linked(nc.vector.tensor_reduce(edge[c][:, 0, :], logits[c][:, :, :], AX.X, ALU.max))
                assert at[0] == A_STEPS
                nc.vector.tensor_tensor(logits[c][:, :, :], logits[c][:, :, :], over_e(edge[c][:, 0, :]),
                                        ALU.subtract).then_inc(centred_logits, 1)

            def route_b(s, n):
                c = s % 4
                pr, ed, cd, ht = probs[c][:, :, :], edge[c], cand[s % 2][:, :, :], hot[c]
                linked, at = linker(b_step, n * B_STEPS)
                dve.wait_ge(exps, n + 1)
                linked(nc.vector.tensor_reduce(ed[:, 1, :], pr, AX.X, ALU.add))
                linked(nc.vector.reciprocal(ed[:, 2, :], ed[:, 1, :]))
                linked(nc.vector.tensor_tensor(pr, pr, over_e(ed[:, 2, :]), ALU.mult))
                for k in range(2):
                    linked(nc.vector.tensor_reduce(ed[:, 3 + k, :], pr, AX.X, ALU.max))
                    linked(nc.vector.tensor_tensor(cd, pr, over_e(ed[:, 3 + k, :]), ALU.is_ge))
                    linked(nc.vector.tensor_tensor(cd, cd, over_t(descend[:, :]), ALU.mult))
                    linked(nc.vector.tensor_reduce(ed[:, 5 + k, :], cd, AX.X, ALU.max))
                    if k == 1:
                        nc.vector.tensor_tensor(ed[:, 7, :], ed[:, 3, :], ed[:, 4, :], ALU.add)
                    linked(nc.vector.tensor_tensor(ht[:, k, :, :], over_t(descend[:, :]), over_e(ed[:, 5 + k, :]),
                                                   ALU.is_equal))
                    if k == 0:
                        linked(nc.vector.scalar_tensor_tensor(pr, ht[:, 0, :, :], -4.0, pr, ALU.mult, ALU.add))
                nc.vector.tensor_tensor(chosen[c][:, :, :], ht[:, 0, :, :], ht[:, 1, :, :], ALU.add)
                linked(nc.vector.reciprocal(ed[:, 1, :], ed[:, 7, :]))
                assert at[0] == B_STEPS
                nc.vector.tensor_copy(rows_a[s][:, :, FIRST], ed[:, 5, :])
                for k in range(2):
                    nc.vector.tensor_tensor(rows_a[s][:, :, WEIGHT + k], ed[:, 3 + k, :], ed[:, 1, :], ALU.mult)
                nc.vector.tensor_reduce(taken_new[s % 2][:, :], chosen[c][:, :, :].rearrange("p t e -> p e t"), AX.X,
                                        ALU.add).then_inc(chosen_ready, 1)

            def route_c(s, n):
                c = s % 4
                linked, at = linker(c_step, n * C_STEPS)
                dve.wait_ge(rank_psum, n + 1)
                nc.vector.tensor_tensor(taken[:, :], taken[:, :], taken_new[s % 2][:, :], ALU.add)
                linked(nc.vector.tensor_tensor(logits[c][:, :, :], ps[c][:, 4, 0:TILES * NE].rearrange(
                    "p (t e) -> p t e", e=NE), over_t(region_0[:, :]), ALU.add))
                nc.vector.tensor_copy(taken_bf[:, :], taken[:, :])
                linked(nc.vector.tensor_tensor(hot[c][:, :, :, :], hot[c][:, :, :, :], logits[c][:, :, :].unsqueeze(1)
                                               .to_broadcast([P, 2, TILES, NE]), ALU.mult))
                linked(nc.vector.tensor_reduce(rank[c][:, :, :], hot[c][:, :, :, :], AX.X, ALU.add))
                assert at[0] == C_STEPS
                nc.vector.tensor_copy(slot[:, s, :, :], rank[c][:, :, :]).then_inc(slots_ready, 1)

            with dve.Fori(0, GROUPS) as g:
                nc.vector.memset(tick[:, :], 0.0).then_inc(group_open, 1)
                def iteration(base, peeled=False, tail=False, slots=range(STREAMS)):
                    for k in slots:
                        (n, s), (o, w), (m, r) = stages([STATS_LAG, STATS_LAG + 1, SCALE_LAG], k, base, peeled, tail)
                        if n is not None:
                            dve.wait_ge(silu_done, n + 1)
                            tile_statistics(act_z[s % 4], s % 4, range(TILES // 2))
                        if o is not None:
                            between_halves(w % 4, it_step, o)
                        if n is not None:
                            tile_statistics(act_z[s % 4], s % 4, range(TILES // 2, TILES)).then_inc(it_step, 1)
                        if o is not None:
                            variance(w % 4, it_step, o, it_var)
                        if m is not None and r % 2 == 0:
                            dve.wait_ge(it_pow, m + 1)
                            t = POOL_TILES
                            nc.vector.tensor_scalar(scaled[r % 4][:, t, :], act_z[r % 4][:, t, :],
                                                    rstd[r % 4][:, t:t + 1], None,
                                                    ALU.mult).then_inc(it_scaled_v, 2)
                        if tail:
                            dve.wait_ge(product, base + (k - STREAMS + 1))
                            nc.vector.tensor_tensor(resid[k][:, :, :], ps[k % 4][:, :, :], resid[k][:, :, :],
                                                    ALU.add).then_inc(x2_ready, 1)
                        else:
                            h = start_h[k] if peeled else ps[k % 4][:, :, :]
                            dve.wait_ge(tanh_done, base + (k + 1))
                            nc.vector.scalar_tensor_tensor(work[k % 4][:, :, :], work[k % 4][:, :, :], 0.01,
                                                           h, ALU.mult, ALU.add).then_inc(state_read, 1)
                        if n is not None:
                            half_differences(s % 4, it_step, n)
                        if tail:
                            dve.wait_ge(x2_ready, g * STREAMS + k + 1)
                            if k >= 4:
                                dve.wait_ge(stat_pow[2], g * STREAMS + k - 3)
                            statistics(resid[k], 4 + k % 4, stat_step[2], g * STREAMS + k, stat_var[2])

                q0 = g * STEPS
                for k in range(GNN0_SLOTS):
                    a, b, d, e = in_flight(k, H_LAG, NUM_LAG, 0, X1_STATS_LAG)
                    if b is not None:
                        c, n = b % 4, g * STREAMS + b
                        dve.wait_ge(den_psum, n + 1)
                        nc.vector.tensor_tensor(soft[c][:, 0, :], ps[c][:, 0, 0:TILES], soft_e[c][:, :],
                                                ALU.mult).then_inc(soft_step, 1)
                        dve.wait_ge(soft_step, n * 2 + 1)
                        nc.vector.reciprocal(soft[c][:, 1, :], soft[c][:, 0, :]).then_inc(soft_step, 1)
                        dve.wait_ge(soft_step, n * 2 + 2)
                        nc.vector.tensor_tensor(soft[c][:, 2, :], soft[c][:, 1, :], soft_e[c][:, :],
                                                ALU.mult).then_inc(ratio_ready, 1)
                    if d is not None:
                        dve.wait_ge(x_in[d], g * 16 + 16)
                        statistics(resid[d], 4 + d % 4, stat_step[0], g * STREAMS + d, stat_var[0])
                    if a is not None:
                        c, n = a % 4, g * STREAMS + a
                        dve.wait_ge(h_psum, n + 1)
                        nc.vector.tensor_tensor(work[c][:, :, :], ps[c][:, :, :], wide(soft_f[c][:, :]),
                                                ALU.mult).then_inc(src_ready, 1)
                    if e is not None:
                        dve.wait_ge(x1_ready, g * STREAMS + e + 1)
                        statistics(resid[e], e % 4, stat_step[1], g * STREAMS + e, stat_var[1], g * STREAMS + e)
                    if b is not None:
                        c, n = b % 4, g * STREAMS + b
                        dve.wait_ge(num_psum, n + 1)
                        dve.wait_ge(ratio_ready, n + 1)
                        for t in range(TILES):
                            last = nc.vector.scalar_tensor_tensor(resid[b][:, t, :], ps[c][:, t, :],
                                                                  soft[c][:, 2, t:t + 1], resid[b][:, t, :],
                                                                  ALU.mult, ALU.add)
                        last.then_inc(x1_ready, 1)
                    if k >= STEP_0:
                        iteration(q0, peeled=True, slots=[k - STEP_0])

                iteration(q0, peeled=True, slots=range(GNN0_SLOTS - STEP_0, STREAMS))
                with dve.Fori(q0 + STREAMS, q0 + STEPS, STREAMS) as q:
                    iteration(q)
                iteration(g * STEPS + STEPS, tail=True)
                for k in range(STREAMS + RANK_R):
                    s, a, b, d = in_flight(k, MIX_LAG, FLIP_R, CHOICE_R, RANK_R)
                    if s is not None:
                        dve.wait_ge(mix_psum, g * STREAMS + s + 1)
                        nc.vector.scalar_tensor_tensor(resid[s][:, :, :], ps[s % 4][:, :, :], 0.0, resid[s][:, :, :],
                                                       ALU.max, ALU.add).then_inc(x3_ready, 1)
                        n = g * STREAMS + s
                        dve.wait_ge(x3_ready, n + 1)
                        if s >= 4:
                            dve.wait_ge(r_small, (n - 3) * SMALL_STEPS)
                        statistics(resid[s], s % 4, r_stat, n, r_var, n, r_mean)
                        dve.wait_ge(r_var, n + 1)
                        nc.vector.tensor_scalar(extra[s % 4][:, 0, :], var[s % 4][:, :], 1.0 + EPS, -EPS, ALU.mult,
                                                ALU.add).then_inc(r_var2, 1)
                    if d is not None:
                        route_c(d, g * STREAMS + d)
                    if b is not None:
                        route_b(b, g * STREAMS + b)
                    if a is not None:
                        route_a(a, g * STREAMS + a)

            def table(ins):
                table_at[0] += 1
                ins.then_inc(table_step, 1)
                dve.wait_ge(table_step, table_at[0])

            table_at = [0]
            dve.wait_ge(total_psum, 1)
            table(nc.vector.tensor_copy(count_f[:, :], ps[0][:, 0, 0:NE]))
            shape = [P, NE, TOKENS // SLAB]
            table(nc.vector.tensor_tensor(below, slab_rows[:, :].unsqueeze(1).to_broadcast(shape),
                                          count_f[:, :].unsqueeze(2).to_broadcast(shape), ALU.is_lt))
            nc.vector.tensor_tensor(pad_f[:, :], count_f[:, :], region_0[:, :], ALU.add)
            table(nc.vector.tensor_reduce(slabs_f[:, :], below, AX.X, ALU.add))
            nc.vector.tensor_copy(pad_row[:, :], pad_f[:, :])
            table(nc.vector.tensor_copy(slab_end[:, 0:1], slabs_f[:, 0:1]))
            for e in range(1, NE):
                table(nc.vector.tensor_tensor(slab_end[:, e:e + 1], slab_end[:, e - 1:e], slabs_f[:, e:e + 1], ALU.add))
            shape = [P, SLABS, NE]
            table(nc.vector.tensor_tensor(past, slab_j[:, :].unsqueeze(2).to_broadcast(shape),
                                          slab_end[:, :].unsqueeze(1).to_broadcast(shape), ALU.is_ge))
            nc.vector.tensor_reduce(slab_e[:, :], past, AX.X, ALU.add)
            table(nc.vector.tensor_tensor(before, past, slabs_f[:, :].unsqueeze(1).to_broadcast(shape), ALU.mult))
            table(nc.vector.tensor_reduce(slab_0[:, :], before, AX.X, ALU.add))
            table(nc.vector.tensor_tensor(slab_0[:, :], slab_j[:, :], slab_0[:, :], ALU.subtract))
            table(nc.vector.tensor_scalar(slab_0[:, :], slab_0[:, :], float(SLAB), None, ALU.mult))
            table(nc.vector.scalar_tensor_tensor(slab_0[:, :], slab_e[:, :], float(REGION), slab_0[:, :], ALU.mult,
                                                 ALU.add))
            nc.vector.tensor_scalar(slab_row[:, :], slab_0[:, :], float(NE * REGION), None, ALU.min)
            nc.vector.tensor_scalar(slab_exp[:, :], slab_e[:, :], float(NE - 1), None,
                                    ALU.min).then_inc(tables_ready, 1)

            def turn(j, n, q, b):
                dve.wait_ge(slab_in[q], j * (4 * SLAB_LOADS) + 16 * SLAB_LOADS)
                nc.vector.tensor_copy(w1_parts[b][:, 0, :], w1_in[q]).then_inc(w1_hi, 1)
                dve.wait_ge(w1_hi, n + 1)
                nc.vector.tensor_tensor(w1_parts[b][:, 1, :], w1_in[q], w1_parts[b][:, 0, :].bitcast(F32),
                                        ALU.subtract)
                dve.wait_ge(slab_32, n + 1)
                nc.vector.tensor_copy(rows_T[b][:, 0, :], turned_32[b]).then_inc(slab_hi, 1)
                dve.wait_ge(slab_hi, n + 1)
                nc.vector.tensor_tensor(rows_T[b][:, 1, :], turned_32[b], rows_T[b][:, 0, :].bitcast(F32),
                                        ALU.subtract).then_inc(slab_turned, 1)
                row_weights(n, q)

            def expert(j, peeled=False, second=False, end=False):
                for q in range(4):
                    n = j + q
                    if not (end and q == 3):
                        turn(j if q < 3 else j + 4, n + 1, (q + 1) % 4, (q + 1) % 2)
                    if q or not peeled:
                        join_bias(j + (q - 1), j if q else j - 4, (q - 1) % 4, peeled or second and q == 0)

            def row_weights(n, q):
                first, expert_of = rows_in[q][:, :, FIRST], params_in[q][:, 2 + HC:3 + HC]
                nc.vector.scalar_tensor_tensor(slab_w[q][:, 0, :], first, expert_of, rows_in[q][:, :, WEIGHT],
                                               ALU.is_equal, ALU.mult)
                nc.vector.scalar_tensor_tensor(slab_w[q][:, 1, :], first, expert_of, rows_in[q][:, :, WEIGHT + 1],
                                               ALU.not_equal, ALU.mult).then_inc(weight_step, 1)

            def join_bias(n, j, q, peeled):
                dve.wait_ge(weight_step, n + 1)
                nc.vector.tensor_tensor(slab_w[q][:, 2, :], slab_w[q][:, 0, :], slab_w[q][:, 1, :],
                                        ALU.add)
                dve.wait_ge(y_psum, n + 1)
                if not peeled:
                    dve.wait_ge(y_stored[q], j * (4 * SUBS))
                nc.vector.tensor_copy(tokens_out[q][:, :], rows_in[q][:, :, TOKEN].bitcast(I32))
                nc.vector.tensor_tensor(y_out[q], psY[q % 2], b2_in[q].unsqueeze(1).to_broadcast([P, SUBS, D]),
                                        ALU.add).then_inc(y_biased, 1)
                dve.wait_ge(y_biased, n + 1)
                nc.vector.tensor_tensor(y_out[q], y_out[q], slab_w[q][:, 2, :].unsqueeze(2).to_broadcast(
                    [P, SUBS, D]), ALU.mult).then_inc(y_ready, 1)

            turn(0, 0, 0, 0)
            expert(0, peeled=True)
            expert(4, second=True)
            with dve.Fori(8, SLABS - 4, 4) as j:
                expert(j)
            expert(SLABS - 4, end=True)
            join_bias(SLABS - 1, SLABS - 4, 3, False)

        @block.scalar
        def _(act):
            with act.Fori(0, GROUPS) as g:
                def iteration(base, peeled=False, tail=False, slots=range(STREAMS)):
                    for k in slots:
                        (n, s), (m, r), (l, v) = stages([EVAC_LAG, SCALE_LAG, SILU_LAG], k, base, peeled, tail)
                        if n is not None:
                            act.wait_ge(it_flip, n + 1)
                            nc.scalar.copy(turned[s % 4][:, :, :], ps[s % 4][:, :, :]).then_inc(it_turned, 1)
                        if not tail:
                            if peeled:
                                h = start_h[k]
                                if k < 4:
                                    act.wait_ge(x1_ready, g * STREAMS + k + 5)
                            else:
                                h = ps[k % 4][:, :, :]
                                act.wait_ge(product, base + (k - STREAMS + 1))
                            nc.scalar.activation(work[k % 4][:, :, :], h, ACT.Tanh).then_inc(tanh_done, 1)
                        if m is not None:
                            act.wait_ge(it_pow, m + 1)
                            for t in range(POOL_TILES + (r % 2 == 0), TILES):
                                last = nc.scalar.mul(scaled[r % 4][:, t, :], act_z[r % 4][:, t, :],
                                                     rstd[r % 4][:, t:t + 1])
                            last.then_inc(it_scaled_a, 1)
                        if l is not None:
                            act.wait_ge(state_read, l + 1)
                            if not (peeled and v < 4):
                                act.wait_ge(it_scaled, l - 3)
                                if v % 2 == 0:
                                    act.wait_ge(it_scaled_v, l - 2)
                                act.wait_ge(it_scaled_a, l - 3)
                            nc.scalar.activation(act_z[v % 4][:, :, :], work[v % 4][:, :, :],
                                                 ACT.Silu).then_inc(silu_done, 1)

                q0 = g * STEPS
                for k in range(GNN0_SLOTS):
                    a, b, d, e = in_flight(k, ADJ_LAG, TURN_LAG, H0_LAG, X_LAG)
                    if e is not None:
                        act.wait_ge(stat_pow[0], g * STREAMS + e + 1)
                        if e >= 4:
                            act.wait_ge(x_flip, g * STREAMS + e - 3)
                        for t in range(TILES):
                            last = nc.scalar.mul(scaled[e % 4][:, t, :], resid[e][:, t, :],
                                                 rstd[4 + e % 4][:, t:t + 1])
                        last.then_inc(x_scaled, 1)
                    if b is not None:
                        c, n = b % 4, g * STREAMS + b
                        act.wait_ge(x_flip, n + 1)
                        nc.scalar.copy(turned[c][:, :, :], ps[c][:, :, :]).then_inc(x_turned, 1)
                    if d is not None:
                        act.wait_ge(shift_ready, g * STREAMS + d + 1)
                        for t in range(TILES):
                            last = nc.scalar.activation(start_h[d][:, t, :], resid[d][:, t, :], ACT.Identity,
                                                        bias=shift[d % 4][:, t:t + 1], scale=rstd[d % 4][:, t:t + 1])
                        last.then_inc(h0_ready, 1)
                    if a is not None:
                        act.wait_ge(adj_psum, g * STREAMS + a + 1)
                        nc.scalar.copy(adjT[a][:, :, :], ps[a % 4][:, :, :]).then_inc(adjT_ready, 1)
                    if b is not None:
                        act.wait_ge(ef_psum, n + 1)
                        ef = ps[c][:, 0, 0:2 * TILES].rearrange("p (t k) -> p t k", k=2)
                        nc.scalar.activation(soft_f[c][:, :], ef[:, :, 1], ACT.Exp, bias=c_ef[:, 1:2])
                        nc.scalar.activation(soft_e[c][:, :], ef[:, :, 0], ACT.Exp,
                                             bias=c_ef[:, 0:1]).then_inc(soft_e_ready, 1)
                    if k == STEP_0 + SILU_LAG:
                        nc.scalar.activation(act_tick[:, :], minus_half[:, 0:1], ACT.Silu)
                    if k >= STEP_0:
                        iteration(q0, peeled=True, slots=[k - STEP_0])

                iteration(q0, peeled=True, slots=range(GNN0_SLOTS - STEP_0, STREAMS))
                with act.Fori(q0 + STREAMS, q0 + STEPS, STREAMS) as q:
                    iteration(q)
                iteration(g * STEPS + STEPS, tail=True, slots=range(EVAC_LAG))
                act.wait_ge(product, g * STEPS + STEPS)
                for k in range(STREAMS + CHOICE_R):
                    f, d = in_flight(k, FLIP_R, CHOICE_R)
                    if d is not None:
                        act.wait_ge(centred_logits, g * STREAMS + d + 1)
                        nc.scalar.activation(probs[d % 4][:, :, :], logits[d % 4][:, :, :], ACT.Exp).then_inc(exps, 1)
                    a, b, d = in_flight(k, 0, Q_LAG, ROWS_LAG)
                    if a is not None:
                        act.wait_ge(x2_flip, g * STREAMS + a + 1)
                        if a >= 4:
                            act.wait_ge(mix_psum, g * STREAMS + a - 3)
                        nc.scalar.copy(turned[a % 4][:, :, :], ps[a % 4][:, :, :]).then_inc(x2_turned, 1)
                    if f is not None:
                        act.wait_ge(r_flip, g * STREAMS + f + 1)
                        nc.scalar.copy(turned[f % 4][:, :, :], ps[f % 4][:, :, :]).then_inc(r_turned, 1)
                    if b is not None:
                        act.wait_ge(q_psum, g * STREAMS + b + 1)
                        nc.scalar.copy(act_z[b % 4][:, :, :], ps[b % 4][:, :, :]).then_inc(q_copied, 1)
                    if d is not None:
                        act.wait_ge(r_small, (g * STREAMS + d) * SMALL_STEPS + SMALL_STEPS)
                        for t in range(TILES):
                            last = nc.scalar.activation(rows_a[d][:, t, 0:D], resid[d][:, t, :], ACT.Identity,
                                                        bias=shift[d % 4][:, t:t + 1],
                                                        scale=extra[d % 4][:, 1, t:t + 1])
                        last.then_inc(rows_ready, 1)

            def gelus(n, q, b):
                for c in range(HC):
                    act.wait_ge(hidden_psum, n * HC + (c + 1))
                    nc.scalar.activation(hidden[b][c], psH[c], ACT.Gelu,
                                         bias=params_in[q][:, 2 + c:3 + c]).then_inc(hidden_ready, 1)

            def turn(n, q, b):
                act.wait_ge(slab_flip, n + 1)
                nc.scalar.activation(turned_32[b], psX[b], ACT.Identity, bias=params_in[q][:, 1:2],
                                     scale=params_in[q][:, 0:1]).then_inc(slab_32, 1)

            def expert(j, end=False):
                for q in range(4):
                    gelus(j + q, q, q % 2)
                    if not (end and q == 3):
                        turn(j + (q + 1), (q + 1) % 4, (q + 1) % 2)

            turn(0, 0, 0)
            with act.Fori(0, SLABS - 4, 4) as j:
                expert(j)
            expert(SLABS - 4, end=True)

        @block.tensor
        def _(pe):
            pe.wait_ge(consts_ready, 1)
            pe.wait_ge(prep_v, 4)
            nc.tensor.transpose(ps[0][:, 0, :], centred[:, 0, :], ident[:, :])
            nc.tensor.transpose(ps[0][:, 1, :], centred[:, 1, :], ident[:, :])
            nc.tensor.transpose(ps[0][:, 2, :], wl[:, 1, :], ident[:, :])
            nc.tensor.matmul(ps[1][:, 0, 0:2], centred[:, 0, :], cols_in[:, 0:2], start=True, stop=True)
            nc.tensor.matmul(ps[1][:, 0, 8:10], wb_wide[:, :], cols_in[:, 0:2], start=True, stop=True)
            nc.tensor.matmul(ps[2][:, 0:2, :], mean_mat[:, :], wl[:, 2:4, :], start=True,
                             stop=True).then_inc(prep_t, 1)
            pe.wait_ge(prep_v, 5)
            nc.tensor.matmul(ps[3][:, 0, :], lnb_wide[:, :], w_ffn_plain[:, :], start=True,
                             stop=True).then_inc(prep_t, 1)
            pe.wait_ge(weights_late, 16 * len(late_loads))
            nc.tensor.transpose(ps[1][:, 4, 0:(2 + HC) * NE], params_rows[:, :],
                                ident[0:(2 + HC) * NE, 0:(2 + HC) * NE]).then_inc(prep_t, 1)
            pe.wait_ge(prep_v, prep_ready[0])

            def flip(c, src):
                for t in range(TILES):
                    last = nc.tensor.transpose(ps[c][:, t, :], src[:, t, :], ident[:, :])
                return last

            def rows(c, terms, bias=None):
                for bank in range(2):
                    if bias is not None:
                        nc.tensor.matmul(ps[c][:, 4 * bank:4 * bank + 4, :], ones_bf[:, :], bias_mv[bias][:, :, :],
                                         start=True, stop=False, skip_group_check=True)
                    for t in range(4 * bank, 4 * bank + 4):
                        for m, (stationary, moving) in enumerate(terms):
                            last = nc.tensor.matmul(ps[c][:, t, :], stationary[:, t, :], moving(t),
                                                    start=bias is None and m == 0, stop=m == len(terms) - 1,
                                                    skip_group_check=True)
                return last

            with pe.Fori(0, GROUPS) as g:
                pe.wait_ge(group_open, g + 1)
                for k in range(ADJ_LAG, STREAMS + NUM_LAG):
                    a, b, d, e = in_flight(k, ADJ_LAG, TURN_LAG, NUM_LAG, H_LAG)
                    if d is not None:
                        pe.wait_ge(src_ready, g * STREAMS + d + 1)
                        for t in range(TILES):
                            last = nc.tensor.matmul(ps[d % 4][:, 0, t:t + 1], adjT[d][:, t, :],
                                                    soft_f[d % 4][:, t:t + 1], start=True, stop=True)
                        last.then_inc(den_psum, 1)
                    if b is not None:
                        pe.wait_ge(adjT_ready, g * STREAMS + b + 1)
                        pe.wait_ge(x_scaled, g * STREAMS + b + 1)
                        flip(b % 4, scaled[b % 4]).then_inc(x_flip, 1)
                    if e is not None:
                        pe.wait_ge(soft_e_ready, g * STREAMS + e + 1)
                        rows(e % 4, [(turned[e % 4], lambda t: w_gnn0[:, :])], bias=0).then_inc(h_psum, 1)
                    if a is not None:
                        pe.wait_ge(adj_in[a % 4], g * (16 * STREAMS // 4) + 16 * (a // 4 + 1))
                        if a >= 4:
                            pe.wait_ge(x1_ready, g * STREAMS + a - 3)
                        flip(a % 4, act_z[a % 4]).then_inc(adj_psum, 1)
                    if d is not None:
                        pe.wait_ge(ratio_ready, g * STREAMS + d + 1)
                        rows(d % 4, [(adjT[d], lambda t, c=d % 4: work[c][:, t, :])]).then_inc(num_psum, 1)
                    if b is not None:
                        c = b % 4
                        pe.wait_ge(x_turned, g * STREAMS + b + 1)
                        for t in range(TILES):
                            last = nc.tensor.matmul(ps[c][:, 0, 2 * t:2 * t + 2], turned[c][:, t, :], w_ef[:, :],
                                                    start=True, stop=True)
                        last.then_inc(ef_psum, 1)

                def iteration(base, peeled=False, tail=False):
                    for k in range(STREAMS):
                        (n, s), (m, r) = stages([FLIP_LAG, EVAC_LAG], k, base, peeled, tail)
                        if n is not None:
                            pe.wait_ge(it_scaled, n + 1)
                            if s % 2 == 0:
                                pe.wait_ge(it_scaled_v, n + 2)
                            pe.wait_ge(it_scaled_a, n + 1)
                            if tail and s >= 4:
                                pe.wait_ge(x2_ready, g * STREAMS + s - 3)
                            else:
                                pe.wait_ge(state_read, n + 5)
                            flip(s % 4, scaled[s % 4]).then_inc(it_flip, 1)
                        if m is not None:
                            pe.wait_ge(it_turned, m + 1)
                            rows(r % 4, [(turned[r % 4], lambda t: w_ffn[:, :])], bias=1).then_inc(product, 1)

                pe.wait_ge(x1_ready, g * STREAMS + STREAMS)
                q0 = g * STEPS
                iteration(q0, peeled=True)
                with pe.Fori(q0 + STREAMS, q0 + STEPS, STREAMS) as q:
                    iteration(q)
                iteration(g * STEPS + STEPS, tail=True)
                for k in range(STREAMS + RANK_R):
                    a, b, d, f, h = in_flight(k, 0, Q_LAG, MIX_LAG, FLIP_R, RANK_R)
                    if a is not None:
                        pe.wait_ge(x2_scaled, g * STREAMS + a + 1)
                        if a < 4:
                            pe.wait_ge(x2_ready, g * STREAMS + a + 5)
                        else:
                            pe.wait_ge(x3_ready, g * STREAMS + a - 3)
                        flip(a % 4, scaled[a % 4]).then_inc(x2_flip, 1)
                    if f is not None:
                        c, n = f % 4, g * STREAMS + f
                        pe.wait_ge(rows_ready, n + 1)
                        if f < 4:
                            pe.wait_ge(x3_ready, g * STREAMS + f + 5)
                        else:
                            pe.wait_ge(slots_ready, n - 3)
                        flip(c, start_h[f]).then_inc(r_flip, 1)
                    if b is not None:
                        pe.wait_ge(x2_turned, g * STREAMS + b + 1)
                        rows(b % 4, [(turned[b % 4], lambda t: w_mix[:, 1, :])]).then_inc(q_psum, 1)
                    if d is not None:
                        pe.wait_ge(q_copied, g * STREAMS + d + 1)
                        rows(d % 4, [(turned[d % 4], lambda t: w_mix[:, 0, :]),
                                     (adjT[d], lambda t, c=d % 4: act_z[c][:, t, :])], bias=2).then_inc(mix_psum, 1)
                    if h is not None:
                        c, n = h % 4, g * STREAMS + h
                        pe.wait_ge(chosen_ready, n + 1)
                        if h:
                            pe.wait_ge(slots_ready, n)
                        ranks = ps[c][:, 4, 0:TILES * NE].rearrange("p (t e) -> p t e", e=NE)
                        nc.tensor.matmul(ranks, tri[:, :], chosen[c][:, :, :], start=True, stop=False,
                                         skip_group_check=True)
                        for t in range(TILES - 1):
                            rest = TILES - 1 - t
                            nc.tensor.matmul(ranks[:, t + 1:TILES, :], ones_bf[:, :],
                                             chosen[c][:, t, :].unsqueeze(1).to_broadcast([P, rest, NE]),
                                             start=False, stop=False, skip_group_check=True)
                        nc.tensor.matmul(ranks, ones_bf[:, :],
                                         taken_bf[:, :].unsqueeze(1).to_broadcast([P, TILES, NE]),
                                         start=False, stop=True, skip_group_check=True).then_inc(rank_psum, 1)
                    if f is not None:
                        c, n = f % 4, g * STREAMS + f
                        pe.wait_ge(r_turned, n + 1)
                        for t in range(TILES):
                            last = nc.tensor.matmul(ps[c][:, 0, t * NE:(t + 1) * NE], turned[c][:, t, :], wr[:, :],
                                                    start=True, stop=True)
                        last.then_inc(logit_psum, 1)

            pe.wait_ge(slots_ready, GROUPS * STREAMS)
            nc.tensor.matmul(ps[0][:, 0, 0:NE], ones_bf[:, :], taken_bf[:, :], start=True,
                             stop=True).then_inc(total_psum, 1)
            pe.wait_ge(tables_ready, 1)

            def turn(j, q, b):
                pe.wait_ge(slab_in[q], j * (4 * SLAB_LOADS) + 16 * SLAB_LOADS)
                for t in range(SUBS):
                    last = nc.tensor.transpose(psX[b][:, t * P:(t + 1) * P], rows_in[q][:, t, 0:D], ident[:, :])
                last.then_inc(slab_flip, 1)

            def first_product(n, q, b, peeled):
                pe.wait_ge(slab_turned, n + 1)
                for c in range(HC):
                    if not peeled:
                        pe.wait_ge(hidden_ready, (n - 1) * HC + (c + 1))
                    for m, (w, x) in enumerate(((0, 0), (0, 1), (1, 0))):
                        last = nc.tensor.matmul(psH[c], w1_parts[b][:, w, c * P:(c + 1) * P],
                                                rows_T[b][:, x, :], start=m == 0, stop=m == 2)
                    last.then_inc(hidden_psum, 1)

            def second_product(n, q, b, peeled):
                pe.wait_ge(hidden_ready, n * HC + HC)
                if not peeled:
                    pe.wait_ge(y_ready, n - 1)
                for t in range(SUBS):
                    for c in range(HC):
                        last = nc.tensor.matmul(psY[b][:, t, :], hidden[b][c][:, t * P:(t + 1) * P],
                                                w2_in[q][:, c, :], start=c == 0, stop=c == HC - 1,
                                                skip_group_check=True)
                last.then_inc(y_psum, 1)

            def expert(j, first=False, end=False):
                for q in range(4):
                    n = j + q
                    first_product(n, q, q % 2, first and q == 0)
                    if not (end and q == 3):
                        turn(j if q < 3 else j + 4, (q + 1) % 4, (q + 1) % 2)
                    if not (first and q == 0):
                        second_product(j + (q - 1), (q - 1) % 4, (q - 1) % 2, first and q < 3)

            turn(0, 0, 0)
            expert(0, first=True)
            with pe.Fori(4, SLABS - 4, 4) as j:
                expert(j)
            expert(SLABS - 4, end=True)
            second_product(SLABS - 1, 3, 1, False)


_INS = ["x", "adj", "L0_gnn_W_w", "L0_gnn_W_b", "L0_gnn_a_w", "L0_gnn_a_b", "L0_ffn_ln_w", "L0_ffn_ln_b",
        "L0_ffn_W", "L0_ffn_b", "L1_gnn_weight", "L1_gnn_bias", "L1_ffn_Wr", "L1_ffn_br", "L1_ffn_ln_g", "L1_ffn_ln_b", "L1_ffn_W1",
        "L1_ffn_b1", "L1_ffn_W2", "L1_ffn_b2"]
_OUTS = [((128, 128, 128), "float32")]


def kernel(**inputs):
    import numpy as _np
    import concourse.bacc as _bacc
    from concourse import mybir as _mybir
    from concourse.bass_utils import run_bass_kernel_spmd as _run

    nc = _bacc.Bacc("TRN2", target_bir_lowering=False, num_devices=1)
    arrays, args = {}, []
    for name in _INS:
        a = _np.ascontiguousarray(inputs[name])
        arrays[f"in_{name}_dram"] = a
        args.append(nc.dram_tensor(f"in_{name}_dram", a.shape, _mybir.dt.from_np(a.dtype), kind="ExternalInput").ap())
    for i, (shape, dtype) in enumerate(_OUTS):
        dt = _mybir.dt.from_np(_np.dtype(dtype))
        args.append(nc.dram_tensor(f"out_{i}_dram", shape, dt, kind="ExternalOutput").ap())
    network(nc, *args)
    r = _run(nc, [arrays], core_ids=[0])
    got = tuple(r.results[0][f"out_{i}_dram"] for i in range(len(_OUTS)))
    return got[0]
```
